# Optimizing a Trainium2 kernel written in Bass

```python
import numpy as np
import jax
import jax.numpy as jnp

def _softmax(x, axis=-1):
    return jax.nn.softmax(x, axis=axis)

def _gelu(x):
    return jax.nn.gelu(x, approximate=True)

def _silu(x):
    return jax.nn.silu(x)

def _sigmoid(x):
    return jax.nn.sigmoid(x)

def _layernorm(x, axis=-1, eps=1e-05):
    m = jnp.mean(x, axis=axis, keepdims=True)
    v = jnp.var(x, axis=axis, keepdims=True)
    return (x - m) / jnp.sqrt(v + eps)

def _scatter_add(tgt, idx, src, axis=0):
    return tgt.at[idx].add(src)

def _segment_sum(src, seg, n):
    return jax.ops.segment_sum(src, seg, n)
kernel_name = 'mk_flamingo_gated_d2_seqx_r8_235aa1'

def setup_inputs(seed: int=0):
    np.random.seed(seed)
    _w = jnp.asarray

    def _rec_inputs():
        import jax
        import jax.numpy as jnp
        _rk = jax.random.key(seed)
        x = -0.0002928 + 1 * jax.random.normal(jax.random.fold_in(_rk, 1), (4, 512, 128), jnp.float32)
        _lenS = 512 - jax.random.randint(jax.random.fold_in(_rk, 7), (4,), 0, max(1, 512 // 4) + 1, jnp.int32)
        _lenS2 = 154 - jax.random.randint(jax.random.fold_in(_rk, 8), (4,), 0, max(1, 154 // 4) + 1, jnp.int32)
        _ctx_1024P = jax.random.normal(jax.random.fold_in(_rk, 11), (4, 16, 128), jnp.float32)
        _ctx_1024c = jax.random.dirichlet(jax.random.fold_in(_rk, 511), 0.3 * jnp.ones((16,), jnp.float32), (4, 154))
        _ctx_1024t = jnp.einsum('bsk,bkd->bsd', _ctx_1024c, _ctx_1024P)
        _ctx_1024t = _ctx_1024t * jax.lax.rsqrt(jnp.mean(jnp.square(_ctx_1024t)) + 1e-12) * 0.953939
        ctx_1024 = 4.13588e-05 + 0.999923 * (_ctx_1024t + 0.3 * jax.random.normal(jax.random.fold_in(_rk, 611), (4, 154, 128), jnp.float32))
        _validS = jnp.arange(512)[None, :] < _lenS[:, None]
        _validS2 = jnp.arange(154)[None, :] < _lenS2[:, None]
        _causal = jnp.tril(jnp.ones((512, 512), dtype=bool))
        mask_BxSxS2_bf0 = jnp.logical_not(jnp.ones((4, 512, 154), dtype=bool))
        mask_BxS2_if0 = jnp.where(jnp.ones((4, 154), dtype=bool), 0, 1).astype(jnp.int32)
        _g = jax.random.normal(jax.random.fold_in(_rk, 9001), (2, 2), jnp.float32)
        _g = jnp.sign(_g) * jnp.maximum(jnp.abs(_g), 1.0) + (_g == 0) * 1.0
        g_xattn = _g[0]
        g_ffn = _g[1]
        return (x, ctx_1024, mask_BxSxS2_bf0, mask_BxS2_if0, g_xattn, g_ffn)
    x, ctx_1024, mask_BxSxS2_bf0, mask_BxS2_if0, g_xattn, g_ffn = _rec_inputs()

    def _L0_xattn_setup():
        import jax, jax.numpy as jnp
        import numpy as np
        HIDDEN = 128
        HEADS = 16
        D_K = HIDDEN // HEADS
        B, LQ, LKV = (4, 128, 256)
        NEG_INF = -1e+18
        key = jax.random.key(seed)
        ks = jax.random.split(key, 12)
        s = 1.0 / np.sqrt(HIDDEN)
        return {'tgt': jax.random.normal(ks[0], (B, LQ, HIDDEN), jnp.float32), 'memory': jax.random.normal(ks[1], (B, LKV, HIDDEN), jnp.float32), 'mask': jnp.zeros((B, LQ, LKV), dtype=bool), 'Wq': jax.random.normal(ks[2], (HIDDEN, HIDDEN), jnp.float32) * s, 'bq': jnp.zeros((HIDDEN,), jnp.float32), 'Wk': jax.random.normal(ks[3], (HIDDEN, HIDDEN), jnp.float32) * s, 'bk': jnp.zeros((HIDDEN,), jnp.float32), 'Wv': jax.random.normal(ks[4], (HIDDEN, HIDDEN), jnp.float32) * s, 'bv': jnp.zeros((HIDDEN,), jnp.float32), 'Wo': jax.random.normal(ks[5], (HIDDEN, HIDDEN), jnp.float32) * s, 'bo': jnp.zeros((HIDDEN,), jnp.float32)}
    _L0_xattn_all = _L0_xattn_setup()
    _L0_xattn_in = {k: v for k, v in _L0_xattn_all.items() if k in ('Wq', 'bq', 'Wk', 'bk', 'Wv', 'bv', 'Wo', 'bo')}
    del _L0_xattn_all

    def _L0_ffn_setup():
        import jax, jax.numpy as jnp
        import numpy as np
        B, T, C = (2, 64, 128)
        I = 512
        E = 8
        K = 2
        key = jax.random.key(seed)
        ks = jax.random.split(key, 8)
        s = 0.02
        return {'x': jax.random.normal(ks[0], (B, T, C), jnp.float32), 'Wr1': jax.random.normal(ks[1], (C, C // 4), jnp.float32) * s, 'br1': jnp.zeros((C // 4,), jnp.float32), 'Wr2': jax.random.normal(ks[2], (C // 4, E), jnp.float32) * s, 'br2': jnp.zeros((E,), jnp.float32), 'Ws1': jax.random.normal(ks[3], (C, I), jnp.float32) * s, 'bs1': jnp.zeros((I,), jnp.float32), 'Ws2': jax.random.normal(ks[4], (I, C), jnp.float32) * s, 'bs2': jnp.zeros((C,), jnp.float32), 'We1': jax.random.normal(ks[5], (E, C, I), jnp.float32) * s, 'be1': jnp.zeros((E, I), jnp.float32), 'We2': jax.random.normal(ks[6], (E, I, C), jnp.float32) * s, 'be2': jnp.zeros((E, C), jnp.float32)}
    _L0_ffn_all = _L0_ffn_setup()
    _L0_ffn_in = {k: v for k, v in _L0_ffn_all.items() if k in ('Wr1', 'br1', 'Wr2', 'br2', 'Ws1', 'bs1', 'Ws2', 'bs2', 'We1', 'be1', 'We2', 'be2')}
    del _L0_ffn_all

    def _L1_xattn_setup():
        import jax, jax.numpy as jnp
        import numpy as np
        import math
        B, M, D, H, NK = (4, 256, 128, 16, 5)
        HD = D // H

        def _gather_pad0(x, idx):
            Bx, Hx, W, hd = x.shape
            valid = (idx >= 0) & (idx < W)
            idxc = jnp.clip(idx, 0, W - 1).reshape(Bx, Hx, -1)
            g = jnp.take_along_axis(x, idxc[..., None], axis=2)
            g = g.reshape(idx.shape + (hd,))
            return g * valid[..., None].astype(x.dtype)
        key = jax.random.key(seed)
        ks = jax.random.split(key, 9)
        w = lambda k, shape: jax.random.normal(k, shape, jnp.float32) * 0.02
        return {'k': jax.random.normal(ks[0], (B, M, D), jnp.float32), 'v': jax.random.normal(ks[1], (B, M, D), jnp.float32), 'q': jax.random.normal(ks[2], (B, M, D), jnp.float32), 'mask': jnp.zeros((B, M), jnp.int32), 'Wk': w(ks[3], (D, D)), 'bk': jnp.zeros((D,), jnp.float32), 'Wv': w(ks[4], (D, D)), 'bv': jnp.zeros((D,), jnp.float32), 'Wq': w(ks[5], (D, D)), 'bq': jnp.zeros((D,), jnp.float32), 'Woff': w(ks[6], (H * NK, D)), 'boff': jnp.zeros((H * NK,), jnp.float32), 'Wo': w(ks[7], (D, D)), 'bo': jnp.zeros((D,), jnp.float32)}
    _L1_xattn_all = _L1_xattn_setup()
    _L1_xattn_in = {k: v for k, v in _L1_xattn_all.items() if k in ('Wk', 'bk', 'Wv', 'bv', 'Wq', 'bq', 'Woff', 'boff', 'Wo', 'bo')}
    del _L1_xattn_all

    def _L1_ffn_setup():
        import jax, jax.numpy as jnp
        import numpy as np
        NUM_OPS, B, T, D = (8, 8, 64, 128)
        key = jax.random.key(seed)
        k1, k2, k3, k4 = jax.random.split(key, 4)
        x = jax.random.normal(k1, (B, T, D), dtype=jnp.float32)
        W = jax.random.normal(k2, (NUM_OPS, D, D), dtype=jnp.float32) * 0.02
        b = jnp.zeros((NUM_OPS, D), dtype=jnp.float32)
        logits = 0.001 * jax.random.normal(k3, (NUM_OPS,), dtype=jnp.float32)
        u = jax.random.uniform(k4, (NUM_OPS,), dtype=jnp.float32, minval=1e-06, maxval=1.0 - 1e-06)
        return {'x': x, 'W': W, 'b': b, 'logits': logits, 'u': u}
    _L1_ffn_all = _L1_ffn_setup()
    _L1_ffn_in = {k: v for k, v in _L1_ffn_all.items() if k in ('W', 'b', 'logits', 'u')}
    del _L1_ffn_all
    return {'x': x, 'ctx_1024': ctx_1024, 'mask_BxSxS2_bf0': mask_BxSxS2_bf0, 'mask_BxS2_if0': mask_BxS2_if0, 'g_xattn': g_xattn, 'g_ffn': g_ffn, 'L0_xattn_Wq': _L0_xattn_in['Wq'], 'L0_xattn_bq': _L0_xattn_in['bq'], 'L0_xattn_Wk': _L0_xattn_in['Wk'], 'L0_xattn_bk': _L0_xattn_in['bk'], 'L0_xattn_Wv': _L0_xattn_in['Wv'], 'L0_xattn_bv': _L0_xattn_in['bv'], 'L0_xattn_Wo': _L0_xattn_in['Wo'], 'L0_xattn_bo': _L0_xattn_in['bo'], 'L0_ffn_Wr1': _L0_ffn_in['Wr1'], 'L0_ffn_br1': _L0_ffn_in['br1'], 'L0_ffn_Wr2': _L0_ffn_in['Wr2'], 'L0_ffn_br2': _L0_ffn_in['br2'], 'L0_ffn_Ws1': _L0_ffn_in['Ws1'], 'L0_ffn_bs1': _L0_ffn_in['bs1'], 'L0_ffn_Ws2': _L0_ffn_in['Ws2'], 'L0_ffn_bs2': _L0_ffn_in['bs2'], 'L0_ffn_We1': _L0_ffn_in['We1'], 'L0_ffn_be1': _L0_ffn_in['be1'], 'L0_ffn_We2': _L0_ffn_in['We2'], 'L0_ffn_be2': _L0_ffn_in['be2'], 'L1_xattn_Wk': _L1_xattn_in['Wk'], 'L1_xattn_bk': _L1_xattn_in['bk'], 'L1_xattn_Wv': _L1_xattn_in['Wv'], 'L1_xattn_bv': _L1_xattn_in['bv'], 'L1_xattn_Wq': _L1_xattn_in['Wq'], 'L1_xattn_bq': _L1_xattn_in['bq'], 'L1_xattn_Woff': _L1_xattn_in['Woff'], 'L1_xattn_boff': _L1_xattn_in['boff'], 'L1_xattn_Wo': _L1_xattn_in['Wo'], 'L1_xattn_bo': _L1_xattn_in['bo'], 'L1_ffn_W': _L1_ffn_in['W'], 'L1_ffn_b': _L1_ffn_in['b'], 'L1_ffn_logits': _L1_ffn_in['logits'], 'L1_ffn_u': _L1_ffn_in['u']}

def reference(x, ctx_1024, mask_BxSxS2_bf0, mask_BxS2_if0, g_xattn, g_ffn, L0_xattn_Wq, L0_xattn_bq, L0_xattn_Wk, L0_xattn_bk, L0_xattn_Wv, L0_xattn_bv, L0_xattn_Wo, L0_xattn_bo, L0_ffn_Wr1, L0_ffn_br1, L0_ffn_Wr2, L0_ffn_br2, L0_ffn_Ws1, L0_ffn_bs1, L0_ffn_Ws2, L0_ffn_bs2, L0_ffn_We1, L0_ffn_be1, L0_ffn_We2, L0_ffn_be2, L1_xattn_Wk, L1_xattn_bk, L1_xattn_Wv, L1_xattn_bv, L1_xattn_Wq, L1_xattn_bq, L1_xattn_Woff, L1_xattn_boff, L1_xattn_Wo, L1_xattn_bo, L1_ffn_W, L1_ffn_b, L1_ffn_logits, L1_ffn_u):
    import jax
    import jax.numpy as jnp

    def _L0_xattn_ref(tgt, memory, mask, Wq, bq, Wk, bk, Wv, bv, Wo, bo):
        import jax, jax.numpy as jnp
        import numpy as np
        HIDDEN = 128
        HEADS = 16
        D_K = HIDDEN // HEADS
        B, LQ, LKV = (4, 128, 256)
        NEG_INF = -1e+18
        b = tgt.shape[0]

        def heads(x):
            return x.reshape(b, -1, HEADS, D_K).transpose(0, 2, 1, 3)
        q = heads(tgt @ Wq + bq) / jnp.sqrt(jnp.asarray(D_K, tgt.dtype))
        k = heads(memory @ Wk + bk)
        v = heads(memory @ Wv + bv)
        scores = jnp.einsum('bhqd,bhkd->bhqk', q, k)
        scores = jnp.where(mask[:, None, :, :], NEG_INF, scores)
        attn = jax.nn.softmax(scores, axis=-1)
        ctx = jnp.einsum('bhqk,bhkd->bhqd', attn, v)
        ctx = ctx.transpose(0, 2, 1, 3).reshape(b, -1, HIDDEN)
        return ctx @ Wo + bo

    def _L0_ffn_ref(x, Wr1, br1, Wr2, br2, Ws1, bs1, Ws2, bs2, We1, be1, We2, be2):
        import jax, jax.numpy as jnp
        import numpy as np
        B, T, C = (2, 64, 128)
        I = 512
        E = 8
        K = 2
        Bb, Tt, Cc = x.shape
        xf = x.reshape(-1, Cc)
        logits = jax.nn.relu(xf @ Wr1 + br1) @ Wr2 + br2
        gates = jax.nn.softmax(logits, axis=-1)
        tg, ti = jax.lax.top_k(gates, K)
        tg = jax.nn.softmax(tg / K, axis=-1)
        out = jax.nn.silu(xf @ Ws1 + bs1) @ Ws2 + bs2
        for e in range(E):
            h = jax.nn.silu(xf @ We1[e] + be1[e]) @ We2[e] + be2[e]
            w = jnp.sum(tg * (ti == e), axis=-1)
            out = out + w[:, None] * h
        return out.reshape(Bb, Tt, Cc)

    def _L1_xattn_ref(k, v, q, mask, Wk, bk, Wv, bv, Wq, bq, Woff, boff, Wo, bo):
        import jax, jax.numpy as jnp
        import numpy as np
        import math
        B, M, D, H, NK = (4, 256, 128, 16, 5)
        HD = D // H

        def _gather_pad0(x, idx):
            Bx, Hx, W, hd = x.shape
            valid = (idx >= 0) & (idx < W)
            idxc = jnp.clip(idx, 0, W - 1).reshape(Bx, Hx, -1)
            g = jnp.take_along_axis(x, idxc[..., None], axis=2)
            g = g.reshape(idx.shape + (hd,))
            return g * valid[..., None].astype(x.dtype)
        Bq, Q, _ = q.shape
        key_len = k.shape[1]
        K = jnp.einsum('bmd,ed->bme', k, Wk) + bk
        V = jnp.einsum('bmd,ed->bme', v, Wv) + bv
        Qp = jnp.einsum('bqd,ed->bqe', q, Wq) + bq
        off = jnp.einsum('bqd,ed->bqe', Qp, Woff) + boff
        off = off.reshape(Bq, Q, H, NK).transpose(0, 2, 1, 3)
        Kh = K.reshape(Bq, key_len, H, HD).transpose(0, 2, 1, 3)
        Vh = V.reshape(Bq, key_len, H, HD).transpose(0, 2, 1, 3)
        Qh = Qp.reshape(Bq, Q, H, HD).transpose(0, 2, 1, 3)
        loc = jnp.arange(Q, dtype=jnp.float32)[:, None]
        left = -NK // 2
        ref = jnp.arange(left, NK + left, dtype=jnp.float32)
        sign_lens = (1 - mask).sum(-1).astype(jnp.float32) - 1.0
        loc_x = jnp.mod(ref + off + loc, sign_lens[:, None, None, None])
        xg = loc_x / (key_len - 1) * 2.0 - 1.0
        ix = ((xg + 1.0) * key_len - 1.0) / 2.0
        x0 = jnp.floor(ix)
        dx = ix - x0
        i0 = x0.astype(jnp.int32)
        i1 = i0 + 1
        w0 = (1.0 - dx)[..., None]
        w1 = dx[..., None]
        sk = 0.5 * (w0 * _gather_pad0(Kh, i0) + w1 * _gather_pad0(Kh, i1))
        sv = 0.5 * (w0 * _gather_pad0(Vh, i0) + w1 * _gather_pad0(Vh, i1))
        scores = jnp.einsum('bhqd,bhqkd->bhqk', Qh / math.sqrt(HD), sk)
        attn = jax.nn.softmax(scores, axis=-1)
        ctx = jnp.einsum('bhqk,bhqkd->bhqd', attn, sv)
        ctx = ctx.transpose(0, 2, 1, 3).reshape(Bq, Q, H * HD)
        return jnp.einsum('bqd,ed->bqe', ctx, Wo) + bo

    def _L1_ffn_ref(x, W, b, logits, u):
        import jax, jax.numpy as jnp
        import numpy as np
        NUM_OPS, B, T, D = (8, 8, 64, 128)
        gumbel = -jnp.log(-jnp.log(u))
        idx = jnp.argmax(jax.nn.log_softmax(logits) + gumbel)
        out = jnp.einsum('btd,de->bte', x, W[idx]) + b[idx]
        return out
    x = x + jnp.tanh(g_xattn[0]) * _L0_xattn_ref(_layernorm(x, axis=-1), ctx_1024, mask_BxSxS2_bf0, L0_xattn_Wq, L0_xattn_bq, L0_xattn_Wk, L0_xattn_bk, L0_xattn_Wv, L0_xattn_bv, L0_xattn_Wo, L0_xattn_bo)
    x = x + jnp.tanh(g_ffn[0]) * _L0_ffn_ref(_layernorm(x, axis=-1), L0_ffn_Wr1, L0_ffn_br1, L0_ffn_Wr2, L0_ffn_br2, L0_ffn_Ws1, L0_ffn_bs1, L0_ffn_Ws2, L0_ffn_bs2, L0_ffn_We1, L0_ffn_be1, L0_ffn_We2, L0_ffn_be2)
    x = x + jnp.tanh(g_xattn[1]) * _L1_xattn_ref(ctx_1024, ctx_1024, _layernorm(x, axis=-1), mask_BxS2_if0, L1_xattn_Wk, L1_xattn_bk, L1_xattn_Wv, L1_xattn_bv, L1_xattn_Wq, L1_xattn_bq, L1_xattn_Woff, L1_xattn_boff, L1_xattn_Wo, L1_xattn_bo)
    x = x + jnp.tanh(g_ffn[1]) * _L1_ffn_ref(_layernorm(x, axis=-1), L1_ffn_W, L1_ffn_b, L1_ffn_logits, L1_ffn_u)
    return x

_drawn_inputs = setup_inputs


def setup_inputs(seed=0):
    import zlib

    import numpy as np

    out = dict(_drawn_inputs(seed))
    spreads = {'g_ffn': (-1.0, 0.6),
     'L0_xattn_bq': (0.0, 0.402),
     'L0_xattn_bk': (0.0, 0.8),
     'L0_xattn_bv': (0.0, 0.1),
     'L0_xattn_bo': (0.0, 0.1),
     'L0_ffn_br1': (0.0, 0.573),
     'L0_ffn_br2': (0.0, 0.1),
     'L0_ffn_bs1': (0.0, 0.488),
     'L0_ffn_bs2': (0.0, 0.1),
     'L0_ffn_be1': (0.0, 0.716),
     'L0_ffn_be2': (0.0, 0.1),
     'L1_xattn_bk': (0.0, 0.8),
     'L1_xattn_bv': (0.0, 0.8),
     'L1_xattn_bq': (0.0, 0.8),
     'L1_xattn_boff': (0.0, 0.8),
     'L1_xattn_bo': (0.0, 0.1),
     'L1_ffn_b': (0.0, 0.1)}
    factors = {'L0_ffn_Wr1': 2.708,
     'L1_xattn_Wk': 8.0,
     'L1_xattn_Wv': 4.114,
     'L1_xattn_Wq': 8.0,
     'L1_xattn_Woff': 8.0,
     'L1_xattn_Wo': 3.264}
    for name, (base, spread) in spreads.items():
        noise = np.random.default_rng([zlib.crc32(name.encode()), seed]).standard_normal(out[name].shape)
        drawn = base * np.exp(spread * noise) if base else spread * noise
        out[name] = jnp.asarray(drawn.astype(out[name].dtype))
    for name, factor in factors.items():
        out[name] = (out[name] * factor).astype(out[name].dtype)
    return out
```

```python
import concourse.bass as bass
from concourse import mybir
from contextlib import ExitStack
import math

F32 = mybir.dt.float32
BF16 = mybir.dt.bfloat16
ALU = mybir.AluOpType
ACT = mybir.ActivationFunctionType
AX = mybir.AxisListType

B, S, D = 4, 512, 128
S2 = 154
H, DK = 16, 8
NT = S // 128
KH = S2 // 2
NE, NC = 9, 4
NK = 5
HN = H * NK
NS = 3
SLOT_Q = (0, 0, 0, 1, 1, 2)
SLOT_K = (0, 1, 2, 0, 1, 0)
QR = len(SLOT_Q) * DK
QM = QR + NS
HG = (3, 3, 3, 3, 2, 2)
R0 = 128
RR = NS * 32
MASKED = -1e18
MAGIC = 12582912.0
EPS = 1e-5
HS = 6
C_ID, C_K0, C_KR, C_LOC, C_REF, C_RANK, C_N = 0, 128, 129, 130, 134, 214, 222


def build(nc, x, ctxT, mask, maskT, kmask, gates, consts, wq, wk, wv, wo, bq_col, bk_col, rows,
          wr1, br1_col, wr2, br2, w1, b1_cols, w2, b2, wkT, wvT, wqT, woffT, woT, bq1_col, boff,
          w8, b8_src, logits, u, out):
    ctx = ExitStack()
    dq = nc.dram_tensor("scratch_q_parts", [B, NS, 128, S], BF16, kind="Internal").ap()
    dk = nc.dram_tensor("scratch_k_parts", [NS, 128, B * S2], BF16, kind="Internal").ap()
    dm = nc.dram_tensor("scratch_max_parts", [B, NT, H, NS, 128], BF16, kind="Internal").ap()
    dj = nc.dram_tensor("scratch_positions", [B, HN, S], BF16, kind="Internal").ap()

    with ctx:
        def sb(name, shape, dt=F32):
            return ctx.enter_context(nc.sbuf_tensor(name, shape, dt))

        def pb(name, shape):
            return ctx.enter_context(nc.psum_tensor(name, shape, F32))

        def sem(name):
            return ctx.enter_context(nc.semaphore(name))

        X = sb("X", [128, B, NT, D])
        cst = sb("cst", [128, C_N])
        ident = cst[:, C_ID:C_ID + 128]
        identb = sb("identb", [128, 128], BF16)
        ones = sb("ones", [1, 128])
        Wq, Wk, Wv, Wo = (sb(n, [128, 128]) for n in ("Wq", "Wk", "Wv", "Wo"))
        WkT, WvT, WqT, WoT = (sb(n, [128, 128]) for n in ("WkT", "WvT", "WqT", "WoT"))
        WoffT = sb("WoffT", [128, HN])
        brow = sb("brow", [1, 6, 128])
        bcol = sb("bcol", [128, 3])
        boffr = sb("boffr", [1, HN])
        Wr1 = sb("Wr1", [128, 32])
        br1 = sb("br1", [32, 1])
        Wr2 = sb("Wr2", [33, 8])
        W1 = sb("W1", [128, NE, NC * 128])
        b1 = sb("b1", [128, NE, NC])
        W2 = sb("W2", [128, NE, NC, D])
        B2 = sb("B2", [NE, D])
        Wsel = sb("Wsel", [128, 128])
        bsel = sb("bsel", [1, 128])
        tg = sb("tg", [128, 4])
        lens = sb("lens", [128, 4, B])
        sgn = sb("sgn", [128, B])
        KA = sb("KA", [QM, H, S2], BF16)
        V0 = sb("V0", [KH, B, 2, H, DK + 1])
        T0 = sb("T0", [R0, B, NS, H, 32], BF16)
        TR = sb("TR", [RR, B, H, 32], BF16)
        mraw = sb("mraw", [128, NT, S2], mybir.dt.uint8)
        mrawT = sb("mrawT", [KH, 2, S], mybir.dt.uint8)
        mb = sb("mb", [128, NT, S2], BF16)
        mbT = sb("mbT", [KH, 2, S], BF16)
        QA = sb("QA", [QM, H, S], BF16)
        qf = sb("qf", [128, S])
        qs = sb("qs", [128, NS, S], BF16)
        nmax = sb("nmax", [128, NT, H])
        nmr = sb("nmr", [NT * H, 128])
        nms = sb("nms", [NT * H, NS, 128], BF16)
        PT = sb("PT", [KH, 2, 2, 256])
        rden = sb("rden", [128, 2, H])
        cx = sb("cx", [128, NT, D])
        cxT = sb("cxT", [128, S])
        xn = sb("xn", [128, NT, D])
        st = sb("st", [128, NT, 6])
        mv = sb("mv", [128, NT, 2])
        ve = sb("ve", [128, NT])
        rstd = sb("rstd", [128, NT])
        mhalf = sb("mhalf", [128, NT])
        xnT = sb("xnT", [128, S])
        xnTf = sb("xnTf", [128, S])
        r1 = sb("r1", [33, S])
        gt = sb("gt", [128, 12, NT, 8])
        gs = sb("gs", [128, 10, NT])
        W9 = sb("W9", [128, NT, NE])
        w9T = sb("w9T", [NE, S])
        hT = sb("hT", [128, HS, S])
        acc = sb("acc", [128, NT, D])
        QpT = sb("QpT", [128, S])
        Qp = sb("Qp", [128, NT, D])
        pos = sb("pos", [128, 5, NT, HN])
        wts = sb("wts", [128, NT, HN, 2])
        jT = sb("jT", [HN, S], BF16)
        JB = sb("JB", [128, 2, NK, S], BF16)
        OH = sb("OH", [R0, 2, NK, S], BF16)
        OHR = sb("OHR", [RR, 2, NK, S], BF16)
        prod = sb("prod", [128, 2, NT, 10, DK])
        GS = sb("GS", [128, 2 + H, NT, NK * 16])
        GV = GS[:, 2:2 + H]
        dots = sb("dots", [128, NT, H, 10])
        aw = sb("aw", [128, NT, HN, 2])
        sc = sb("sc", [128, NT, HN])
        sm = sb("sm", [128, 3, NT * H])
        GVf = GV.rearrange("p h t c -> p (h t c)")
        W8 = GVf[:, 0:1024].rearrange("p (o e) -> p o e", o=8)
        ctxP = GVf[:, 1024:1024 + B * 162].rearrange("p (b k) -> p b k", b=B)
        ctxR = GVf[:, 1672:1672 + B * 192].rearrange("p (b w s k) -> p b w s k", b=B, w=2, s=3)
        ksf = GVf[:, 2440:2440 + B * S2]
        tabf = GVf[:, 3056:3568]
        ks = hT[:, 0:2, :].rearrange("p a s -> p (a s)").bitcast(BF16)[:, 0:NS * B * S2] \
            .rearrange("p (s k) -> p s k", s=NS)
        tabb = GVf[:, 3568:3824].bitcast(BF16)
        b8 = GVf[0:1, 3824:4848].rearrange("p (o e) -> p o e", o=8)
        km = aw[:, :, :, :].rearrange("p t n w -> p (t n w)").bitcast(mybir.dt.int32)[:, 0:B * S2]
        kmf = dots[:, :, :, :].rearrange("p t h w -> p (t h w)")[:, 0:B * S2].rearrange("p (b k) -> p b k", b=B)
        vrow = sb("vrow", [1, 162])
        vrowR = sb("vrowR", [1, 2, NS, 32])
        lg = sb("lg", [128, 8, 8])
        lg1 = sb("lg1", [128, 4])
        gin = sb("gin", [128, 4])

        UP = pb("UP", [128, 2, 512])
        DOWN = pb("DOWN", [128, 512])
        MISC = pb("MISC", [128, 512])
        RING = pb("RING", [128, 2, 512])
        GC = pb("GC", [128, 2, 512])

        schedule = order()
        uses = {"A0": 2, "A2": 1, "A5": 2, "F0": 4, "G0": 5, "G3": 4}
        misc_at, n = {}, 0
        for piece in schedule:
            misc_at[piece] = n
            n += uses.get(piece[0], 0)
        norm_at = {p: n for n, p in enumerate([(p[0], p[1], k) for p in schedule
                                               for k in range({"A0": 1, "F0": 1, "G0": 1, "G3": 1}.get(p[0], 0))])}

        def before(piece, kind):
            return sum(p[0] == kind for p in schedule[:schedule.index(piece)])

        ld_const = sem("ld_const")
        ld_attn = sem("ld_attn")
        ld_x = sem("ld_x")
        ld_moe = sem("ld_moe")
        ld_l1 = sem("ld_l1")
        ld_mask = sem("ld_mask")
        mask_ready = sem("mask_ready")
        dve_done = sem("dve_done")
        act_done = sem("act_done")
        pool_done = sem("pool_done")
        pre_dve = sem("pre_dve")
        pre_pe = sem("pre_pe")
        pre_act = sem("pre_act")
        pre_pool = sem("pre_pool")
        kparts_out = sem("kparts_out")
        kparts_in = sem("kparts_in")
        misc_ready = sem("misc_ready")
        misc_free = sem("misc_free")
        var_ready = sem("var_ready")
        rstd_ready = sem("rstd_ready")
        xn_ready = sem("xn_ready")
        xnT_ready = sem("xnT_ready")
        qs_ready = sem("qs_ready")
        qs_out = sem("qs_out")
        qa_in = sem("qa_in")
        sa_ready = sem("sa_ready")
        sa_free = sem("sa_free")
        nms_ready = sem("nms_ready")
        nms_out = sem("nms_out")
        qm_in = sem("qm_in")
        st_ready = sem("st_ready")
        p_ready = sem("p_ready")
        pv_done = sem("pv_done")
        ctx_ready = sem("ctx_ready")
        cxT_ready = sem("cxT_ready")
        r1_ready = sem("r1_ready")
        d_ready = sem("d_ready")
        ex_out = sem("ex_out")
        w9_ready = sem("w9_ready")
        w9T_ready = sem("w9T_ready")
        up_ready = sem("up_ready")
        h_ready = sem("h_ready")
        down_ready = sem("down_ready")
        down_free = sem("down_free")
        qpT_ready = sem("qpT_ready")
        qp_ready = sem("qp_ready")
        pos_ready = sem("pos_ready")
        jT_ready = sem("jT_ready")
        j_out = sem("j_out")
        jb_in = [sem(f"jb_in{i}") for i in range(2)]
        oh_ready = sem("oh_ready")
        g_ready = sem("g_ready")
        g_free = sem("g_free")
        gk_used = sem("gk_used")
        z_ready = sem("z_ready")
        e_ready = sem("e_ready")
        cx1_ready = sem("cx1_ready")
        x3_ready = sem("x3_ready")
        x_done = sem("x_done")
        stored = sem("stored")

        def down_count(k):
            return k // (NC * NE) * (NE + 1) + k // NC % NE + 2

        block = ctx.enter_context(nc.Block())

        @block.sync
        def _(sp):
            for dst, src in ((cst[:], consts), (gin[:], gates.partition_broadcast(128)),
                             (lg[:, 0, :], logits.partition_broadcast(128)),
                             (lg[:, 1, :], u.partition_broadcast(128)),
                             (km, kmask.rearrange("b k -> (b k)").partition_broadcast(128))):
                sp.dma_start(dst, src).then_inc(ld_const, 16)
            sp.wait_ge(pre_pool, 1)
            for dst, src in ((ctxP[:, :, 1:1 + S2], ctxT), (Wk[:], wk), (Wv[:], wv), (bcol[:, 1:2], bk_col),
                             (brow[:], rows), (WkT[:], wkT), (WvT[:], wvT),
                             (W8, w8.rearrange("o d e -> d o e")), (b8, b8_src)):
                sp.dma_start(dst, src).then_inc(ld_attn, 16)
            for b in range(B):
                sp.dma_start(X[:, b], x[b].rearrange("(t p) d -> p t d", p=128)).then_inc(ld_x, 16)
            for dst, src in ((Wq[:], wq), (bcol[:, 0:1], bq_col), (Wo[:], wo)):
                sp.dma_start(dst, src).then_inc(ld_x, 16)
            sp.wait_ge(pre_dve, 3)
            sp.dma_start(dk.rearrange("s e k -> e s k"), ks).then_inc(kparts_out, 16)
            sp.wait_ge(kparts_out, 16)
            sp.wait_ge(pre_pool, 2)
            for dst, src in ((Wr1[:], wr1), (br1[:], br1_col), (Wr2[0:32, :], wr2), (Wr2[32:33, :], br2),
                             (b1[:], b1_cols), (B2[:], b2)):
                sp.dma_start(dst, src).then_inc(ld_moe, 16)
            for e in range(NE):
                sp.dma_start(W1[:, e], w1[e]).then_inc(ld_moe, 16)
                sp.dma_start(W2[:, e], w2[e].rearrange("(c i) d -> i c d", i=128)).then_inc(ld_moe, 16)
            for dst, src in ((WqT[:], wqT), (WoT[:], woT), (WoffT[:], woffT), (bcol[:, 2:3], bq1_col),
                             (boffr[:], boff)):
                sp.dma_start(dst, src).then_inc(ld_l1, 16)
            for piece in schedule:
                kind, b = piece[0], piece[1]
                if kind == "A0":
                    if b >= 1:
                        sp.wait_ge(mask_ready, b)
                    sp.dma_start(mraw[:], mask[b].rearrange("(t p) k -> p t k", p=128)).then_inc(ld_mask, 16)
                    sp.dma_start(mrawT[:], maskT[b].rearrange("(c k) q -> k c q", c=2)).then_inc(ld_mask, 16)
                    sp.wait_ge(qs_ready, b + 1)
                    sp.dma_start(dq[b].rearrange("s e q -> e s q"), qs[:]).then_inc(qs_out, 16)
                    sp.wait_ge(qs_out, 16 * (b + 1))
                    if b >= 1:
                        sp.wait_ge(st_ready, b * 2 * H)
                    for i, s in enumerate(SLOT_K):
                        sp.dma_start(KA[i * DK:(i + 1) * DK], dk[s].rearrange("(h d) k -> d h k", d=DK)
                                     [:, :, b * S2:(b + 1) * S2]).then_inc(kparts_in, 16)
                    for i, s in enumerate(SLOT_Q):
                        sp.dma_start(QA[i * DK:(i + 1) * DK], dq[b, s].rearrange("(h d) q -> d h q", d=DK)).then_inc(qa_in, 16)
                elif kind == "A2":
                    sp.wait_ge(nms_ready, b + 1)
                    sp.dma_start(dm[b].rearrange("t h s q -> (t h) s q"), nms[:]).then_inc(nms_out, 16)
                    sp.wait_ge(nms_out, 16 * (b + 1))
                    for t in range(NT):
                        sp.dma_start(QA[QR:QM, :, t * 128:(t + 1) * 128], dm[b, t].rearrange("h s q -> s h q")).then_inc(qm_in, 16)
                elif kind == "G0":
                    sp.wait_ge(jT_ready, b + 1)
                    sp.dma_start(dj[b], jT[:]).then_inc(j_out, 16)
                    sp.wait_ge(j_out, 16 * (b + 1))
                    for h in range(2):
                        if b >= 1:
                            sp.wait_ge(oh_ready, b * H + h - 1)
                        sp.dma_start(JB[:, h % 2], dj[b, h * NK:(h + 1) * NK].partition_broadcast(128)).then_inc(jb_in[h % 2], 16)
                elif kind == "G1" and piece[2] + 2 < H:
                    h = piece[2] + 2
                    sp.wait_ge(oh_ready, b * H + h - 1)
                    sp.dma_start(JB[:, h % 2], dj[b, h * NK:(h + 1) * NK].partition_broadcast(128)).then_inc(jb_in[h % 2], 16)
                elif kind == "G3":
                    sp.wait_ge(x_done, b + 1)
                    sp.dma_start(out[b].rearrange("(t p) d -> p t d", p=128), X[:, b]).then_inc(stored, 16)
            sp.wait_ge(stored, 16 * B)

        @block.gpsimd
        def _(pool):
            done = [0]

            def step(ins):
                done[0] += 1
                ins.then_inc(pool_done, 1)
                pool.wait_ge(pool_done, done[0])

            pool.memset(GVf[:, 1024:1672], 0.0).then_inc(pre_pool, 1)
            step(pool.memset(vrow[:], 0.0))
            step(pool.memset(vrow[:, 1:1 + S2], 1.0))
            for t, v in ((ones, 1.0), (mhalf, -0.5), (V0, 1.0), (W9, 1.0), (KA, 1.0)):
                step(pool.memset(t[:], v))
            step(pool.memset(r1[32:33, :], 1.0))
            for w in range(2):
                last = pool.tensor_copy(vrowR[:, w], vrow[:, R0 + w:R0 + w + 32].unsqueeze(1).broadcast_to((1, NS, 32)))
            last.then_inc(pre_pool, 1)
            for n in range(4 * B):
                pool.wait_ge(var_ready, n + 1)
                pool.tensor_tensor(rstd[:], ve[:], mhalf[:], ALU.pow).then_inc(rstd_ready, 1)

        @block.scalar
        def _(act):
            act.wait_ge(ld_const, 16 * 5)
            act.activation(tg[:], gin[:], ACT.Tanh).then_inc(pre_act, 1)
            act.wait_ge(pre_dve, 1)
            act.activation(lg[:, 3, :], lg[:, 2, :], ACT.Exp, accum_out=lg1[:, 1:2]).then_inc(act_done, 1)
            act.wait_ge(act_done, 1)
            act.activation(lg1[:, 2:3], lg1[:, 1:2], ACT.Ln)
            act.activation(lg[:, 4, :], lg[:, 1, :], ACT.Ln).then_inc(act_done, 1)
            act.wait_ge(act_done, 2)
            act.activation(lg[:, 5, :], lg[:, 4, :], ACT.Ln, scale=-1.0).then_inc(pre_act, 1)

            def evacuate(use, dst, src, ready, bias=0.0):
                act.wait_ge(misc_ready, use + 1)
                act.activation(dst, src, ACT.Identity, bias=bias).then_inc(misc_free, 1)

            for piece in schedule:
                kind, b = piece[0], piece[1]
                m = misc_at[piece]
                if kind == "A0":
                    evacuate(m, xnT[:], MISC[:], None)
                elif kind == "A3":
                    hb, h = piece[2:]
                    i = (b * 2 + hb) * H + h
                    act.wait_ge(st_ready, i + 1)
                    if i >= 2:
                        act.wait_ge(pv_done, i - 1)
                    act.activation(PT[:, i % 2], RING[0:KH, i % 2, :].rearrange("k (c q) -> k c q", c=2),
                                   ACT.Exp).then_inc(p_ready, 1)
                elif kind == "A5":
                    evacuate(m, cxT[:], MISC[:], None)
                elif kind == "F0":
                    evacuate(m, xnTf[:], MISC[:], None)
                    act.wait_ge(misc_free, m + 3)
                    act.activation(gt[:, 1], gt[:, 0], ACT.Exp).then_inc(ex_out, 1)
                    act.wait_ge(d_ready, b + 1)
                    act.activation(gs[:, 6], gs[:, 5], ACT.Exp, scale=0.5).then_inc(ex_out, 1)
                    evacuate(m + 3, w9T[:], MISC[0:NE, :], None)
                elif kind == "F1":
                    e = piece[2]
                    if b == 0 and e == 0:
                        act.wait_ge(kparts_out, 16)
                        act.wait_ge(ld_moe, 16 * (6 + 2 * NE))
                    for c in range(NC):
                        i = (b * NE + e) * NC + c
                        act.wait_ge(up_ready, i + 1)
                        if i >= HS:
                            act.wait_ge(down_ready, down_count(i - HS))
                        act.activation(hT[:, i % HS, :], UP[:, i % 2, :], ACT.Silu,
                                       bias=b1[:, e, c:c + 1]).then_inc(h_ready, 1)
                elif kind == "G0":
                    evacuate(m, xnT[:], MISC[:], None)
                    act.wait_ge(ld_l1, 16 * 5)
                    evacuate(m + 1, QpT[:], MISC[:], None, bias=bcol[:, 2:3])
                    if b >= 1:
                        act.wait_ge(gk_used, b * H)
                    evacuate(m + 2, Qp[:].rearrange("p t e -> p (t e)"), MISC[:], None)
                    if b >= 1:
                        act.wait_ge(j_out, 16 * b)
                    act.wait_ge(misc_ready, m + 5)
                    act.activation(jT[:], MISC[0:HN, :], ACT.Identity).then_inc(jT_ready, 1)
                    act.wait_ge(jT_ready, b + 1)
                    act.nop().then_inc(misc_free, 1)
                elif kind == "G1":
                    h = piece[2]
                    if h == 0 and b >= 1:
                        act.wait_ge(cx1_ready, b)
                    if b * H + h >= 2:
                        act.wait_ge(gk_used, b * H + h - 1)
                    for tp in range(2):
                        i = (b * H + h) * 2 + tp
                        act.wait_ge(g_ready, i + 1)
                        both = GS[:, h % 2:h + 3:h + 2 - h % 2, 2 * tp:2 * tp + 2, :]
                        act.activation(both.rearrange("p k t c -> p t k c"),
                                       GC[:, i % 2, 0:320].rearrange("p (t k c) -> p t k c", t=2, k=2),
                                       ACT.Identity).then_inc(g_free, 1)
                elif kind == "G2":
                    act.wait_ge(z_ready, b + 1)
                    act.activation(sc[:], sc[:], ACT.Exp, scale=1.0 / math.sqrt(DK)).then_inc(e_ready, 1)
                elif kind == "G3":
                    evacuate(m, cxT[:], MISC[:], None)
                    evacuate(m + 2, xnT[:], MISC[:], None)

        @block.tensor
        def _(pe):
            def take_misc(use):
                if use >= 1:
                    pe.wait_ge(misc_free, use)

            def transposes(use, src, width=128):
                take_misc(use)
                for t in range(NT):
                    last = pe.transpose(MISC[0:width, t * 128:(t + 1) * 128], src[:, t, :], ident)
                last.then_inc(misc_ready, 1)

            def rows_out(use, srcT, w, bias, width=128):
                take_misc(use)
                pe.matmul(MISC[:, 0:NT * width].rearrange("p (t e) -> p t e", t=NT), ones[:],
                          bias.unsqueeze(1).broadcast_to((1, NT, width)), start=True, stop=False)
                for t in range(NT):
                    last = pe.matmul(MISC[:, t * width:(t + 1) * width], srcT[:, t * 128:(t + 1) * 128], w,
                                     start=False, stop=(t == NT - 1))
                last.then_inc(misc_ready, 1)

            pe.wait_ge(ld_attn, 16 * 9)
            for i in range(2):
                last = pe.matmul(RING[:, i, 0:2 * S2].rearrange("p (b k) -> p b k", b=2), Wk[:],
                                 ctxP[:, 2 * i:2 * i + 2, 1:1 + S2], start=True, stop=True)
            last.then_inc(pre_pe, 1)
            pe.wait_ge(pre_pool, 2)
            for b in range(B):
                for c in range(2):
                    o = UP[0:KH, b // 2, (b % 2 * 2 + c) * 128:(b % 2 * 2 + c + 1) * 128]
                    pe.matmul(o, ones[:, 0:KH], brow[:, 0, :], start=True, stop=False)
                    last = pe.matmul(o, ctxP[:, b, 1 + c * KH:1 + (c + 1) * KH], Wv[:], start=False, stop=True)
            last.then_inc(pre_pe, 1)
            pe.wait_ge(pre_dve, 2)
            for b in range(B):
                for ch in range(2):
                    i = 2 * b + ch
                    if i >= 2:
                        pe.wait_ge(pre_dve, 4 + i - 2)
                    for kv, w in enumerate((WkT, WvT)):
                        for two in range(2):
                            if ch == 0:
                                o = GC[:, ch, (kv * 2 + two) * 128:(kv * 2 + two + 1) * 128]
                                valid, rws = vrow[:, two:two + R0], ctxP[:, b, two:two + R0]
                            else:
                                o = GC[0:RR, ch, (kv * 2 + two) * 128:(kv * 2 + two + 1) * 128]
                                valid = vrowR[:, two].rearrange("p s k -> p (s k)")
                                rws = ctxR[:, b, two].rearrange("p s k -> p (s k)")
                            pe.matmul(o, valid, brow[:, 2 + kv, :], start=True, stop=False)
                            last = pe.matmul(o, rws, w[:], start=False, stop=True)
                    last.then_inc(pre_pe, 1)

            def pv(i, b, h):
                pe.wait_ge(p_ready, i + 1)
                for t in range(2):
                    for c in range(2):
                        last = pe.matmul(GC[:, 0, (t * H + h) * 9:(t * H + h) * 9 + 9],
                                         PT[:, i % 2, c, t * 128:(t + 1) * 128], V0[:, b, c, h, :],
                                         start=(c == 0), stop=(c == 1))
                last.then_inc(pv_done, 1)

            def down(b, e):
                n = (b * NE + e) * NC
                pe.wait_ge(h_ready, n + NC)
                pe.wait_ge(down_free, b * (NE + 1) + e + 1)
                for t in range(NT):
                    for c in range(NC):
                        last = pe.matmul(DOWN[:, t * 128:(t + 1) * 128], hT[:, (n + c) % HS, t * 128:(t + 1) * 128],
                                         W2[:, e, c, :], start=(c == 0), stop=(c == NC - 1))
                last.then_inc(down_ready, 1)

            for piece in schedule:
                kind, b = piece[0], piece[1]
                m = misc_at[piece]
                if kind == "A0":
                    pe.wait_ge(ld_x, 16 * 7)
                    pe.wait_ge(xn_ready, norm_at["A0", b, 0] + 1)
                    transposes(m, xn)
                    take_misc(m + 1)
                    pe.matmul(MISC[:], Wq[:], xnT[:], start=True, stop=True).then_inc(misc_ready, 1)
                elif kind == "A1":
                    t = piece[2]
                    if t == 0:
                        pe.wait_ge(qa_in, 16 * len(SLOT_Q) * (b + 1))
                        pe.wait_ge(mask_ready, b + 1)
                        pe.wait_ge(kparts_in, 16 * len(SLOT_K) * (b + 1))
                        if b == 0:
                            pe.wait_ge(pre_dve, 3)
                        else:
                            pe.wait_ge(p_ready, b * 2 * H)
                    h = 0
                    for g, n in enumerate(HG):
                        i = (b * NT + t) * len(HG) + g
                        if i >= 2:
                            pe.wait_ge(sa_free, i - 1)
                        o = RING[:, i % 2, 0:n * S2].rearrange("p (h k) -> p h k", h=n)
                        pe.matmul(o, identb[:], mb[:, t, :].unsqueeze(1).broadcast_to((128, n, S2)),
                                  start=True, stop=False)
                        for k in range(n):
                            last = pe.matmul(o[:, k, :], QA[0:QR, h, t * 128:(t + 1) * 128],
                                             KA[0:QR, h, :], start=False, stop=(k == n - 1))
                            h += 1
                        last.then_inc(sa_ready, 1)
                elif kind == "A2":
                    pe.wait_ge(sa_free, (b + 1) * NT * len(HG))
                    take_misc(m)
                    pe.transpose(MISC[0:NT * H, 0:128], nmax[:].rearrange("p t h -> p (t h)"), ident).then_inc(misc_ready, 1)
                elif kind == "A3":
                    hb, h = piece[2:]
                    i = (b * 2 + hb) * H + h
                    if hb == 0 and h == 0:
                        pe.wait_ge(qm_in, 16 * NT * (b + 1))
                    if h == 0:
                        pe.wait_ge(pre_dve, 4 + 2 * B - 1)
                        if n := before(piece, "G1"):
                            pe.wait_ge(g_free, 2 * n)
                        if b * 2 + hb:
                            pe.wait_ge(ctx_ready, b * 2 + hb)
                    if i >= 2 and not (hb == 0 and h == 0):
                        pe.wait_ge(p_ready, i - 1)
                    o = RING[0:KH, i % 2, :].rearrange("k (c q) -> k c q", c=2)
                    pe.matmul(o, identb[0:KH, 0:KH], mbT[:, :, hb * 256:(hb + 1) * 256], start=True, stop=False)
                    for c in range(2):
                        last = pe.matmul(o[:, c, :], KA[:, h, c * KH:(c + 1) * KH],
                                         QA[:, h, hb * 256:(hb + 1) * 256], start=False, stop=(c == 1))
                    last.then_inc(st_ready, 1)
                    if h >= 1:
                        pv(i - 1, b, h - 1)
                elif kind == "A4":
                    pv((b * 2 + piece[2]) * H + H - 1, b, H - 1)
                elif kind == "A5":
                    pe.wait_ge(ctx_ready, 2 * (b + 1))
                    transposes(m, cx)
                    pe.wait_ge(misc_free, m + 1)
                    rows_out(m + 1, cxT, Wo[:], brow[:, 1, :])
                elif kind == "F0":
                    if b == 0:
                        pe.wait_ge(ld_moe, 16 * (6 + 2 * NE))
                    pe.wait_ge(xn_ready, norm_at["F0", b, 0] + 1)
                    transposes(m, xn)
                    take_misc(m + 1)
                    pe.matmul(MISC[0:32, :], Wr1[:], xnTf[:], start=True, stop=True).then_inc(misc_ready, 1)
                    pe.wait_ge(r1_ready, b + 1)
                    for t in range(NT):
                        last = pe.matmul(MISC[:, t * 8:(t + 1) * 8], r1[:, t * 128:(t + 1) * 128], Wr2[:],
                                         start=True, stop=True)
                    last.then_inc(misc_ready, 1)
                    pe.wait_ge(w9_ready, b + 1)
                    transposes(m + 3, W9, NE)
                    pe.wait_ge(misc_free, m + 4)
                    if b:
                        pe.wait_ge(down_free, b * (NE + 1))
                    for t in range(NT):
                        last = pe.matmul(DOWN[:, t * 128:(t + 1) * 128], w9T[:, t * 128:(t + 1) * 128], B2[:],
                                         start=True, stop=True)
                    last.then_inc(down_ready, 1)
                elif kind == "F1":
                    e = piece[2]
                    for c in range(NC):
                        i = (b * NE + e) * NC + c
                        if i >= 2:
                            pe.wait_ge(h_ready, i - 1)
                        pe.matmul(UP[:, i % 2, :], W1[:, e, c * 128:(c + 1) * 128], xnTf[:],
                                  start=True, stop=True).then_inc(up_ready, 1)
                    if e >= 1:
                        down(b, e - 1)
                elif kind == "F2":
                    down(b, NE - 1)
                elif kind == "G0":
                    if b == 0:
                        pe.wait_ge(ld_l1, 16 * 5)
                    pe.wait_ge(xn_ready, norm_at["G0", b, 0] + 1)
                    transposes(m, xn)
                    take_misc(m + 1)
                    pe.matmul(MISC[:], WqT[:], xnT[:], start=True, stop=True).then_inc(misc_ready, 1)
                    rows_out(m + 2, xnT, WqT[:], brow[:, 4, :])
                    rows_out(m + 3, QpT, WoffT[:], boffr[:], HN)
                    pe.wait_ge(pos_ready, b + 1)
                    transposes(m + 4, pos[:, 1], HN)
                elif kind == "G1":
                    h = piece[2]
                    idx = b * H + h
                    if h == 0:
                        if n := before(piece, "A4"):
                            pe.wait_ge(ctx_ready, n)
                    pe.wait_ge(oh_ready, idx + 1)
                    for tp in range(2):
                        i = idx * 2 + tp
                        if i >= 2:
                            pe.wait_ge(g_free, i - 1)
                        for t in range(2):
                            q = slice((2 * tp + t) * 128, (2 * tp + t + 1) * 128)
                            for n in range(NK):
                                o = GC[:, i % 2, t * 160:(t + 1) * 160].rearrange("p (k n c) -> p k n c", k=2, n=NK)[:, :, n, :]
                                for s in range(NS):
                                    pe.matmul(o, OH[:, idx % 2, n, q], T0[:, b, s, h, :].rearrange("p (k c) -> p k c", k=2),
                                              start=(s == 0), stop=False)
                                last = pe.matmul(o, OHR[:, idx % 2, n, q], TR[:, b, h, :].rearrange("p (k c) -> p k c", k=2),
                                                 start=False, stop=True)
                        last.then_inc(g_ready, 1)
                elif kind == "G3":
                    pe.wait_ge(cx1_ready, b + 1)
                    transposes(m, cx)
                    pe.wait_ge(misc_free, m + 1)
                    rows_out(m + 1, cxT, WoT[:], brow[:, 5, :])
                    pe.wait_ge(xn_ready, norm_at["G3", b, 0] + 1)
                    transposes(m + 2, xn)
                    pe.wait_ge(misc_free, m + 3)
                    rows_out(m + 3, xnT, Wsel[:], bsel[:])

        @block.vector
        def _(dve):
            done = [0]

            def step(ins):
                done[0] += 1
                ins.then_inc(dve_done, 1)
                dve.wait_ge(dve_done, done[0])

            def by_tile(a, n):
                return a.unsqueeze(2).broadcast_to((128, NT, n))

            def norm(b, key):
                n = norm_at[key]
                for t in range(NT):
                    last = dve.bn_stats(st[:, t, :], X[:, b, t, :])
                step(last)
                for t in range(NT):
                    last = dve.bn_aggr(mv[:, t, :], st[:, t, :])
                step(last)
                dve.tensor_scalar(ve[:], mv[:, :, 1], EPS, None, ALU.add).then_inc(var_ready, 1)
                dve.wait_ge(rstd_ready, n + 1)
                for t in range(NT):
                    last = dve.tensor_scalar(xn[:, t, :], X[:, b, t, :], mv[:, t, 0:1], rstd[:, t:t + 1],
                                             ALU.subtract, ALU.mult)
                last.then_inc(xn_ready, 1)

            def add_misc(use, b, gate):
                dve.wait_ge(misc_ready, use + 1)
                xb = X[:, b].rearrange("p t d -> p (t d)")
                dve.scalar_tensor_tensor(out=xb, in0=MISC[:], scalar=tg[:, gate:gate + 1], in1=xb,
                                         op0=ALU.mult, op1=ALU.add).then_inc(misc_free, 1)
                dve.wait_ge(misc_free, use + 1)

            dve.wait_ge(ld_const, 16 * 5)
            dve.tensor_copy(identb[:], ident)
            step(dve.tensor_reduce(lg1[:, 0:1], lg[:, 0, :], AX.X, ALU.max))
            dve.tensor_scalar(lg[:, 2, :], lg[:, 0, :], lg1[:, 0:1], None, ALU.subtract).then_inc(pre_dve, 1)
            step(dve.tensor_scalar(kmf.rearrange("p b k -> p (b k)"), km, -1.0, 1.0, ALU.mult, ALU.add))
            step(dve.tensor_reduce(lens[:, 0, :], kmf, AX.X, ALU.add))
            step(dve.tensor_scalar(lens[:, 0, :], lens[:, 0, :], -1.0, None, ALU.add))
            step(dve.tensor_scalar(sgn[:], lens[:, 0, :], 0.0, None, ALU.is_ge))
            step(dve.tensor_scalar(sgn[:], sgn[:], 2.0, -1.0, ALU.mult, ALU.add))
            step(dve.tensor_tensor(lens[:, 0, :], lens[:, 0, :], sgn[:], ALU.mult))
            dve.tensor_scalar(lens[:, 1, :], lens[:, 0, :], -1.0, None, ALU.mult)
            step(dve.reciprocal(lens[:, 2, :], lens[:, 0, :]))
            dve.tensor_scalar(lens[:, 3, :], sgn[:], S2 / (S2 - 1.0), None, ALU.mult)
            step(dve.tensor_tensor(lens[:, 2, :], lens[:, 2, :], sgn[:], ALU.mult))
            dve.wait_ge(ld_attn, 16 * 9)
            for b in range(B):
                for two in range(2):
                    last = dve.tensor_copy(ctxR[:, b, two], ctxP[:, b, R0 + two:R0 + two + 32].unsqueeze(1)
                                           .broadcast_to((128, NS, 32)))
            last.then_inc(pre_dve, 1)
            dve.wait_ge(pre_pe, 1)
            for i in range(2):
                last = dve.tensor_scalar(ksf[:, 2 * i * S2:2 * (i + 1) * S2], RING[:, i, 0:2 * S2], bcol[:, 1:2],
                                         None, ALU.add)
            step(last)
            for s in range(NS - 1):
                step(dve.tensor_copy(ks[:, s, :], ksf))
                step(dve.tensor_tensor(ksf, ksf, ks[:, s, :], ALU.subtract))
            dve.tensor_copy(ks[:, NS - 1, :], ksf).then_inc(pre_dve, 1)
            dve.wait_ge(pre_pe, 2)
            dve.wait_ge(pre_pool, 2)
            for b in range(B):
                for c in range(2):
                    o = (b % 2 * 2 + c) * 128
                    dve.tensor_copy(V0[:, b, c, :, 0:DK], UP[0:KH, b // 2, o:o + 128].rearrange("k (h d) -> k h d", d=DK))
            for b in range(B):
                for ch in range(2):
                    i = 2 * b + ch
                    dve.wait_ge(pre_pe, 3 + i)
                    n = R0 if ch == 0 else RR
                    ps = GC[0:n, ch, :]

                    def heads(a):
                        return a.rearrange("p (w h d) -> p h w d", w=4, h=H)

                    def entry(a):
                        return a.rearrange("p h (w d) -> p h w d", w=4)

                    if ch == 0:
                        step(dve.tensor_copy(entry(T0[:, b, 0]), heads(ps)))
                        step(dve.tensor_tensor(heads(tabf), heads(ps), entry(T0[:, b, 0]), ALU.subtract))
                        step(dve.tensor_copy(entry(T0[:, b, 1]), heads(tabf)))
                        dve.tensor_tensor(entry(T0[:, b, 2]), heads(tabf), entry(T0[:, b, 1]),
                                          ALU.subtract).then_inc(pre_dve, 1)
                    else:
                        dve.tensor_copy(entry(TR[0:32, b]), heads(GC[0:32, ch, :]))
                        step(dve.tensor_copy(tabb[0:n], ps))
                        step(dve.tensor_tensor(tabf[0:n], ps, tabb[0:n], ALU.subtract))
                        dve.tensor_copy(entry(TR[32:64, b]), heads(tabf[32:64]))
                        step(dve.tensor_copy(tabb[0:n], tabf[0:n]))
                        dve.tensor_tensor(entry(TR[64:96, b]), heads(tabf[64:96]), heads(tabb[64:96]),
                                          ALU.subtract).then_inc(pre_dve, 1)
                    dve.wait_ge(pre_dve, 4 + i)
            dve.wait_ge(pre_act, 2)
            step(dve.tensor_scalar(lg[:, 6, :], lg[:, 2, :], lg1[:, 2:3], None, ALU.subtract))
            step(dve.tensor_tensor(lg[:, 6, :], lg[:, 6, :], lg[:, 5, :], ALU.subtract))
            step(dve.tensor_reduce(lg1[:, 0:1], lg[:, 6, :], AX.X, ALU.max))
            step(dve.tensor_scalar(lg[:, 7, :], lg[:, 6, :], lg1[:, 0:1], None, ALU.is_equal))
            step(dve.tensor_tensor(lg[:, 6, :], lg[:, 7, :], cst[:, C_RANK:C_RANK + 8], ALU.mult))
            step(dve.tensor_reduce(lg1[:, 0:1], lg[:, 6, :], AX.X, ALU.max))
            step(dve.tensor_scalar(lg[:, 7, :], lg[:, 6, :], lg1[:, 0:1], None, ALU.is_equal))
            dve.tensor_scalar(Wsel[:], W8[:, 0, :], lg[:, 7, 0:1], None, ALU.mult)
            step(dve.tensor_scalar(bsel[:], b8[:, 0, :], lg[0:1, 7, 0:1], None, ALU.mult))
            for o in range(1, 8):
                dve.scalar_tensor_tensor(out=Wsel[:], in0=W8[:, o, :], scalar=lg[:, 7, o:o + 1], in1=Wsel[:],
                                         op0=ALU.mult, op1=ALU.add)
                step(dve.scalar_tensor_tensor(out=bsel[:], in0=b8[:, o, :], scalar=lg[0:1, 7, o:o + 1], in1=bsel[:],
                                              op0=ALU.mult, op1=ALU.add))
            dve.wait_ge(ld_x, 16 * 7)

            def onehot(b, h):
                idx = b * H + h
                dve.wait_ge(jb_in[h % 2], 16 * (idx // 2 + 1))
                if idx >= 2:
                    dve.wait_ge(g_ready, 2 * (idx - 1))
                dve.tensor_scalar(OH[:, idx % 2], JB[:, h % 2], cst[:, C_K0:C_K0 + 1], None, ALU.is_equal)
                dve.tensor_scalar(OHR[:, idx % 2], JB[0:RR, h % 2], cst[0:RR, C_KR:C_KR + 1], None,
                                  ALU.is_equal).then_inc(oh_ready, 1)

            for piece in schedule:
                kind, b = piece[0], piece[1]
                m = misc_at[piece]
                if kind == "A0":
                    norm(b, ("A0", b, 0))
                    if b:
                        dve.wait_ge(st_ready, b * 2 * H)
                    dve.wait_ge(ld_mask, 32 * (b + 1))
                    dve.tensor_scalar(mb[:], mraw[:], MASKED, None, ALU.mult)
                    dve.tensor_scalar(mbT[:], mrawT[:], MASKED, None, ALU.mult).then_inc(mask_ready, 1)
                    dve.wait_ge(misc_ready, m + 2)
                    dve.tensor_scalar(qf[:], MISC[:], bcol[:, 0:1], 1.0 / math.sqrt(DK), ALU.add,
                                      ALU.mult).then_inc(misc_free, 1)
                    dve.wait_ge(misc_free, m + 2)
                    if b:
                        dve.wait_ge(qs_out, 16 * b)
                    for s in range(NS - 1):
                        step(dve.tensor_copy(qs[:, s, :], qf[:]))
                        step(dve.tensor_tensor(qf[:], qf[:], qs[:, s, :], ALU.subtract))
                    dve.tensor_copy(qs[:, NS - 1, :], qf[:]).then_inc(qs_ready, 1)
                elif kind == "A1":
                    t, h = piece[2], 0
                    for g, n in enumerate(HG):
                        i = (b * NT + t) * len(HG) + g
                        dve.wait_ge(sa_ready, i + 1)
                        dve.tensor_reduce(nmax[:, t, h:h + n], RING[:, i % 2, 0:n * S2].rearrange("p (h k) -> p h k", h=n),
                                          AX.X, ALU.max, negate=True).then_inc(sa_free, 1)
                        h += n
                elif kind == "A2":
                    dve.wait_ge(misc_ready, m + 1)
                    dve.tensor_copy(nmr[:], MISC[0:NT * H, 0:128]).then_inc(misc_free, 1)
                    dve.wait_ge(misc_free, m + 1)
                    if b:
                        dve.wait_ge(nms_out, 16 * b)
                    for s in range(NS - 1):
                        step(dve.tensor_copy(nms[:, s, :], nmr[:]))
                        step(dve.tensor_tensor(nmr[:], nmr[:], nms[:, s, :], ALU.subtract))
                    dve.tensor_copy(nms[:, NS - 1, :], nmr[:]).then_inc(nms_ready, 1)
                elif kind == "A4":
                    hb = piece[2]
                    dve.wait_ge(pv_done, (b * 2 + hb + 1) * H)
                    sums = GC[:, 0, 0:2 * H * 9].rearrange("p (t h d) -> p t h d", t=2, h=H)
                    step(dve.reciprocal(rden[:], sums[:, :, :, DK]))
                    dve.tensor_tensor(cx[:, 2 * hb:2 * hb + 2, :].rearrange("p t (h d) -> p t h d", d=DK),
                                      sums[:, :, :, 0:DK], rden[:].unsqueeze(3).broadcast_to((128, 2, H, DK)),
                                      ALU.mult).then_inc(ctx_ready, 1)
                elif kind == "A5":
                    add_misc(m + 1, b, 0)
                elif kind == "F0":
                    norm(b, ("F0", b, 0))
                    if b == 0:
                        dve.wait_ge(ld_moe, 16 * (6 + 2 * NE))
                    dve.wait_ge(misc_ready, m + 2)
                    dve.tensor_scalar(r1[0:32, :], MISC[0:32, :], br1[:, 0:1], 0.0, ALU.add, ALU.max).then_inc(r1_ready, 1)
                    dve.wait_ge(r1_ready, b + 1)
                    dve.nop().then_inc(misc_free, 1)
                    dve.wait_ge(misc_ready, m + 3)
                    lgt = MISC[:, 0:NT * 8].rearrange("p (t e) -> p t e", t=NT)
                    rank = cst[:, C_RANK:C_RANK + 8].unsqueeze(1).broadcast_to((128, NT, 8))
                    step(dve.tensor_reduce(gs[:, 0], lgt, AX.X, ALU.max))
                    dve.tensor_tensor(gt[:, 0], lgt, by_tile(gs[:, 0], 8), ALU.subtract).then_inc(misc_free, 1)
                    dve.wait_ge(ex_out, 2 * b + 1)
                    step(dve.tensor_reduce(gs[:, 1], gt[:, 1], AX.X, ALU.add))
                    step(dve.reciprocal(gs[:, 2], gs[:, 1]))
                    step(dve.tensor_tensor(gt[:, 2], gt[:, 1], by_tile(gs[:, 2], 8), ALU.mult))

                    def greatest(g, top, eq, rk, at, first):
                        step(dve.tensor_reduce(gs[:, top], gt[:, g], AX.X, ALU.max))
                        step(dve.tensor_tensor(gt[:, eq], gt[:, g], by_tile(gs[:, top], 8), ALU.is_equal))
                        step(dve.tensor_tensor(gt[:, rk], gt[:, eq], rank, ALU.mult))
                        step(dve.tensor_reduce(gs[:, at], gt[:, rk], AX.X, ALU.max))
                        step(dve.tensor_tensor(gt[:, first], gt[:, rk], by_tile(gs[:, at], 8), ALU.is_equal))

                    greatest(2, 3, 3, 4, 4, 5)
                    step(dve.scalar_tensor_tensor(out=gt[:, 6], in0=gt[:, 5], scalar=-4.0, in1=gt[:, 2],
                                                  op0=ALU.mult, op1=ALU.add))
                    greatest(6, 7, 7, 8, 8, 9)
                    dve.tensor_tensor(gs[:, 5], gs[:, 7], gs[:, 3], ALU.subtract).then_inc(d_ready, 1)
                    dve.wait_ge(ex_out, 2 * b + 2)
                    step(dve.tensor_scalar(gs[:, 9], gs[:, 6], 1.0, None, ALU.add))
                    step(dve.reciprocal(gs[:, 1], gs[:, 9]))
                    step(dve.tensor_tensor(gs[:, 2], gs[:, 6], gs[:, 1], ALU.mult))
                    dve.tensor_tensor(gt[:, 10], gt[:, 5], by_tile(gs[:, 1], 8), ALU.mult)
                    step(dve.tensor_tensor(gt[:, 11], gt[:, 9], by_tile(gs[:, 2], 8), ALU.mult))
                    dve.tensor_tensor(W9[:, :, 0:8], gt[:, 10], gt[:, 11], ALU.add).then_inc(w9_ready, 1)
                    dve.wait_ge(down_ready, b * (NE + 1) + 1)
                    dve.tensor_copy(acc[:].rearrange("p t d -> p (t d)"), DOWN[:]).then_inc(down_free, 1)
                elif kind in ("F1", "F2"):
                    e = piece[2] - 1 if kind == "F1" else NE - 1
                    if e >= 0:
                        n = b * (NE + 1) + 1 + e
                        dve.wait_ge(down_ready, n + 1)
                        dve.wait_ge(down_free, n)
                        for t in range(NT):
                            last = dve.scalar_tensor_tensor(out=acc[:, t, :], in0=DOWN[:, t * 128:(t + 1) * 128],
                                                            scalar=W9[:, t, e:e + 1], in1=acc[:, t, :],
                                                            op0=ALU.mult, op1=ALU.add)
                        last.then_inc(down_free, 1)
                    if kind == "F2":
                        dve.wait_ge(down_free, (b + 1) * (NE + 1))
                        step(dve.scalar_tensor_tensor(out=X[:, b], in0=acc[:], scalar=tg[:, 2:3], in1=X[:, b],
                                                      op0=ALU.mult, op1=ALU.add))
                elif kind == "G0":
                    norm(b, ("G0", b, 0))
                    p = [pos[:, i] for i in range(5)]
                    dve.wait_ge(misc_ready, m + 4)
                    dve.tensor_tensor(p[0], MISC[:, 0:NT * HN].rearrange("p (t n) -> p t n", t=NT),
                                      cst[:, C_REF:C_REF + HN].unsqueeze(1).broadcast_to((128, NT, HN)),
                                      ALU.add).then_inc(misc_free, 1)
                    dve.wait_ge(misc_free, m + 4)
                    step(dve.tensor_tensor(p[1], p[0], by_tile(cst[:, C_LOC:C_LOC + NT], HN), ALU.add))
                    size, less, per, back = (lens[:, i, b:b + 1] for i in range(4))
                    dve.tensor_scalar(p[0], p[1], sgn[:, b:b + 1], None, ALU.mult)
                    step(dve.tensor_scalar(p[2], p[1], per, -0.5, ALU.mult, ALU.add))
                    step(dve.tensor_scalar(p[2], p[2], MAGIC, None, ALU.add))
                    step(dve.tensor_scalar(p[2], p[2], -MAGIC, less, ALU.add, ALU.mult))
                    step(dve.tensor_tensor(p[0], p[0], p[2], ALU.add))
                    step(dve.tensor_scalar(p[1], p[0], size, less, ALU.is_ge, ALU.mult))
                    step(dve.tensor_tensor(p[0], p[0], p[1], ALU.add))
                    step(dve.tensor_scalar(p[1], p[0], 0.0, size, ALU.is_lt, ALU.mult))
                    step(dve.tensor_tensor(p[0], p[0], p[1], ALU.add))
                    step(dve.tensor_scalar(p[2], p[0], back, -0.5, ALU.mult, ALU.add))
                    step(dve.tensor_scalar(p[3], p[2], -0.5, MAGIC, ALU.add, ALU.add))
                    step(dve.tensor_scalar(p[3], p[3], -MAGIC, None, ALU.add))
                    dve.tensor_scalar(p[1], p[3], 1.0, None, ALU.add).then_inc(pos_ready, 1)
                    step(dve.tensor_tensor(p[4], p[2], p[3], ALU.subtract))
                    dve.tensor_scalar(wts[:, :, :, 1], p[4], 0.5, None, ALU.mult)
                    step(dve.tensor_scalar(wts[:, :, :, 0], p[4], -0.5, 0.5, ALU.mult, ALU.add))
                    onehot(b, 0)
                elif kind == "G1":
                    h = piece[2]
                    if h + 1 < H:
                        onehot(b, h + 1)
                    if h == 0:
                        dve.wait_ge(misc_free, misc_at["G0", b] + 3)
                    idx = b * H + h
                    dve.wait_ge(g_free, 2 * (idx + 1))
                    dve.tensor_tensor(prod[:, h % 2], GS[:, h % 2].rearrange("p t (n d) -> p t n d", d=DK),
                                      Qp[:, :, h * DK:(h + 1) * DK].unsqueeze(2).broadcast_to((128, NT, 10, DK)),
                                      ALU.mult).then_inc(gk_used, 1)
                    dve.wait_ge(gk_used, idx + 1)
                    step(dve.tensor_reduce(dots[:, :, h, :], prod[:, h % 2], AX.X, ALU.add))
                elif kind == "G2":
                    wf = wts[:].rearrange("p t n w -> p (t n w)")
                    df = dots[:].rearrange("p t h w -> p (t h w)")
                    scf = sc[:].rearrange("p t (h n) -> p (t h) n", n=NK)

                    def taps(a):
                        return a.unsqueeze(2).broadcast_to((128, NT * H, NK))

                    step(dve.tensor_tensor(df, df, wf, ALU.mult))
                    step(dve.tensor_reduce(sc[:].rearrange("p t n -> p (t n)"), df.rearrange("p (n w) -> p n w", w=2),
                                           AX.X, ALU.add))
                    step(dve.tensor_reduce(sm[:, 0], scf, AX.X, ALU.max))
                    dve.tensor_tensor(scf, scf, taps(sm[:, 0]), ALU.subtract).then_inc(z_ready, 1)
                    dve.wait_ge(e_ready, b + 1)
                    step(dve.tensor_reduce(sm[:, 1], scf, AX.X, ALU.add))
                    step(dve.reciprocal(sm[:, 2], sm[:, 1]))
                    step(dve.tensor_tensor(scf, scf, taps(sm[:, 2]), ALU.mult))
                    step(dve.tensor_tensor(aw[:], wts[:], sc[:].unsqueeze(3).broadcast_to((128, NT, HN, 2)), ALU.mult))
                    for t in range(NT):
                        gv = GV[:, :, t, :].rearrange("p h (m d) -> p h m d", d=DK)
                        last = dve.tensor_tensor(gv, gv, aw[:, t].rearrange("p (h n) w -> p h (n w)", h=H).unsqueeze(3)
                                                 .broadcast_to((128, H, 10, DK)), ALU.mult)
                    step(last)
                    for t in range(NT):
                        last = dve.tensor_reduce(cx[:, t].rearrange("p (h d) -> p h d", d=DK),
                                                 GV[:, :, t, :].rearrange("p h (m d) -> p h d m", d=DK), AX.X, ALU.add)
                    last.then_inc(cx1_ready, 1)
                elif kind == "G3":
                    add_misc(m + 1, b, 1)
                    norm(b, ("G3", b, 0))
                    add_misc(m + 3, b, 3)
                    dve.nop().then_inc(x_done, 1)


def order():
    schedule = []
    for b in range(B):
        schedule += [("A0", b)] + [("A1", b, t) for t in range(NT)] + [("A2", b)]
        for hb in range(2):
            schedule += [("A3", b, hb, h) for h in range(H)] + [("A4", b, hb)]
        schedule += [("A5", b), ("F0", b)] + [("F1", b, e) for e in range(NE)] + [("F2", b)]
        schedule += [("G0", b)] + [("G1", b, h) for h in range(H)] + [("G2", b), ("G3", b)]
    return schedule


def kernel(**inputs):
    import numpy as np
    import concourse.bacc as bacc
    from concourse.bass_utils import run_bass_kernel_spmd

    a = {k: np.ascontiguousarray(v) for k, v in inputs.items()}
    row = np.arange(128)
    consts = np.zeros((128, C_N), np.float32)
    consts[:, C_ID:C_ID + 128] = np.eye(128)
    consts[:, C_K0] = row
    consts[:, C_KR] = R0 + row % 32
    consts[:, C_LOC:C_LOC + NT] = row[:, None] + 128 * np.arange(NT)
    consts[:, C_REF:C_REF + HN] = np.tile(np.arange(NK) + (-NK // 2), H)
    consts[:, C_RANK:C_RANK + 8] = 8 - np.arange(8)
    mask = a["mask_BxSxS2_bf0"]
    b1 = np.concatenate([a["L0_ffn_be1"], a["L0_ffn_bs1"][None]])
    laid_out = {
        "x": a["x"],
        "ctxT": a["ctx_1024"].transpose(2, 0, 1),
        "mask": mask,
        "maskT": mask.transpose(0, 2, 1),
        "kmask": a["mask_BxS2_if0"],
        "gates": np.concatenate([a["g_xattn"], a["g_ffn"]]),
        "consts": consts,
        "wq": a["L0_xattn_Wq"], "wk": a["L0_xattn_Wk"], "wv": a["L0_xattn_Wv"], "wo": a["L0_xattn_Wo"],
        "bq_col": a["L0_xattn_bq"][:, None], "bk_col": a["L0_xattn_bk"][:, None],
        "rows": np.stack([a["L0_xattn_bv"], a["L0_xattn_bo"], a["L1_xattn_bk"], a["L1_xattn_bv"],
                          a["L1_xattn_bq"], a["L1_xattn_bo"]])[None],
        "wr1": a["L0_ffn_Wr1"], "br1_col": a["L0_ffn_br1"][:, None],
        "wr2": a["L0_ffn_Wr2"], "br2": a["L0_ffn_br2"][None],
        "w1": np.concatenate([a["L0_ffn_We1"], a["L0_ffn_Ws1"][None]]),
        "b1_cols": b1.reshape(NE, NC, 128).transpose(2, 0, 1),
        "w2": np.concatenate([a["L0_ffn_We2"], a["L0_ffn_Ws2"][None]]),
        "b2": np.concatenate([a["L0_ffn_be2"], a["L0_ffn_bs2"][None]]),
        "wkT": a["L1_xattn_Wk"].T, "wvT": a["L1_xattn_Wv"].T, "wqT": a["L1_xattn_Wq"].T,
        "woffT": a["L1_xattn_Woff"].T, "woT": a["L1_xattn_Wo"].T,
        "bq1_col": a["L1_xattn_bq"][:, None], "boff": a["L1_xattn_boff"][None],
        "w8": a["L1_ffn_W"], "b8": a["L1_ffn_b"][None], "logits": a["L1_ffn_logits"], "u": a["L1_ffn_u"],
    }
    nc = bacc.Bacc("TRN2", target_bir_lowering=False, num_devices=1, dynamic_dma_scratch_size=1024)
    arrays, args = {}, []
    for name, v in laid_out.items():
        v = np.ascontiguousarray(v)
        arrays[f"in_{name}"] = v
        args.append(nc.dram_tensor(f"in_{name}", v.shape, mybir.dt.from_np(v.dtype), kind="ExternalInput").ap())
    args.append(nc.dram_tensor("out_x", (B, S, D), F32, kind="ExternalOutput").ap())
    build(nc, *args)
    r = run_bass_kernel_spmd(nc, [arrays], core_ids=[0])
    return r.results[0]["out_x"]
```

```python
import concourse.bass as bass
from concourse import mybir
from contextlib import ExitStack
import math

F32 = mybir.dt.float32
BF16 = mybir.dt.bfloat16
ALU = mybir.AluOpType
ACT = mybir.ActivationFunctionType
AX = mybir.AxisListType

B, S, D = 4, 512, 128
S2 = 154
H, DK = 16, 8
NT = S // 128
KM, KT = 128, S2 - 128
SU = 12
VW = 8 * (DK + 1)
NE, NC = 9, 4
NK = 5
HN = H * NK
NS = 3
SLOT_Q = (0, 0, 0, 1, 1, 2)
SLOT_K = (0, 1, 2, 0, 1, 0)
QR = len(SLOT_Q) * DK
QM = QR + NS
HG = (3, 3, 3, 3, 2, 2)
R0 = 128
RR = NS * 32
MASKED = -1e18
MAGIC = 12582912.0
EPS = 1e-5
HS = 8
LD_MOE = 6 + 2 * (NE // 3)
C_ID, C_K0, C_KR, C_LOC, C_REF, C_RANK, C_TAIL, C_N = 0, 128, 129, 130, 134, 214, 222, 223


def build(nc, x, ctxT, mask, maskT, kmask, gates, consts, wq, wk, wv, wo, bq_col, bk_col, rows,
          wr1, br1_col, wr2, br2, w1, b1_cols, w2, b2, wkT, wvT, wqT, woffT, woT, bq1_col, boff,
          w8, b8_src, logits, u, out):
    ctx = ExitStack()
    dq = nc.dram_tensor("scratch_q_parts", [B, NS, 128, S], BF16, kind="Internal").ap()
    dk = nc.dram_tensor("scratch_k_parts", [NS, 128, B * S2], BF16, kind="Internal").ap()
    dm = nc.dram_tensor("scratch_max_parts", [B, NT, H, NS, 128], BF16, kind="Internal").ap()
    dj = nc.dram_tensor("scratch_positions", [B, HN, S], BF16, kind="Internal").ap()

    with ctx:
        def sb(name, shape, dt=F32):
            return ctx.enter_context(nc.sbuf_tensor(name, shape, dt))

        def pb(name, shape):
            return ctx.enter_context(nc.psum_tensor(name, shape, F32))

        def sem(name):
            return ctx.enter_context(nc.semaphore(name))

        X = sb("X", [128, B, NT, D])
        cst = sb("cst", [128, C_N])
        ident = cst[:, C_ID:C_ID + 128]
        identb = sb("identb", [128, 128], BF16)
        ones = sb("ones", [1, 128])
        Wq, Wk, Wv, Wo = (sb(n, [128, 128]) for n in ("Wq", "Wk", "Wv", "Wo"))
        WkT, WvT, WqT, WoT = (sb(n, [128, 128]) for n in ("WkT", "WvT", "WqT", "WoT"))
        WoffT = sb("WoffT", [128, HN])
        brow = sb("brow", [1, 6, 128])
        bcol = sb("bcol", [128, 3])
        boffr = sb("boffr", [1, HN])
        Wr1 = sb("Wr1", [128, 32])
        br1 = sb("br1", [32, 1])
        Wr2 = sb("Wr2", [33, 8])
        W1 = sb("W1", [128, NE, NC * 128])
        b1 = sb("b1", [128, NE, NC])
        W2 = sb("W2", [128, NE, NC, D])
        B2 = sb("B2", [NE, D])
        Wsel = sb("Wsel", [128, 128])
        bsel = sb("bsel", [1, 128])
        tg = sb("tg", [128, 4])
        lens = sb("lens", [128, 4, B])
        sgn = sb("sgn", [128, B])
        KA = sb("KA", [QM, H, S2], BF16)
        VC = sb("VC", [128, B, 2, 128])
        VM = sb("VM", [128, VW - DK - 1 + H * VW])
        VT = sb("VT", [128, 2, 2 * VW])
        T0 = sb("T0", [R0, B, NS, H, 32], BF16)
        TR = sb("TR", [RR, B, H, 32], BF16)
        mraw = sb("mraw", [128, NT, S2], mybir.dt.uint8)
        mrawM = sb("mrawM", [KM, S], mybir.dt.uint8)
        mrawR = sb("mrawR", [KT, S], mybir.dt.uint8)
        mb = sb("mb", [128, NT, S2], BF16)
        mbM = sb("mbM", [KM, S], BF16)
        mbR = sb("mbR", [KT, S], BF16)
        ident4 = sb("ident4", [KT, 4, 32], BF16)
        QA = sb("QA", [QM, H, S], BF16)
        qs = sb("qs", [128, NS, S], BF16)
        nmax = sb("nmax", [128, NT, H])
        nmr = sb("nmr", [NT * H, 128])
        nms = sb("nms", [NT * H, NS, 128], BF16)
        PT = sb("PT", [128, 2, 2, 256])
        OT = sb("OT", [VW, 2, 256])
        rden = sb("rden", [128, 2, H])
        cx = sb("cx", [128, NT, D])
        xn = sb("xn", [128, NT, D])
        qf = xn[:].rearrange("p t d -> p (t d)")
        st = sb("st", [128, NT, 6])
        mv = sb("mv", [128, NT, 2])
        ve = sb("ve", [128, NT])
        rstd = sb("rstd", [128, NT])
        mhalf = sb("mhalf", [128, NT])
        ones128 = sb("ones128", [128, H])
        one_col = ones128[:]
        xnT = sb("xnT", [128, S])
        cxT = xnT
        xnTf = sb("xnTf", [128, 2, S])
        r1 = sb("r1", [33, S])
        gt = sb("gt", [128, 10, NT, 8])
        gs = sb("gs", [128, 10, NT])
        W9 = sb("W9", [128, 2, NT, NE])
        w9T = sb("w9T", [NE, S])
        hT = sb("hT", [128, HS, S])
        acc = sb("acc", [128, NT, D])
        QpT = sb("QpT", [128, S])
        Qp = sb("Qp", [128, NT, D])
        pos = sb("pos", [128, 5, NT, HN])
        wts = sb("wts", [128, NT, HN, 2])
        jT = sb("jT", [HN, S], BF16)
        JB = sb("JB", [128, 2, NK, S], BF16)
        OH = sb("OH", [R0, 2, NK, S], BF16)
        OHR = sb("OHR", [RR, 2, NK, S], BF16)
        prod = sb("prod", [128, NT, 10, DK])
        GS = sb("GS", [128, 2 + H, NT, NK * 16])
        GV = GS[:, 2:2 + H]
        dots = sb("dots", [128, NT, H, 10])
        aw = pos[:, 2:4].rearrange("p a t n -> p (a t n)").rearrange("p (t n w) -> p t n w", t=NT, w=2)
        sc = pos[:, 0]
        sm = sb("sm", [128, 3, NT * H])
        GVf = GV.rearrange("p h t c -> p (h t c)")
        W8 = GVf[:, 0:1024].rearrange("p (o e) -> p o e", o=8)
        ctxP = GVf[:, 1024:1024 + B * 162].rearrange("p (b k) -> p b k", b=B)
        ctxR = GVf[:, 3824:3824 + B * 256].rearrange("p (b w s k) -> p b w s k", b=B, w=2, s=4)
        ksf = GVf[:, 2696:2696 + B * S2]
        tabf = GVf[:, 3312:3824]
        ks = hT[:, 0:2, :].rearrange("p a s -> p (a s)").bitcast(BF16)[:, 0:NS * B * S2] \
            .rearrange("p (s k) -> p s k", s=NS)
        tabb = GVf[:, 4848:5104].bitcast(BF16)
        b8 = GVf[0:1, 1672:2696].rearrange("p (o e) -> p o e", o=8)
        km = aw.rearrange("p t n w -> p (t n w)").bitcast(mybir.dt.int32)[:, 0:B * S2]
        kmf = dots[:, :, :, :].rearrange("p t h w -> p (t h w)")[:, 0:B * S2].rearrange("p (b k) -> p b k", b=B)
        vrow = hT[0:1, 4, 0:162]
        vrowR = hT[0:1, 5, 0:256].rearrange("p (w s k) -> p w s k", w=2, s=4)
        lg = sb("lg", [128, 8, 8])
        lg1 = sb("lg1", [128, 4])
        gin = sb("gin", [128, 4])

        UP = pb("UP", [128, 2, 512])
        DOWN = pb("DOWN", [128, 2, 512])
        MISC = pb("MISC", [128, 512])
        RING = pb("RING", [128, 2, 512])
        SUM = pb("SUM", [128, 512])

        schedule = order()
        uses = {k: 1 for k in ("A0a", "A0b", "A2", "A5a", "A5b", "F0a", "F0b", "F0c", "F0d", "G0a", "G0c", "G0d",
                               "G3a", "G3b", "G3c", "G3d", "A4b")}
        uses["G0b"] = 2
        misc_at, n = {}, 0
        for piece in schedule:
            misc_at[piece] = n
            n += uses.get(piece[0], 0)
        norm_at = {(p[0], p[1]): n for n, p in enumerate(p for p in schedule if p[0] in ("A0a", "F0a", "G0a", "G3c"))}

        def before(piece, kind):
            return sum(p[0] == kind for p in schedule[:schedule.index(piece)])

        ld_const = sem("ld_const")
        ld_ctx = sem("ld_ctx")
        ld_q = sem("ld_q")
        ld_x = sem("ld_x")
        ld_tab = sem("ld_tab")
        ld_moe = sem("ld_moe")
        ld_l1 = sem("ld_l1")
        ld_mask = sem("ld_mask")
        mask_ready = sem("mask_ready")
        dve_done = sem("dve_done")
        act_done = sem("act_done")
        pool_done = sem("pool_done")
        lg_ready = sem("lg_ready")
        noise_ready = sem("noise_ready")
        gate_ready = sem("gate_ready")
        k_ready = sem("k_ready")
        ks_ready = sem("ks_ready")
        v_ready = sem("v_ready")
        v_read = sem("v_read")
        cr_ready = sem("cr_ready")
        t_ready = sem("t_ready")
        t_read = sem("t_read")
        pre_pool = sem("pre_pool")
        kparts_out = sem("kparts_out")
        kparts_in = sem("kparts_in")
        misc_ready = sem("misc_ready")
        misc_free = sem("misc_free")
        var_ready = sem("var_ready")
        rstd_ready = sem("rstd_ready")
        xn_ready = sem("xn_ready")
        xnT_ready = sem("xnT_ready")
        qs_ready = sem("qs_ready")
        qs_out = sem("qs_out")
        qa_in = sem("qa_in")
        sa_ready = sem("sa_ready")
        sa_free = sem("sa_free")
        nms_ready = sem("nms_ready")
        nms_out = sem("nms_out")
        qm_in = sem("qm_in")
        st_ready = sem("st_ready")
        p_ready = sem("p_ready")
        pv_done = sem("pv_done")
        vm_ready = sem("vm_ready")
        ot_ready = sem("ot_ready")
        ctx_ready = sem("ctx_ready")
        cxT_ready = sem("cxT_ready")
        r1_ready = sem("r1_ready")
        d_ready = sem("d_ready")
        ex_out = sem("ex_out")
        w9_ready = sem("w9_ready")
        w9T_ready = sem("w9T_ready")
        up_ready = sem("up_ready")
        h_ready = sem("h_ready")
        down_ready = sem("down_ready")
        down_free = sem("down_free")
        qpT_ready = sem("qpT_ready")
        qp_ready = sem("qp_ready")
        pos_ready = sem("pos_ready")
        jT_ready = sem("jT_ready")
        j_out = sem("j_out")
        jb_in = [sem(f"jb_in{i}") for i in range(2)]
        oh_ready = sem("oh_ready")
        g_ready = sem("g_ready")
        g_free = sem("g_free")
        gk_used = sem("gk_used")
        z_ready = sem("z_ready")
        e_ready = sem("e_ready")
        cx1_ready = sem("cx1_ready")
        x3_ready = sem("x3_ready")
        x_done = sem("x_done")
        stored = sem("stored")

        def down_count(k):
            return k // (NC * NE) * (NE + 1) + k // NC % NE + 2

        block = ctx.enter_context(nc.Block())

        @block.sync
        def _(sp):
            for dst, src in ((cst[:], consts), (gin[:], gates.partition_broadcast(128)),
                             (lg[:, 0, :], logits.partition_broadcast(128)),
                             (lg[:, 1, :], u.partition_broadcast(128)),
                             (km, kmask.rearrange("b k -> (b k)").partition_broadcast(128))):
                sp.dma_start(dst, src).then_inc(ld_const, 16)
            sp.wait_ge(pre_pool, 1)
            for dst, src in ((ctxP[:, :, 1:1 + S2], ctxT), (Wk[:], wk), (bcol[:, 1:2], bk_col), (Wv[:], wv),
                             (brow[:], rows)):
                sp.dma_start(dst, src).then_inc(ld_ctx, 16)
            for dst, src in ((X[:, 0], x[0].rearrange("(t p) d -> p t d", p=128)), (Wq[:], wq),
                             (bcol[:, 0:1], bq_col), (Wo[:], wo)):
                sp.dma_start(dst, src).then_inc(ld_q, 16)
            for dst, src in ((WkT[:], wkT), (WvT[:], wvT), (W8, w8.rearrange("o d e -> d o e")), (b8, b8_src)):
                sp.dma_start(dst, src).then_inc(ld_tab, 16)
            for piece in schedule:
                kind, b = piece[0], piece[1]
                if kind == "K":
                    sp.wait_ge(ks_ready, 1)
                    sp.dma_start(dk.rearrange("s e k -> e s k"), ks).then_inc(kparts_out, 16)
                elif kind == "A0b":
                    if b >= 1:
                        sp.wait_ge(mask_ready, b)
                    sp.dma_start(mraw[:], mask[b].rearrange("(t p) k -> p t k", p=128)).then_inc(ld_mask, 16)
                    sp.dma_start(mrawM[:], maskT[b, 0:KM]).then_inc(ld_mask, 16)
                    sp.dma_start(mrawR[:], maskT[b, KM:S2]).then_inc(ld_mask, 16)
                    sp.wait_ge(qs_ready, b + 1)
                    sp.dma_start(dq[b].rearrange("s e q -> e s q"), qs[:]).then_inc(qs_out, 16)
                    sp.wait_ge(qs_out, 16 * (b + 1))
                    if b >= 1:
                        sp.wait_ge(st_ready, b * 2 * SU)
                    else:
                        sp.wait_ge(kparts_out, 16)
                        sp.wait_ge(pre_pool, 2)
                    for i, s in enumerate(SLOT_K):
                        sp.dma_start(KA[i * DK:(i + 1) * DK], dk[s].rearrange("(h d) k -> d h k", d=DK)
                                     [:, :, b * S2:(b + 1) * S2]).then_inc(kparts_in, 16)
                    for i, s in enumerate(SLOT_Q):
                        sp.dma_start(QA[i * DK:(i + 1) * DK], dq[b, s].rearrange("(h d) q -> d h q", d=DK)).then_inc(qa_in, 16)
                elif kind == "A2":
                    sp.wait_ge(nms_ready, b + 1)
                    sp.dma_start(dm[b].rearrange("t h s q -> (t h) s q"), nms[:]).then_inc(nms_out, 16)
                    sp.wait_ge(nms_out, 16 * (b + 1))
                    for t in range(NT):
                        sp.dma_start(QA[QR:QM, :, t * 128:(t + 1) * 128], dm[b, t].rearrange("h s q -> s h q")).then_inc(qm_in, 16)
                elif kind == "G0d":
                    sp.wait_ge(jT_ready, b + 1)
                    sp.dma_start(dj[b], jT[:]).then_inc(j_out, 16)
                    sp.wait_ge(j_out, 16 * (b + 1))
                    for h in range(2):
                        if b >= 1:
                            sp.wait_ge(oh_ready, b * H + h - 1)
                        sp.dma_start(JB[:, h % 2], dj[b, h * NK:(h + 1) * NK].partition_broadcast(128)).then_inc(jb_in[h % 2], 16)
                elif kind == "G1" and piece[2] + 2 < H:
                    h = piece[2] + 2
                    sp.wait_ge(oh_ready, b * H + h - 1)
                    sp.dma_start(JB[:, h % 2], dj[b, h * NK:(h + 1) * NK].partition_broadcast(128)).then_inc(jb_in[h % 2], 16)
                elif kind == "G3d":
                    sp.wait_ge(x_done, b + 1)
                    sp.dma_start(out[b].rearrange("(t p) d -> p t d", p=128), X[:, b]).then_inc(stored, 16)
            sp.wait_ge(stored, 16 * B)

        @block.gpsimd
        def _(pool):
            done = [0]

            def step(ins):
                done[0] += 1
                ins.then_inc(pool_done, 1)
                pool.wait_ge(pool_done, done[0])

            pool.memset(GVf[:, 1024:1672], 0.0).then_inc(pre_pool, 1)
            step(pool.memset(vrow, 0.0))
            step(pool.memset(vrow[:, 1:1 + S2], 1.0))
            for t, v in ((ones, 1.0), (ones128, 1.0), (mhalf, -0.5), (VM, 0.0), (VT, 0.0), (W9, 1.0), (KA, 1.0)):
                step(pool.memset(t[:], v))
            step(pool.memset(r1[32:33, :], 1.0))
            for w in range(2):
                last = pool.tensor_copy(vrowR[:, w], vrow[:, R0 + w:R0 + w + 32].unsqueeze(1).broadcast_to((1, 4, 32)))
            last.then_inc(pre_pool, 1)
            for n in range(4 * B):
                pool.wait_ge(var_ready, n + 1)
                pool.tensor_tensor(rstd[:], ve[:], mhalf[:], ALU.pow).then_inc(rstd_ready, 1)

        @block.scalar
        def _(act):
            for dst, src in ((Wr1[:], wr1), (br1[:], br1_col), (Wr2[0:32, :], wr2), (Wr2[32:33, :], br2),
                             (b1[:], b1_cols), (B2[:], b2)):
                act.dma_start(dst, src).then_inc(ld_moe, 16)
            for b in range(1, B):
                act.dma_start(X[:, b], x[b].rearrange("(t p) d -> p t d", p=128)).then_inc(ld_x, 16)
            for e in range(0, NE, 3):
                act.dma_start(W1[:, e:e + 3], w1[e:e + 3].rearrange("e d i -> d e i")).then_inc(ld_moe, 16)
                act.dma_start(W2[:, e:e + 3], w2[e:e + 3].rearrange("e (c i) d -> i e c d", i=128)).then_inc(ld_moe, 16)
            for dst, src in ((WqT[:], wqT), (WoT[:], woT), (WoffT[:], woffT), (bcol[:, 2:3], bq1_col),
                             (boffr[:], boff)):
                act.dma_start(dst, src).then_inc(ld_l1, 16)
            act.wait_ge(ld_const, 16 * 5)
            act.activation(tg[:], gin[:], ACT.Tanh).then_inc(gate_ready, 1)

            def evacuate(use, dst, src, bias=0.0):
                act.wait_ge(misc_ready, use + 1)
                act.activation(dst, src, ACT.Identity, bias=bias).then_inc(misc_free, 1)

            for piece in schedule:
                kind, b = piece[0], piece[1]
                m = misc_at[piece]
                if kind == "W":
                    act.wait_ge(lg_ready, 1)
                    act.activation(lg[:, 3, :], lg[:, 2, :], ACT.Exp, accum_out=lg1[:, 1:2]).then_inc(act_done, 1)
                    act.wait_ge(act_done, 1)
                    act.activation(lg1[:, 2:3], lg1[:, 1:2], ACT.Ln)
                    act.activation(lg[:, 4, :], lg[:, 1, :], ACT.Ln).then_inc(act_done, 1)
                    act.wait_ge(act_done, 2)
                    act.activation(lg[:, 5, :], lg[:, 4, :], ACT.Ln, scale=-1.0).then_inc(noise_ready, 1)
                elif kind in ("A0a", "G0a", "G3c"):
                    evacuate(m, xnT[:], MISC[:])
                elif kind == "A3":
                    hb, u = piece[2:]
                    i = (b * 2 + hb) * SU + u
                    act.wait_ge(st_ready, i + 1)
                    if i >= 2:
                        act.wait_ge(pv_done, i - 1)
                    n = 1 if u % 3 == 2 else 2
                    act.activation(PT[:, i % 2, 0:n, :], RING[:, i % 2, 0:n * 256].rearrange("k (h q) -> k h q", h=n),
                                   ACT.Exp).then_inc(p_ready, 1)
                elif kind == "A4a":
                    act.wait_ge(pv_done, (b * 2 + piece[2] + 1) * SU)
                    if b * 2 + piece[2]:
                        act.wait_ge(ctx_ready, b * 2 + piece[2])
                    act.activation(OT[:], SUM[0:VW, :].rearrange("k (g q) -> k g q", g=2), ACT.Identity).then_inc(ot_ready, 1)
                elif kind in ("A5a", "G3a"):
                    evacuate(m, cxT[:], MISC[:])
                elif kind == "F0a":
                    evacuate(m, xnTf[:, b % 2], MISC[:])
                elif kind == "F0c":
                    act.wait_ge(misc_free, m + 1)
                    act.activation(gt[:, 1], gt[:, 0], ACT.Exp).then_inc(ex_out, 1)
                    act.wait_ge(d_ready, b + 1)
                    act.activation(gs[:, 6], gs[:, 5], ACT.Exp, scale=0.5).then_inc(ex_out, 1)
                elif kind == "F0d":
                    evacuate(m, w9T[:], MISC[0:NE, :])
                elif kind == "F1" and piece[2] < NE:
                    e, c = piece[2:]
                    if b == 0 and e == 0 and c == 0:
                        act.wait_ge(kparts_out, 16)
                        act.wait_ge(ld_moe, 16 * LD_MOE)
                    i = (b * NE + e) * NC + c
                    act.wait_ge(up_ready, i + 1)
                    if i >= HS:
                        act.wait_ge(down_ready, down_count(i - HS))
                    act.activation(hT[:, i % HS, :], UP[:, i % 2, :], ACT.Silu,
                                   bias=b1[:, e, c:c + 1]).then_inc(h_ready, 1)
                elif kind == "G0b":
                    act.wait_ge(ld_l1, 16 * 5)
                    evacuate(m, QpT[:], MISC[:], bias=bcol[:, 2:3])
                    if b >= 1:
                        act.wait_ge(gk_used, b * H)
                    evacuate(m + 1, Qp[:].rearrange("p t e -> p (t e)"), MISC[:])
                elif kind == "G0d":
                    if b >= 1:
                        act.wait_ge(j_out, 16 * b)
                    act.wait_ge(misc_ready, m + 1)
                    act.activation(jT[:], MISC[0:HN, :], ACT.Identity).then_inc(jT_ready, 1)
                    act.wait_ge(jT_ready, b + 1)
                    act.nop().then_inc(misc_free, 1)
                elif kind == "G1":
                    h = piece[2]
                    if h == 0 and b >= 1:
                        act.wait_ge(cx1_ready, b)
                    if b * H + h >= 2:
                        act.wait_ge(gk_used, b * H + h - 1)
                    for tp in range(2):
                        i = (b * H + h) * 2 + tp
                        act.wait_ge(g_ready, i + 1)
                        both = GS[:, h % 2:h + 3:h + 2 - h % 2, 2 * tp:2 * tp + 2, :]
                        act.activation(both.rearrange("p k t c -> p t k c"),
                                       RING[:, i % 2, 0:320].rearrange("p (t k c) -> p t k c", t=2, k=2),
                                       ACT.Identity).then_inc(g_free, 1)
                elif kind == "G2a":
                    act.wait_ge(z_ready, b + 1)
                    act.activation(sc, sc, ACT.Exp, scale=1.0 / math.sqrt(DK)).then_inc(e_ready, 1)

        @block.tensor
        def _(pe):
            def take_misc(use):
                if use >= 1:
                    pe.wait_ge(misc_free, use)

            def transposes(use, src, width=128):
                take_misc(use)
                for t in range(NT):
                    last = pe.transpose(MISC[0:width, t * 128:(t + 1) * 128], src[:, t, :], ident)
                last.then_inc(misc_ready, 1)

            def rows_out(use, srcT, w, bias, width=128):
                take_misc(use)
                pe.matmul(MISC[:, 0:NT * width].rearrange("p (t e) -> p t e", t=NT), ones[:],
                          bias.unsqueeze(1).broadcast_to((1, NT, width)), start=True, stop=False)
                for t in range(NT):
                    last = pe.matmul(MISC[:, t * width:(t + 1) * width], srcT[:, t * 128:(t + 1) * 128], w,
                                     start=False, stop=(t == NT - 1))
                last.then_inc(misc_ready, 1)

            def pv(b, hb, u):
                i = (b * 2 + hb) * SU + u
                pe.wait_ge(p_ready, i + 1)
                four, r = divmod(u, 3)
                o = SUM[0:VW, four // 2 * 256:(four // 2 + 1) * 256]
                if r < 2:
                    for k in range(2):
                        h = 4 * four + 2 * r + k
                        first = h * VW + VW - (DK + 1) - (DK + 1) * (h % 8)
                        last = pe.matmul(o, VM[:, first:first + VW], PT[:, i % 2, k, :],
                                         start=(h % 8 == 0), stop=False)
                else:
                    last = pe.matmul(o, VT[:, four // 2, four % 2 * VW:(four % 2 + 1) * VW], PT[:, i % 2, 0, :],
                                     start=False, stop=(four % 2 == 1))
                last.then_inc(pv_done, 1)

            def down(b, e, t):
                k = (b * NE + e) * NC
                n = b * (NE + 1) + 1 + e
                if t == 0:
                    pe.wait_ge(h_ready, k + NC)
                    pe.wait_ge(down_free, n - 1)
                for c in range(NC):
                    last = pe.matmul(DOWN[:, n % 2, t * 128:(t + 1) * 128], hT[:, (k + c) % HS, t * 128:(t + 1) * 128],
                                     W2[:, e, c, :], start=(c == 0), stop=(c == NC - 1))
                if t == NT - 1:
                    last.then_inc(down_ready, 1)

            for piece in schedule:
                kind, b = piece[0], piece[1]
                m = misc_at[piece]
                if kind == "K":
                    pe.wait_ge(ld_ctx, 16 * 5)
                    for i in range(2):
                        last = pe.matmul(DOWN[:, i, 0:2 * S2].rearrange("p (b k) -> p b k", b=2), Wk[:],
                                         ctxP[:, 2 * i:2 * i + 2, 1:1 + S2], start=True, stop=True)
                    last.then_inc(k_ready, 1)
                elif kind == "V":
                    pe.wait_ge(pre_pool, 2)
                    pe.wait_ge(cr_ready, 1)
                    for n in range(B):
                        for c, (rws, valid) in enumerate((
                                (ctxP[:, n, 1:1 + KM], ones[:]),
                                (ctxR[:, n, 1].rearrange("p s k -> p (s k)"), vrowR[:, 1].rearrange("p s k -> p (s k)")))):
                            o = UP[:, n // 2, (n % 2 * 2 + c) * 128:(n % 2 * 2 + c + 1) * 128]
                            pe.matmul(o, valid, brow[:, 0, :], start=True, stop=False)
                            last = pe.matmul(o, rws, Wv[:], start=False, stop=True)
                    last.then_inc(v_ready, 1)
                elif kind == "T":
                    ch = piece[2]
                    i = 2 * b + ch
                    if i == 0:
                        pe.wait_ge(ld_tab, 16 * 4)
                        pe.wait_ge(v_read, 1)
                    if i >= 2:
                        pe.wait_ge(t_read, i - 1)
                    for kv, w in enumerate((WkT, WvT)):
                        for two in range(2):
                            if ch == 0:
                                o = UP[:, ch, (kv * 2 + two) * 128:(kv * 2 + two + 1) * 128]
                                valid, rws = vrow[:, two:two + R0], ctxP[:, b, two:two + R0]
                            else:
                                o = UP[0:RR, ch, (kv * 2 + two) * 128:(kv * 2 + two + 1) * 128]
                                valid = vrowR[:, two, 0:NS].rearrange("p s k -> p (s k)")
                                rws = ctxR[:, b, two, 0:NS].rearrange("p s k -> p (s k)")
                            pe.matmul(o, valid, brow[:, 2 + kv, :], start=True, stop=False)
                            last = pe.matmul(o, rws, w[:], start=False, stop=True)
                    last.then_inc(t_ready, 1)
                elif kind == "A0a":
                    if b == 0:
                        pe.wait_ge(ld_q, 16 * 4)
                    pe.wait_ge(xn_ready, norm_at["A0a", b] + 1)
                    transposes(m, xn)
                elif kind == "A0b":
                    take_misc(m)
                    pe.matmul(MISC[:], Wq[:], xnT[:], start=True, stop=True).then_inc(misc_ready, 1)
                elif kind == "A1":
                    t = piece[2]
                    if t == 0:
                        pe.wait_ge(qa_in, 16 * len(SLOT_Q) * (b + 1))
                        pe.wait_ge(mask_ready, b + 1)
                        pe.wait_ge(kparts_in, 16 * len(SLOT_K) * (b + 1))
                        if b:
                            pe.wait_ge(p_ready, b * 2 * SU)
                        if n := before(piece, "G1"):
                            pe.wait_ge(g_free, 2 * n)
                    h = 0
                    for g, n in enumerate(HG):
                        i = (b * NT + t) * len(HG) + g
                        if i >= 2:
                            pe.wait_ge(sa_free, i - 1)
                        o = RING[:, i % 2, 0:n * S2].rearrange("p (h k) -> p h k", h=n)
                        pe.matmul(o, identb[:], mb[:, t, :].unsqueeze(1).broadcast_to((128, n, S2)),
                                  start=True, stop=False)
                        for k in range(n):
                            last = pe.matmul(o[:, k, :], QA[0:QR, h, t * 128:(t + 1) * 128],
                                             KA[0:QR, h, :], start=False, stop=(k == n - 1))
                            h += 1
                        last.then_inc(sa_ready, 1)
                elif kind == "A2":
                    pe.wait_ge(sa_free, (b + 1) * NT * len(HG))
                    take_misc(m)
                    pe.transpose(MISC[0:NT * H, 0:128], nmax[:].rearrange("p t h -> p (t h)"), ident).then_inc(misc_ready, 1)
                elif kind == "A3":
                    hb, u = piece[2:]
                    i = (b * 2 + hb) * SU + u
                    if u == 0:
                        if hb == 0:
                            pe.wait_ge(qm_in, 16 * NT * (b + 1))
                            pe.wait_ge(vm_ready, b + 1)
                        if b * 2 + hb:
                            pe.wait_ge(ot_ready, b * 2 + hb)
                    if i >= 2 and not (hb == 0 and u == 0):
                        pe.wait_ge(p_ready, i - 1)
                    q = slice(hb * 256, (hb + 1) * 256)
                    four, part = divmod(u, 3)
                    if part < 2:
                        o = RING[:, i % 2, :].rearrange("k (h q) -> k h q", h=2)
                        pe.matmul(o, identb[:], mbM[:, q].unsqueeze(1).broadcast_to((KM, 2, 256)), start=True, stop=False)
                        for k in range(2):
                            h = 4 * four + 2 * part + k
                            last = pe.matmul(o[:, k, :], KA[:, h, 0:KM], QA[:, h, q], start=False, stop=(k == 1))
                    else:
                        pe.matmul(RING[:, i % 2, 0:256], ident4[:].rearrange("k j c -> k (j c)"), mbR[:, q],
                                  start=True, stop=False)
                        for j in range(4):
                            last = pe.matmul(RING[32 * j:32 * j + KT, i % 2, 0:256], KA[:, 4 * four + j, KM:S2],
                                             QA[:, 4 * four + j, q], start=False, stop=True)
                    last.then_inc(st_ready, 1)
                    if u >= 1:
                        pv(b, hb, u - 1)
                elif kind == "A4a":
                    pv(b, piece[2], SU - 1)
                elif kind == "A4b":
                    pe.wait_ge(ot_ready, b * 2 + piece[2] + 1)
                    take_misc(m)
                    for t in range(2):
                        for g in range(2):
                            last = pe.transpose(MISC[:, (t * 2 + g) * VW:(t * 2 + g + 1) * VW],
                                                OT[:, g, t * 128:(t + 1) * 128], ident[0:VW, 0:VW])
                    last.then_inc(misc_ready, 1)
                elif kind == "A5a":
                    pe.wait_ge(ctx_ready, 2 * (b + 1))
                    transposes(m, cx)
                elif kind == "A5b":
                    rows_out(m, cxT, Wo[:], brow[:, 1, :])
                elif kind == "F0a":
                    if b == 0:
                        pe.wait_ge(ld_moe, 16 * LD_MOE)
                    pe.wait_ge(xn_ready, norm_at["F0a", b] + 1)
                    transposes(m, xn)
                elif kind == "F0b":
                    take_misc(m)
                    pe.matmul(MISC[0:32, :], Wr1[:], xnTf[:, b % 2], start=True, stop=True).then_inc(misc_ready, 1)
                elif kind == "F0c":
                    take_misc(m)
                    for t in range(NT):
                        last = pe.matmul(MISC[:, t * 8:(t + 1) * 8], r1[:, t * 128:(t + 1) * 128], Wr2[:],
                                         start=True, stop=True)
                    last.then_inc(misc_ready, 1)
                elif kind == "F0d":
                    pe.wait_ge(w9_ready, b + 1)
                    transposes(m, W9[:, b % 2], NE)
                elif kind == "F0e":
                    n = b * (NE + 1)
                    pe.wait_ge(misc_free, misc_at["F0d", b] + 1)
                    pe.wait_ge(ks_ready, 1)
                    if b:
                        pe.wait_ge(down_free, n - 1)
                    for t in range(NT):
                        last = pe.matmul(DOWN[:, n % 2, t * 128:(t + 1) * 128], w9T[:, t * 128:(t + 1) * 128], B2[:],
                                         start=True, stop=True)
                    last.then_inc(down_ready, 1)
                elif kind == "F1":
                    e, c = piece[2:]
                    if e < NE:
                        i = (b * NE + e) * NC + c
                        if i == 0:
                            pe.wait_ge(t_read, 2 * B)
                        if i >= 2:
                            pe.wait_ge(h_ready, i - 1)
                        pe.matmul(UP[:, i % 2, :], W1[:, e, c * 128:(c + 1) * 128], xnTf[:, b % 2],
                                  start=True, stop=True).then_inc(up_ready, 1)
                    if e >= 1:
                        down(b, e - 1, c)
                elif kind == "G0a":
                    if b == 0:
                        pe.wait_ge(ld_l1, 16 * 5)
                    pe.wait_ge(xn_ready, norm_at["G0a", b] + 1)
                    transposes(m, xn)
                elif kind == "G0b":
                    take_misc(m)
                    pe.matmul(MISC[:], WqT[:], xnT[:], start=True, stop=True).then_inc(misc_ready, 1)
                    rows_out(m + 1, xnT, WqT[:], brow[:, 4, :])
                elif kind == "G0c":
                    rows_out(m, QpT, WoffT[:], boffr[:], HN)
                elif kind == "G0d":
                    pe.wait_ge(pos_ready, b + 1)
                    transposes(m, pos[:, 1], HN)
                elif kind == "G1":
                    h = piece[2]
                    idx = b * H + h
                    if h == 0:
                        pe.wait_ge(p_ready, before(piece, "A3"))
                    pe.wait_ge(oh_ready, idx + 1)
                    for tp in range(2):
                        i = idx * 2 + tp
                        if i >= 2:
                            pe.wait_ge(g_free, i - 1)
                        for t in range(2):
                            q = slice((2 * tp + t) * 128, (2 * tp + t + 1) * 128)
                            for n in range(NK):
                                o = RING[:, i % 2, t * 160:(t + 1) * 160].rearrange("p (k n c) -> p k n c", k=2, n=NK)[:, :, n, :]
                                for s in range(NS):
                                    pe.matmul(o, OH[:, idx % 2, n, q], T0[:, b, s, h, :].rearrange("p (k c) -> p k c", k=2),
                                              start=(s == 0), stop=False)
                                last = pe.matmul(o, OHR[:, idx % 2, n, q], TR[:, b, h, :].rearrange("p (k c) -> p k c", k=2),
                                                 start=False, stop=True)
                        last.then_inc(g_ready, 1)
                elif kind == "G3a":
                    pe.wait_ge(cx1_ready, b + 1)
                    transposes(m, cx)
                elif kind == "G3b":
                    rows_out(m, cxT, WoT[:], brow[:, 5, :])
                elif kind == "G3c":
                    pe.wait_ge(xn_ready, norm_at["G3c", b] + 1)
                    transposes(m, xn)
                elif kind == "G3d":
                    rows_out(m, xnT, Wsel[:], bsel[:])

        @block.vector
        def _(dve):
            done = [0]

            def step(ins):
                done[0] += 1
                ins.then_inc(dve_done, 1)
                dve.wait_ge(dve_done, done[0])

            def by_tile(a, n):
                return a.unsqueeze(2).broadcast_to((128, NT, n))

            def norm(b, key):
                n = norm_at[key]
                for t in range(NT):
                    last = dve.bn_stats(st[:, t, :], X[:, b, t, :])
                step(last)
                for t in range(NT):
                    last = dve.bn_aggr(mv[:, t, :], st[:, t, :])
                step(last)
                dve.tensor_scalar(ve[:], mv[:, :, 1], EPS, None, ALU.add).then_inc(var_ready, 1)
                dve.wait_ge(rstd_ready, n + 1)
                for t in range(NT):
                    last = dve.tensor_scalar(xn[:, t, :], X[:, b, t, :], mv[:, t, 0:1], rstd[:, t:t + 1],
                                             ALU.subtract, ALU.mult)
                last.then_inc(xn_ready, 1)

            def add_misc(use, b, gate):
                dve.wait_ge(misc_ready, use + 1)
                dve.wait_ge(gate_ready, 1)
                xb = X[:, b].rearrange("p t d -> p (t d)")
                dve.scalar_tensor_tensor(out=xb, in0=MISC[:], scalar=tg[:, gate:gate + 1], in1=xb,
                                         op0=ALU.mult, op1=ALU.add).then_inc(misc_free, 1)
                dve.wait_ge(misc_free, use + 1)

            dve.wait_ge(ld_const, 16 * 5)
            dve.tensor_copy(identb[:], ident)
            dve.tensor_copy(ident4[:], ident[0:KT, 0:32].unsqueeze(1).broadcast_to((KT, 4, 32)))
            step(dve.tensor_reduce(lg1[:, 0:1], lg[:, 0, :], AX.X, ALU.max))
            dve.tensor_scalar(lg[:, 2, :], lg[:, 0, :], lg1[:, 0:1], None, ALU.subtract).then_inc(lg_ready, 1)
            step(dve.tensor_scalar(kmf.rearrange("p b k -> p (b k)"), km, -1.0, 1.0, ALU.mult, ALU.add))
            step(dve.tensor_reduce(lens[:, 0, :], kmf, AX.X, ALU.add))
            step(dve.tensor_scalar(lens[:, 0, :], lens[:, 0, :], -1.0, None, ALU.add))
            step(dve.tensor_scalar(sgn[:], lens[:, 0, :], 0.0, None, ALU.is_ge))
            step(dve.tensor_scalar(sgn[:], sgn[:], 2.0, -1.0, ALU.mult, ALU.add))
            step(dve.tensor_tensor(lens[:, 0, :], lens[:, 0, :], sgn[:], ALU.mult))
            dve.tensor_scalar(lens[:, 1, :], lens[:, 0, :], -1.0, None, ALU.mult)
            step(dve.reciprocal(lens[:, 2, :], lens[:, 0, :]))
            dve.tensor_scalar(lens[:, 3, :], sgn[:], S2 / (S2 - 1.0), None, ALU.mult)
            step(dve.tensor_tensor(lens[:, 2, :], lens[:, 2, :], sgn[:], ALU.mult))
            def onehot(b, h):
                idx = b * H + h
                dve.wait_ge(jb_in[h % 2], 16 * (idx // 2 + 1))
                if idx >= 2:
                    dve.wait_ge(g_ready, 2 * (idx - 1))
                dve.tensor_scalar(OH[:, idx % 2], JB[:, h % 2], cst[:, C_K0:C_K0 + 1], None, ALU.is_equal)
                dve.tensor_scalar(OHR[:, idx % 2], JB[0:RR, h % 2], cst[0:RR, C_KR:C_KR + 1], None,
                                  ALU.is_equal).then_inc(oh_ready, 1)

            scf = sc.rearrange("p t (h n) -> p (t h) n", n=NK)

            def taps(a):
                return a.unsqueeze(2).broadcast_to((128, NT * H, NK))

            for piece in schedule:
                kind, b = piece[0], piece[1]
                m = misc_at[piece]
                if kind == "K":
                    dve.wait_ge(k_ready, 1)
                    for i in range(2):
                        last = dve.tensor_scalar(ksf[:, 2 * i * S2:2 * (i + 1) * S2], DOWN[:, i, 0:2 * S2], bcol[:, 1:2],
                                                 None, ALU.add)
                    step(last)
                    for s in range(NS - 1):
                        step(dve.tensor_copy(ks[:, s, :], ksf))
                        step(dve.tensor_tensor(ksf, ksf, ks[:, s, :], ALU.subtract))
                    dve.tensor_copy(ks[:, NS - 1, :], ksf).then_inc(ks_ready, 1)
                elif kind == "V":
                    dve.wait_ge(ld_ctx, 16 * 5)
                    for n in range(B):
                        for two in range(2):
                            last = dve.tensor_copy(ctxR[:, n, two], ctxP[:, n, R0 + two:R0 + two + 32].unsqueeze(1)
                                                   .broadcast_to((128, 4, 32)))
                    last.then_inc(cr_ready, 1)
                    dve.wait_ge(v_ready, 1)
                    dve.wait_ge(pre_pool, 2)
                    for n in range(2):
                        dve.tensor_copy(VC[:, 2 * n:2 * n + 2].rearrange("p b c e -> p (b c e)"), UP[:, n, :])
                    dve.tensor_copy(VM[:, VW - DK - 1:].rearrange("p (h w) -> p h w", h=H)[:, :, DK], one_col)
                    for j in range(4):
                        for rp in range(2):
                            at = rp * (VW + 4 * (DK + 1)) + j * (DK + 1) + DK
                            last = dve.tensor_copy(VT[32 * j:32 * j + 32, :, at],
                                                   cst[32 * j:32 * j + 32, C_TAIL:C_TAIL + 1].broadcast_to((32, 2)))
                    last.then_inc(v_read, 1)
                elif kind == "T":
                    ch = piece[2]
                    i = 2 * b + ch
                    dve.wait_ge(t_ready, i + 1)
                    n = R0 if ch == 0 else RR
                    ps = UP[0:n, ch, :]

                    def heads(a):
                        return a.rearrange("p (w h d) -> p h w d", w=4, h=H)

                    def entry(a):
                        return a.rearrange("p h (w d) -> p h w d", w=4)

                    if ch == 0:
                        step(dve.tensor_copy(entry(T0[:, b, 0]), heads(ps)))
                        step(dve.tensor_tensor(heads(tabf), heads(ps), entry(T0[:, b, 0]), ALU.subtract))
                        step(dve.tensor_copy(entry(T0[:, b, 1]), heads(tabf)))
                        dve.tensor_tensor(entry(T0[:, b, 2]), heads(tabf), entry(T0[:, b, 1]),
                                          ALU.subtract).then_inc(t_read, 1)
                    else:
                        dve.tensor_copy(entry(TR[0:32, b]), heads(UP[0:32, ch, :]))
                        step(dve.tensor_copy(tabb[0:n], ps))
                        step(dve.tensor_tensor(tabf[0:n], ps, tabb[0:n], ALU.subtract))
                        dve.tensor_copy(entry(TR[32:64, b]), heads(tabf[32:64]))
                        step(dve.tensor_copy(tabb[0:n], tabf[0:n]))
                        dve.tensor_tensor(entry(TR[64:96, b]), heads(tabf[64:96]), heads(tabb[64:96]),
                                          ALU.subtract).then_inc(t_read, 1)
                    dve.wait_ge(t_read, i + 1)
                elif kind == "W":
                    dve.wait_ge(noise_ready, 1)
                    dve.wait_ge(ld_tab, 16 * 4)
                    step(dve.tensor_scalar(lg[:, 6, :], lg[:, 2, :], lg1[:, 2:3], None, ALU.subtract))
                    step(dve.tensor_tensor(lg[:, 6, :], lg[:, 6, :], lg[:, 5, :], ALU.subtract))
                    step(dve.tensor_reduce(lg1[:, 0:1], lg[:, 6, :], AX.X, ALU.max))
                    step(dve.tensor_scalar(lg[:, 7, :], lg[:, 6, :], lg1[:, 0:1], None, ALU.is_equal))
                    step(dve.tensor_tensor(lg[:, 6, :], lg[:, 7, :], cst[:, C_RANK:C_RANK + 8], ALU.mult))
                    step(dve.tensor_reduce(lg1[:, 0:1], lg[:, 6, :], AX.X, ALU.max))
                    step(dve.tensor_scalar(lg[:, 7, :], lg[:, 6, :], lg1[:, 0:1], None, ALU.is_equal))
                    dve.tensor_scalar(Wsel[:], W8[:, 0, :], lg[:, 7, 0:1], None, ALU.mult)
                    step(dve.tensor_scalar(bsel[:], b8[:, 0, :], lg[0:1, 7, 0:1], None, ALU.mult))
                    for o in range(1, 8):
                        dve.scalar_tensor_tensor(out=Wsel[:], in0=W8[:, o, :], scalar=lg[:, 7, o:o + 1], in1=Wsel[:],
                                                 op0=ALU.mult, op1=ALU.add)
                        step(dve.scalar_tensor_tensor(out=bsel[:], in0=b8[:, o, :], scalar=lg[0:1, 7, o:o + 1], in1=bsel[:],
                                                      op0=ALU.mult, op1=ALU.add))
                elif kind in ("A0a", "F0a", "G0a", "G3c"):
                    if kind == "A0a":
                        if b == 0:
                            dve.wait_ge(ld_q, 16 * 4)
                        else:
                            dve.wait_ge(ld_x, 16 * (B - 1))
                    norm(b, (kind, b))
                elif kind == "A0b":
                    if b:
                        dve.wait_ge(st_ready, b * 2 * SU)
                    dve.wait_ge(ld_mask, 48 * (b + 1))
                    dve.tensor_scalar(mb[:], mraw[:], MASKED, None, ALU.mult)
                    dve.tensor_scalar(mbM[:], mrawM[:], MASKED, None, ALU.mult)
                    dve.tensor_scalar(mbR[:], mrawR[:], MASKED, None, ALU.mult).then_inc(mask_ready, 1)
                    if b:
                        dve.wait_ge(pv_done, b * 2 * SU)
                    dve.wait_ge(v_read, 1)
                    dve.tensor_copy(VM[:, VW - DK - 1:].rearrange("p (h w) -> p h w", h=H)[:, :, 0:DK],
                                    VC[:, b, 0, :].rearrange("p (h d) -> p h d", d=DK))
                    for j in range(4):
                        for rp in range(2):
                            at = rp * (VW + 4 * (DK + 1)) + j * (DK + 1)
                            tail = VC[32 * j:32 * j + 32, b, 1, :].rearrange("p (r h d) -> p r h d", r=2, d=DK)
                            last = dve.tensor_copy(VT[32 * j:32 * j + 32, :, at:at + DK], tail[:, :, 4 * rp + j, :])
                    last.then_inc(vm_ready, 1)
                    dve.wait_ge(misc_ready, m + 1)
                    dve.tensor_scalar(qf, MISC[:], bcol[:, 0:1], 1.0 / math.sqrt(DK), ALU.add,
                                      ALU.mult).then_inc(misc_free, 1)
                    dve.wait_ge(misc_free, m + 1)
                    if b:
                        dve.wait_ge(qs_out, 16 * b)
                    for s in range(NS - 1):
                        step(dve.tensor_copy(qs[:, s, :], qf))
                        step(dve.tensor_tensor(qf, qf, qs[:, s, :], ALU.subtract))
                    dve.tensor_copy(qs[:, NS - 1, :], qf).then_inc(qs_ready, 1)
                elif kind == "A1":
                    t, h = piece[2], 0
                    for g, n in enumerate(HG):
                        i = (b * NT + t) * len(HG) + g
                        dve.wait_ge(sa_ready, i + 1)
                        dve.tensor_reduce(nmax[:, t, h:h + n], RING[:, i % 2, 0:n * S2].rearrange("p (h k) -> p h k", h=n),
                                          AX.X, ALU.max, negate=True).then_inc(sa_free, 1)
                        h += n
                elif kind == "A2":
                    dve.wait_ge(misc_ready, m + 1)
                    dve.tensor_copy(nmr[:], MISC[0:NT * H, 0:128]).then_inc(misc_free, 1)
                    dve.wait_ge(misc_free, m + 1)
                    if b:
                        dve.wait_ge(nms_out, 16 * b)
                    for s in range(NS - 1):
                        step(dve.tensor_copy(nms[:, s, :], nmr[:]))
                        step(dve.tensor_tensor(nmr[:], nmr[:], nms[:, s, :], ALU.subtract))
                    dve.tensor_copy(nms[:, NS - 1, :], nmr[:]).then_inc(nms_ready, 1)
                elif kind == "A4b":
                    hb = piece[2]
                    dve.wait_ge(misc_ready, m + 1)
                    sums = MISC[:, 0:2 * H * 9].rearrange("p (t h d) -> p t h d", t=2, h=H)
                    step(dve.reciprocal(rden[:], sums[:, :, :, DK]))
                    step(dve.tensor_tensor(cx[:, 2 * hb:2 * hb + 2, :].rearrange("p t (h d) -> p t h d", d=DK),
                                           sums[:, :, :, 0:DK], rden[:].unsqueeze(3).broadcast_to((128, 2, H, DK)),
                                           ALU.mult))
                    dve.nop().then_inc(misc_free, 1)
                    dve.nop().then_inc(ctx_ready, 1)
                elif kind == "A5b":
                    add_misc(m, b, 0)
                elif kind == "F0b":
                    if b == 0:
                        dve.wait_ge(ld_moe, 16 * LD_MOE)
                    dve.wait_ge(misc_ready, m + 1)
                    dve.tensor_scalar(r1[0:32, :], MISC[0:32, :], br1[:, 0:1], 0.0, ALU.add, ALU.max).then_inc(misc_free, 1)
                elif kind == "F0c":
                    dve.wait_ge(misc_ready, m + 1)
                    lgt = MISC[:, 0:NT * 8].rearrange("p (t e) -> p t e", t=NT)
                    rank = cst[:, C_RANK:C_RANK + 8].unsqueeze(1).broadcast_to((128, NT, 8))
                    step(dve.tensor_reduce(gs[:, 0], lgt, AX.X, ALU.max))
                    dve.tensor_tensor(gt[:, 0], lgt, by_tile(gs[:, 0], 8), ALU.subtract).then_inc(misc_free, 1)
                    dve.wait_ge(ex_out, 2 * b + 1)
                    step(dve.tensor_reduce(gs[:, 1], gt[:, 1], AX.X, ALU.add))
                    step(dve.reciprocal(gs[:, 2], gs[:, 1]))
                    step(dve.tensor_tensor(gt[:, 2], gt[:, 1], by_tile(gs[:, 2], 8), ALU.mult))

                    def greatest(g, top, eq, rk, at, first):
                        step(dve.tensor_reduce(gs[:, top], gt[:, g], AX.X, ALU.max))
                        step(dve.tensor_tensor(gt[:, eq], gt[:, g], by_tile(gs[:, top], 8), ALU.is_equal))
                        step(dve.tensor_tensor(gt[:, rk], gt[:, eq], rank, ALU.mult))
                        step(dve.tensor_reduce(gs[:, at], gt[:, rk], AX.X, ALU.max))
                        step(dve.tensor_tensor(gt[:, first], gt[:, rk], by_tile(gs[:, at], 8), ALU.is_equal))

                    greatest(2, 3, 3, 3, 4, 5)
                    step(dve.scalar_tensor_tensor(out=gt[:, 6], in0=gt[:, 5], scalar=-4.0, in1=gt[:, 2],
                                                  op0=ALU.mult, op1=ALU.add))
                    greatest(6, 7, 7, 7, 8, 9)
                    dve.tensor_tensor(gs[:, 5], gs[:, 7], gs[:, 3], ALU.subtract).then_inc(d_ready, 1)
                    dve.wait_ge(ex_out, 2 * b + 2)
                    step(dve.tensor_scalar(gs[:, 9], gs[:, 6], 1.0, None, ALU.add))
                    step(dve.reciprocal(gs[:, 1], gs[:, 9]))
                    step(dve.tensor_tensor(gs[:, 2], gs[:, 6], gs[:, 1], ALU.mult))
                    dve.tensor_tensor(gt[:, 8], gt[:, 5], by_tile(gs[:, 1], 8), ALU.mult)
                    step(dve.tensor_tensor(gt[:, 4], gt[:, 9], by_tile(gs[:, 2], 8), ALU.mult))
                    dve.tensor_tensor(W9[:, b % 2, :, 0:8], gt[:, 8], gt[:, 4], ALU.add).then_inc(w9_ready, 1)
                elif kind == "F0e":
                    n = b * (NE + 1)
                    dve.wait_ge(down_ready, n + 1)
                    dve.tensor_copy(acc[:].rearrange("p t d -> p (t d)"), DOWN[:, n % 2, :]).then_inc(down_free, 1)
                elif kind == "F1" and piece[2] >= 1 and piece[3] == NC - 1:
                    e = piece[2] - 1
                    n = b * (NE + 1) + 1 + e
                    dve.wait_ge(down_ready, n + 1)
                    dve.wait_ge(down_free, n)
                    for t in range(NT):
                        last = dve.scalar_tensor_tensor(out=acc[:, t, :], in0=DOWN[:, n % 2, t * 128:(t + 1) * 128],
                                                        scalar=W9[:, b % 2, t, e:e + 1], in1=acc[:, t, :],
                                                        op0=ALU.mult, op1=ALU.add)
                    last.then_inc(down_free, 1)
                elif kind == "F2":
                    dve.wait_ge(down_free, (b + 1) * (NE + 1))
                    step(dve.scalar_tensor_tensor(out=X[:, b], in0=acc[:], scalar=tg[:, 2:3], in1=X[:, b],
                                                  op0=ALU.mult, op1=ALU.add))
                elif kind == "G0c":
                    p = [pos[:, i] for i in range(5)]
                    dve.wait_ge(misc_ready, m + 1)
                    dve.tensor_tensor(p[0], MISC[:, 0:NT * HN].rearrange("p (t n) -> p t n", t=NT),
                                      cst[:, C_REF:C_REF + HN].unsqueeze(1).broadcast_to((128, NT, HN)),
                                      ALU.add).then_inc(misc_free, 1)
                    dve.wait_ge(misc_free, m + 1)
                    step(dve.tensor_tensor(p[1], p[0], by_tile(cst[:, C_LOC:C_LOC + NT], HN), ALU.add))
                    size, less, per, back = (lens[:, i, b:b + 1] for i in range(4))
                    dve.tensor_scalar(p[0], p[1], sgn[:, b:b + 1], None, ALU.mult)
                    step(dve.tensor_scalar(p[2], p[1], per, -0.5, ALU.mult, ALU.add))
                    step(dve.tensor_scalar(p[2], p[2], MAGIC, None, ALU.add))
                    step(dve.tensor_scalar(p[2], p[2], -MAGIC, less, ALU.add, ALU.mult))
                    step(dve.tensor_tensor(p[0], p[0], p[2], ALU.add))
                    step(dve.tensor_scalar(p[1], p[0], size, less, ALU.is_ge, ALU.mult))
                    step(dve.tensor_tensor(p[0], p[0], p[1], ALU.add))
                    step(dve.tensor_scalar(p[1], p[0], 0.0, size, ALU.is_lt, ALU.mult))
                    step(dve.tensor_tensor(p[0], p[0], p[1], ALU.add))
                    step(dve.tensor_scalar(p[2], p[0], back, -0.5, ALU.mult, ALU.add))
                    step(dve.tensor_scalar(p[3], p[2], -0.5, MAGIC, ALU.add, ALU.add))
                    step(dve.tensor_scalar(p[3], p[3], -MAGIC, None, ALU.add))
                    dve.tensor_scalar(p[1], p[3], 1.0, None, ALU.add).then_inc(pos_ready, 1)
                    step(dve.tensor_tensor(p[4], p[2], p[3], ALU.subtract))
                    dve.tensor_scalar(wts[:, :, :, 1], p[4], 0.5, None, ALU.mult)
                    step(dve.tensor_scalar(wts[:, :, :, 0], p[4], -0.5, 0.5, ALU.mult, ALU.add))
                elif kind == "G0e":
                    onehot(b, 0)
                elif kind == "G1":
                    h = piece[2]
                    if h + 1 < H:
                        onehot(b, h + 1)
                    if h == 0:
                        dve.wait_ge(misc_free, misc_at["G0b", b] + 2)
                    idx = b * H + h
                    dve.wait_ge(g_free, 2 * (idx + 1))
                    dve.tensor_tensor(prod[:], GS[:, h % 2].rearrange("p t (n d) -> p t n d", d=DK),
                                      Qp[:, :, h * DK:(h + 1) * DK].unsqueeze(2).broadcast_to((128, NT, 10, DK)),
                                      ALU.mult).then_inc(gk_used, 1)
                    dve.wait_ge(gk_used, idx + 1)
                    step(dve.tensor_reduce(dots[:, :, h, :], prod[:], AX.X, ALU.add))
                elif kind == "G2a":
                    wf = wts[:].rearrange("p t n w -> p (t n w)")
                    df = dots[:].rearrange("p t h w -> p (t h w)")
                    step(dve.tensor_tensor(df, df, wf, ALU.mult))
                    step(dve.tensor_reduce(sc.rearrange("p t n -> p (t n)"), df.rearrange("p (n w) -> p n w", w=2),
                                           AX.X, ALU.add))
                    step(dve.tensor_reduce(sm[:, 0], scf, AX.X, ALU.max))
                    dve.tensor_tensor(scf, scf, taps(sm[:, 0]), ALU.subtract).then_inc(z_ready, 1)
                elif kind == "G2b":
                    dve.wait_ge(e_ready, b + 1)
                    step(dve.tensor_reduce(sm[:, 1], scf, AX.X, ALU.add))
                    step(dve.reciprocal(sm[:, 2], sm[:, 1]))
                    step(dve.tensor_tensor(scf, scf, taps(sm[:, 2]), ALU.mult))
                    step(dve.tensor_tensor(aw, wts[:], sc.unsqueeze(3).broadcast_to((128, NT, HN, 2)), ALU.mult))
                    for t in range(NT):
                        gv = GV[:, :, t, :].rearrange("p h (m d) -> p h m d", d=DK)
                        last = dve.tensor_tensor(gv, gv, aw[:, t].rearrange("p (h n) w -> p h (n w)", h=H).unsqueeze(3)
                                                 .broadcast_to((128, H, 10, DK)), ALU.mult)
                    step(last)
                    for t in range(NT):
                        last = dve.tensor_reduce(cx[:, t].rearrange("p (h d) -> p h d", d=DK),
                                                 GV[:, :, t, :].rearrange("p h (m d) -> p h d m", d=DK), AX.X, ALU.add)
                    last.then_inc(cx1_ready, 1)
                elif kind == "G3b":
                    add_misc(m, b, 1)
                elif kind == "G3d":
                    add_misc(m, b, 3)
                    dve.nop().then_inc(x_done, 1)


def attention(b):
    out = [(("A0a", b), 3), (("A0b", b), 8)] + [(("A1", b, t), 1.5) for t in range(NT)] + [(("A2", b), 6)]
    for hb in range(2):
        out += [(("A3", b, hb, u), 0) for u in range(SU)] + [(("A4a", b, hb), 1), (("A4b", b, hb), 0)]
    return out + [(("A5a", b), 1.5), (("A5b", b), 2)]


def router(b):
    return [(("F0a", b), 3), (("F0b", b), 2), (("F0c", b), 4), (("F0d", b), 1)]


def experts(b):
    return [(("F0e", b), 0.1)] + [(("F1", b, e, c), 1.7) for e in range(NE + 1) for c in range(NC)] + [(("F2", b), 0.5)]


def sampling(b):
    return ([(("G0a", b), 3), (("G0b", b), 2.5), (("G0c", b), 6), (("G0d", b), 5), (("G0e", b), 1)]
            + [(("G1", b, h), 0.6) for h in range(H)]
            + [(("G2a", b), 2), (("G2b", b), 8), (("G3a", b), 1.5), (("G3b", b), 2), (("G3c", b), 2), (("G3d", b), 1)])


def spread(*lists):
    timed = []
    for n, pieces in enumerate(lists):
        total = sum(w for _, w in pieces) or 1
        at = 0
        for p, w in pieces:
            timed.append((at / total, n, len(timed), p))
            at += w
    return [p for *_, p in sorted(timed)]


def order():
    tables = [(("V", 0), 1)] + [(("T", b, ch), 1) for b in range(B) for ch in range(2)] + [(("W", 0), 1)]
    schedule = [("K", 0)] + spread(attention(0) + router(0), tables)
    for b in range(B):
        beside = []
        if b >= 1:
            beside += sampling(b - 1)
        if b + 1 < B:
            beside += attention(b + 1) + router(b + 1)
        schedule += spread(experts(b), beside)
    return schedule + [p for p, _ in sampling(B - 1)]


def kernel(**inputs):
    import numpy as np
    import concourse.bacc as bacc
    from concourse.bass_utils import run_bass_kernel_spmd

    a = {k: np.ascontiguousarray(v) for k, v in inputs.items()}
    row = np.arange(128)
    consts = np.zeros((128, C_N), np.float32)
    consts[:, C_ID:C_ID + 128] = np.eye(128)
    consts[:, C_K0] = row
    consts[:, C_KR] = R0 + row % 32
    consts[:, C_LOC:C_LOC + NT] = row[:, None] + 128 * np.arange(NT)
    consts[:, C_REF:C_REF + HN] = np.tile(np.arange(NK) + (-NK // 2), H)
    consts[:, C_TAIL] = row % 32 < KT
    consts[:, C_RANK:C_RANK + 8] = 8 - np.arange(8)
    mask = a["mask_BxSxS2_bf0"]
    b1 = np.concatenate([a["L0_ffn_be1"], a["L0_ffn_bs1"][None]])
    laid_out = {
        "x": a["x"],
        "ctxT": a["ctx_1024"].transpose(2, 0, 1),
        "mask": mask,
        "maskT": mask.transpose(0, 2, 1),
        "kmask": a["mask_BxS2_if0"],
        "gates": np.concatenate([a["g_xattn"], a["g_ffn"]]),
        "consts": consts,
        "wq": a["L0_xattn_Wq"], "wk": a["L0_xattn_Wk"], "wv": a["L0_xattn_Wv"], "wo": a["L0_xattn_Wo"],
        "bq_col": a["L0_xattn_bq"][:, None], "bk_col": a["L0_xattn_bk"][:, None],
        "rows": np.stack([a["L0_xattn_bv"], a["L0_xattn_bo"], a["L1_xattn_bk"], a["L1_xattn_bv"],
                          a["L1_xattn_bq"], a["L1_xattn_bo"]])[None],
        "wr1": a["L0_ffn_Wr1"], "br1_col": a["L0_ffn_br1"][:, None],
        "wr2": a["L0_ffn_Wr2"], "br2": a["L0_ffn_br2"][None],
        "w1": np.concatenate([a["L0_ffn_We1"], a["L0_ffn_Ws1"][None]]),
        "b1_cols": b1.reshape(NE, NC, 128).transpose(2, 0, 1),
        "w2": np.concatenate([a["L0_ffn_We2"], a["L0_ffn_Ws2"][None]]),
        "b2": np.concatenate([a["L0_ffn_be2"], a["L0_ffn_bs2"][None]]),
        "wkT": a["L1_xattn_Wk"].T, "wvT": a["L1_xattn_Wv"].T, "wqT": a["L1_xattn_Wq"].T,
        "woffT": a["L1_xattn_Woff"].T, "woT": a["L1_xattn_Wo"].T,
        "bq1_col": a["L1_xattn_bq"][:, None], "boff": a["L1_xattn_boff"][None],
        "w8": a["L1_ffn_W"], "b8": a["L1_ffn_b"][None], "logits": a["L1_ffn_logits"], "u": a["L1_ffn_u"],
    }
    nc = bacc.Bacc("TRN2", target_bir_lowering=False, num_devices=1, dynamic_dma_scratch_size=1024)
    arrays, args = {}, []
    for name, v in laid_out.items():
        v = np.ascontiguousarray(v)
        arrays[f"in_{name}"] = v
        args.append(nc.dram_tensor(f"in_{name}", v.shape, mybir.dt.from_np(v.dtype), kind="ExternalInput").ap())
    args.append(nc.dram_tensor("out_x", (B, S, D), F32, kind="ExternalOutput").ap())
    build(nc, *args)
    r = run_bass_kernel_spmd(nc, [arrays], core_ids=[0])
    return r.results[0]["out_x"]
```

```python
import concourse.bass as bass
from concourse import mybir
from contextlib import ExitStack
import math

F32 = mybir.dt.float32
BF16 = mybir.dt.bfloat16
F16 = mybir.dt.float16
ALU = mybir.AluOpType
ACT = mybir.ActivationFunctionType
AX = mybir.AxisListType

B, S, D = 4, 512, 128
S2 = 154
H, DK = 16, 8
NT = S // 128
KM, KT = 128, S2 - 128
SU = 12
VW = 8 * (DK + 1)
NE, NC = 9, 4
NK = 5
HN = H * NK
NS = 3
SLOT_Q = (0, 0, 0, 1, 1, 2)
SLOT_K = (0, 1, 2, 0, 1, 0)
QR = len(SLOT_Q) * DK
QM = QR + NS
HG = (3, 3, 3, 3, 2, 2)
R0 = 128
RR = NS * 32
W1SCALE = 64.0
MASKED = -1e18
MAGIC = 12582912.0
EPS = 1e-5
HS = 8
LD_MOE = 6 + NE // 3
FB = 2
C_ID, C_K0, C_KR, C_LOC, C_REF, C_RANK, C_TAIL, C_N = 0, 128, 129, 130, 134, 214, 222, 223

ORDER = """
    K.0 A0a.0 V.0 S.0 S.1 A0b.0 T.0.0-1 A1.0.0 S.2 A1.0.1-3 A2.0 T.1.0 A3.0.0.0-3 T.1.1 A3.0.0.4-7 T.2.0
    A3.0.0.8-9 T.2.1 A3.0.0.10-11 A4a.0.0 A4b.0.0 A3.0.1.0-1 T.3.0 W.0 A3.0.1.2-8 T.3.1 A3.0.1.9-11 A4a.0.1
    A4b.0.1 A5a.0 A5b.0 F0a.0 F0b.0 F1.0.0.0-3 F0c.0 F0g.0 F0h.0 F0d.0 F1.0.1.0-2 A0a.1 F1.0.1.3 A0b.1
    F1.0.2.0-3 F0e.0 F1.0.3.0-3 F1.0.4.0 A1.1.0-2 F1.0.4.1 A1.1.3 F1.0.4.2-3 A2.1 F1.0.5.0-3 A3.1.0.0-11 A4a.1.0
    F1.0.6.0 A4b.1.0 F1.0.6.1 A3.1.1.0-1 F1.0.6.2 A3.1.1.2-5 F1.0.6.3 F1.0.7.0 A3.1.1.6-8 F1.0.7.1-2 A3.1.1.9-11
    A4a.1.1 F1.0.7.3 A4b.1.1 A5a.1 F1.0.8.0-1 A5b.1 F1.0.8.2-3 F0a.1 F1.0.9.0-1 F0b.1 F1.0.9.2-3 F2.0 F1.1.0.0-3
    F0c.1 F0g.1 F0h.1 F1.1.1.0-1 F0d.1 F1.1.1.2 G0a.0 F1.1.1.3 A0a.2 F1.1.2.0-1 A0b.2 F1.1.2.2-3 F0e.1 G0b.0
    F1.1.3.0 G0c.0 G0d.0 G0e.0 F1.1.3.1-3 F1.1.4.0-3 G1.0.0-5 F1.1.5.0 G1.0.6 F1.1.5.1 G1.0.7 F1.1.5.2 G1.0.8-15
    G2a.0 F1.1.5.3 F1.1.6.0-1 A1.2.0-3 A2.2 G2b.0 G2c.0.0 F1.1.6.2-3 F1.1.7.0-1 G2c.0.1-2 F1.1.7.2 G2c.0.3
    A3.2.0.0-11 A4a.2.0 A4b.2.0 A3.2.1.0-5 F1.1.7.3 F1.1.8.0 G3a.0 G3b.0 A3.2.1.6-11 A4a.2.1 G3c.0 A4b.2.1
    F1.1.8.1 A5a.2 A5b.2 F1.1.8.2 G3d.0 F1.1.8.3 F1.1.9.0-3 F0a.2 F0b.2 F0c.2 F2.1 F1.2.0.0 F0g.2 F1.2.0.1-2
    F0h.2 F1.2.0.3 F0d.2 G0a.1 F1.2.1.0 A0a.3 A0b.3 G0b.1 G0c.1 F1.2.1.1-3 F1.2.2.0-1 G0d.1 F1.2.2.2-3 F0e.2
    F1.2.3.0-3 G0e.1 F1.2.4.0 G1.1.0-1 F1.2.4.1 G1.1.2-14 F1.2.4.2 G1.1.15 F1.2.4.3 F1.2.5.0 A1.3.0 F1.2.5.1-2
    A1.3.1-2 F1.2.5.3 A1.3.3 G2a.1 F1.2.6.0-1 A2.3 G2b.1 G2c.1.0 F1.2.6.2-3 F1.2.7.0-2 A3.3.0.0 G2c.1.1-2
    A3.3.0.1-2 F1.2.7.3 A3.3.0.3-6 F1.2.8.0-3 F1.2.9.0 A3.3.0.7-10 G2c.1.3 G3a.1 A3.3.0.11 A4a.3.0 A4b.3.0
    A3.3.1.0-1 G3b.1 A3.3.1.2-10 G3c.1 A3.3.1.11 G3d.1 A4a.3.1 A4b.3.1 A5a.3 A5b.3 F1.2.9.1-3 F0a.3 F2.2 G0a.2
    F0b.3 F0c.3 F1.3.0.0-1 F0g.3 G0b.2 F1.3.0.2-3 G0c.2 F0h.3 F1.3.1.0-3 G0d.2 F1.3.2.0-1 F0d.3 F1.3.2.2-3 F0e.3
    F1.3.3.0-1 G0e.2 F1.3.3.2 G1.2.0 F1.3.3.3 G1.2.1-2 F1.3.4.0-2 G1.2.3-9 F1.3.4.3 G1.2.10 F1.3.5.0-2
    G1.2.11-12 F1.3.5.3 F1.3.6.0-3 F1.3.7.0-3 F1.3.8.0-3 F1.3.9.0-3 F2.3 G0a.3 G1.2.13 G0b.3 G1.2.14 G0c.3
    G1.2.15 G2a.2 G2b.2 G0d.3 G2c.2.0-3 G0e.3 G1.3.0-2 G3a.2 G1.3.3 G3b.2 G1.3.4-5 G3c.2 G1.3.6-7 G3d.2
    G1.3.8-15 G2a.3 G2b.3 G2c.3.0-3 G3a.3 G3b.3 G3c.3 G3d.3
"""


def build(nc, x, ctxT, mask, maskT, kmask, gates, consts, wq, wk, wv, wo, bq_col, bk_col, rows,
          wr1, br1_col, wr2, br2, w1, b1_cols, w2, b2, wkT, wvT, wqT, woffT, woT, bq1_col, boff,
          w8, b8_src, logits, u, out):
    ctx = ExitStack()
    dq = nc.dram_tensor("scratch_q_parts", [B, NS, 128, S], BF16, kind="Internal").ap()
    dk = nc.dram_tensor("scratch_k_parts", [NS, 128, B * S2], BF16, kind="Internal").ap()
    dm = nc.dram_tensor("scratch_max_parts", [B, NT, H, NS, 128], BF16, kind="Internal").ap()
    dj = nc.dram_tensor("scratch_positions", [B, HN, S], BF16, kind="Internal").ap()

    with ctx:
        def sb(name, shape, dt=F32):
            return ctx.enter_context(nc.sbuf_tensor(name, shape, dt))

        def pb(name, shape):
            return ctx.enter_context(nc.psum_tensor(name, shape, F32))

        def sem(name):
            return ctx.enter_context(nc.semaphore(name))

        X = sb("X", [128, B, NT, D])
        cst = sb("cst", [128, C_N])
        ident = cst[:, C_ID:C_ID + 128]
        identb = sb("identb", [128, 128], BF16)
        ones = sb("ones", [1, 128])
        Wq, Wk, Wv, Wo = (sb(n, [128, 128]) for n in ("Wq", "Wk", "Wv", "Wo"))
        WkT, WvT, WqT, WoT = (sb(n, [128, 128]) for n in ("WkT", "WvT", "WqT", "WoT"))
        WoffT = sb("WoffT", [128, HN])
        brow = sb("brow", [RR, 6, 128])
        bcol = sb("bcol", [128, 3])
        boffr = sb("boffr", [RR, HN])
        bparts = sb("bparts", [RR, 4 * 128 + HN], BF16)
        pick = sb("pick", [RR, 128], BF16)
        b_out, b_q1, b_out1, b_sel = (bparts[:, i * 128:(i + 1) * 128] for i in range(4))
        b_off = bparts[:, 4 * 128:]
        Wr1 = sb("Wr1", [128, 32])
        br1 = sb("br1", [32, 1])
        Wr2 = sb("Wr2", [33, 8])
        W1 = sb("W1", [128, 2, NE, NC * 128], F16)
        b1 = sb("b1", [128, NE, NC])
        W2 = sb("W2", [128, NE, NC, D])
        B2 = sb("B2", [NE, D])
        Wsel = sb("Wsel", [128, 128])
        tg = sb("tg", [128, 4])
        lens = sb("lens", [128, 4, B])
        sgn = sb("sgn", [128, B])
        KA0 = sb("KA0", [QM, H, S2], BF16)
        VC = sb("VC", [128, B, 2, 128])
        VM = sb("VM", [128, VW - DK - 1 + H * VW])
        VT = sb("VT", [128, 2, 2 * VW])
        TAB = sb("TAB", [128, B, 2, 2, H, 32], F16)
        mraw = sb("mraw", [128, NT, S2], mybir.dt.uint8)
        mrawM = sb("mrawM", [KM, S], mybir.dt.uint8)
        mrawR = sb("mrawR", [KT, S], mybir.dt.uint8)
        mb0 = sb("mb0", [128, NT, S2], BF16)
        mbM0 = sb("mbM0", [KM, S], BF16)
        mbR0 = sb("mbR0", [KT, S], BF16)
        ident4 = sb("ident4", [KT, 4, 32], BF16)
        QAf = sb("QAf", [128, H * S // 2])
        qs = sb("qs", [128, NS, S], BF16)
        nmax = sb("nmax", [128, NT, H])
        PT = sb("PT", [128, 2, 2, 256])
        OT = sb("OT", [VW, 2, 256])
        rden = sb("rden", [128, 2, H])
        cx = sb("cx", [128, NT, D])
        cxf = cx[:].rearrange("p t d -> p (t d)")
        nmr = cxf[0:NT * H, 0:128]
        nms = cxf[0:NT * H, 128:128 + NS * 64].bitcast(BF16).rearrange("p (s q) -> p s q", s=NS)
        xn = sb("xn", [128, NT, D])
        qf = xn[:].rearrange("p t d -> p (t d)")
        st = sb("st", [128, NT, 6])
        mv = sb("mv", [128, NT, 2])
        ve = sb("ve", [128, NT])
        rstd = sb("rstd", [128, NT])
        mhalf = sb("mhalf", [128, NT])
        one_col = sb("one_col", [128, H])
        xnT = sb("xnT", [128, S])
        cxT = xnT
        xnTf = sb("xnTf", [128, 2, 2, S], F16)
        r1 = sb("r1", [33, S])
        gt = sb("gt", [128, 10, NT, 8])
        gs = sb("gs", [128, 10, NT])
        W9 = sb("W9", [128, 2, NT, NE])
        w9T = sb("w9T", [NE, S])
        hT = sb("hT", [128, HS, S])
        acc = sb("acc", [128, NT, D])
        QpT = sb("QpT", [128, S])
        Qp = sb("Qp", [128, NT, D])
        pos = sb("pos", [128, 5, NT, HN])
        wts = sb("wts", [128, NT, HN, 2])
        jT = sb("jT", [HN, S], BF16)
        JB = sb("JB", [128, 2, NK, S], BF16)
        OH2 = sb("OH2", [128, 2, 2, NK, S], F16)
        OH, OHR = OH2[:, 0], OH2[:, 1]
        prod = sb("prod", [128, NT, 10, DK])
        GS = sb("GS", [128, 2 + H, NT, NK * 16])
        GV = GS[:, 2:2 + H]
        dots = sb("dots", [128, NT, H, 10])
        sm = sb("sm", [128, 3, NT * H])
        JBf = JB[:].rearrange("p a n s -> p (a n s)")
        OHf = OH2[:].rearrange("p k a n s -> p (k a n s)").bitcast(BF16)
        JBR = OHf[:, 2 * NK * S:].rearrange("p (a n s) -> p a n s", a=2, n=NK)
        n1 = H * S2
        KA1 = JBf[0:QM, 0:n1].rearrange("p (h k) -> p h k", h=H)
        mb1 = JBf[:, n1:n1 + NT * S2].rearrange("p (t k) -> p t k", t=NT)
        mbM1 = JBf[0:KM, n1 + NT * S2:n1 + NT * S2 + S]
        mbR1 = JBf[0:KT, n1 + NT * S2 + S:n1 + NT * S2 + 2 * S]
        QA1 = OHf[0:QM, 0:H * S].rearrange("p (h q) -> p h q", h=H)
        QA0 = QAf[0:QM].bitcast(BF16).rearrange("p (h q) -> p h q", h=H)
        KAs, QAs = ([x1 if n == 1 else x0 for n in range(B)] for x0, x1 in ((KA0[:], KA1), (QA0, QA1)))
        mbs, mbMs, mbRs = ([x1 if n == 1 else x0 for n in range(B)]
                           for x0, x1 in ((mb0[:], mb1), (mbM0[:], mbM1), (mbR0[:], mbR1)))
        past = (0, 0, 2 * SU, 3 * 2 * SU)
        at, own = 0, []
        for n in (S, NT * D, 5 * NT * HN, NT * HN * 2):
            own.append(QAf[:, at:at + n])
            at += n
        QpTs = [QpT[:]] * (B - 1) + [own[0]]
        Qps = [Qp[:]] * (B - 1) + [own[1].rearrange("p (t d) -> p t d", t=NT)]
        poss = [pos[:]] * (B - 1) + [own[2].rearrange("p (a t n) -> p a t n", a=5, t=NT)]
        wtss = [wts[:]] * (B - 1) + [own[3].rearrange("p (t n w) -> p t n w", t=NT, w=2)]
        aws = [p[:, 2:4].rearrange("p a t n -> p (a t n)").rearrange("p (t n w) -> p t n w", t=NT, w=2) for p in poss]
        scs = [p[:, 0] for p in poss]
        GVf = GV.rearrange("p h t c -> p (h t c)")
        W8 = GVf[:, 0:1024].rearrange("p (o e) -> p o e", o=8)
        ctxP = GVf[:, 1024:1024 + B * 162].rearrange("p (b k) -> p b k", b=B)
        ctxR = GVf[:, 3824:3824 + B * 256].rearrange("p (b w s k) -> p b w s k", b=B, w=2, s=4)
        ksf = GVf[:, 2696:2696 + B * S2]
        bsel = GVf[0:RR, 3312:3440]
        ks = hT[:, 0:2, :].rearrange("p a s -> p (a s)").bitcast(BF16)[:, 0:NS * B * S2] \
            .rearrange("p (s k) -> p s k", s=NS)
        b8 = GVf[0:RR, 1672:2696].rearrange("p (o e) -> p o e", o=8)
        km = aws[0].rearrange("p t n w -> p (t n w)").bitcast(mybir.dt.int32)[:, 0:B * S2]
        kmf = dots[:, :, :, :].rearrange("p t h w -> p (t h w)")[:, 0:B * S2].rearrange("p (b k) -> p b k", b=B)
        wtf = wts[:].rearrange("p t n w -> p (t n w)")
        vrow = wtf[0:1, 0:162]
        vrowR = wtf[0:1, 162:162 + 256].rearrange("p (w s k) -> p w s k", w=2, s=4)
        w1f = [hT[:, 2 + 3 * i:5 + 3 * i, :] for i in range(2)]
        lg = sb("lg", [128, 8, 8])
        lg1 = sb("lg1", [128, 4])
        gin = sb("gin", [128, 4])

        UP = pb("UP", [128, 2, 512])
        DOWN = pb("DOWN", [128, 2, 512])
        MISC = pb("MISC", [128, 512])
        RING = pb("RING", [128, 2, 512])
        SUM = pb("SUM", [128, 512])

        schedule = order()
        uses = {k: 1 for k in ("A0a", "A0b", "A2", "A5a", "A5b", "F0a", "F0b", "F0c", "F0d", "G0a", "G0c", "G0d",
                               "G3a", "G3b", "G3c", "G3d", "A4b", "T")}
        uses["G0b"] = 2
        misc_at, n = {}, 0
        for piece in schedule:
            misc_at[piece] = n
            n += uses.get(piece[0], 0)
        norms = [p for p in schedule if p[0] in ("A0a", "F0a", "G0a", "G3c")]
        norm_at = {p: n for n, p in enumerate(norms)}

        def before(piece, kind):
            return sum(p[0] == kind for p in schedule[:schedule.index(piece)])

        ld_const = sem("ld_const")
        ld_ctx = sem("ld_ctx")
        ld_q = sem("ld_q")
        ld_x = sem("ld_x")
        ld_tab = sem("ld_tab")
        ld_moe = sem("ld_moe")
        ld_l1 = sem("ld_l1")
        ld_mask = sem("ld_mask")
        mask_ready = sem("mask_ready")
        dve_done = sem("dve_done")
        act_done = sem("act_done")
        pool_done = sem("pool_done")
        lg_ready = sem("lg_ready")
        noise_ready = sem("noise_ready")
        gate_ready = sem("gate_ready")
        k_ready = sem("k_ready")
        ks_ready = sem("ks_ready")
        v_ready = sem("v_ready")
        v_read = sem("v_read")
        cr_ready = sem("cr_ready")
        ld_w1 = [sem(f"ld_w1_{i}") for i in range(2)]
        w1h_ready = sem("w1h_ready")
        w1_ready = sem("w1_ready")
        xh_ready = sem("xh_ready")
        xl_ready = sem("xl_ready")
        bias_ready = sem("bias_ready")
        pre_pool = sem("pre_pool")
        kparts_out = sem("kparts_out")
        kparts_in = sem("kparts_in")
        misc_ready = sem("misc_ready")
        misc_free = sem("misc_free")
        var_ready = sem("var_ready")
        rstd_ready = sem("rstd_ready")
        xn_ready = sem("xn_ready")
        qs_ready = sem("qs_ready")
        qs_out = sem("qs_out")
        qa_in = sem("qa_in")
        sa_ready = sem("sa_ready")
        sa_free = sem("sa_free")
        nms_ready = sem("nms_ready")
        nms_out = sem("nms_out")
        qm_in = sem("qm_in")
        st_ready = sem("st_ready")
        p_ready = sem("p_ready")
        pv_done = sem("pv_done")
        vm_ready = sem("vm_ready")
        ot_ready = sem("ot_ready")
        ctx_ready = sem("ctx_ready")
        d_ready = sem("d_ready")
        ex_out = sem("ex_out")
        w9_ready = sem("w9_ready")
        up_ready = sem("up_ready")
        h_ready = sem("h_ready")
        down_ready = sem("down_ready")
        down_free = sem("down_free")
        pos_ready = sem("pos_ready")
        jT_ready = sem("jT_ready")
        j_out = sem("j_out")
        jb_in = [sem(f"jb_in{i}") for i in range(2)]
        jbr_in = [sem(f"jbr_in{i}") for i in range(2)]
        oh_ready = sem("oh_ready")
        g_ready = sem("g_ready")
        g_free = sem("g_free")
        gk_used = sem("gk_used")
        z_ready = sem("z_ready")
        e_ready = sem("e_ready")
        cx1_ready = sem("cx1_ready")
        x_done = sem("x_done")
        stored = sem("stored")

        def outputs_at(b, e):
            return b * (NE + 1) + e + (e >= FB)

        def down_count(k):
            return outputs_at(k // (NC * NE), k // NC % NE) + 1

        block = ctx.enter_context(nc.Block())

        @block.sync
        def _(sp):
            for dst, src in ((cst[:], consts), (gin[:], gates.partition_broadcast(128)),
                             (lg[:, 0, :], logits.partition_broadcast(128)),
                             (lg[:, 1, :], u.partition_broadcast(128)),
                             (km, kmask.rearrange("b k -> (b k)").partition_broadcast(128))):
                sp.dma_start(dst, src).then_inc(ld_const, 16)
            sp.wait_ge(pre_pool, 1)
            for dst, src in ((ctxP[:, :, 1:1 + S2], ctxT), (Wk[:], wk), (bcol[:, 1:2], bk_col), (Wv[:], wv),
                             (brow[:], rows.partition_broadcast(RR))):
                sp.dma_start(dst, src).then_inc(ld_ctx, 16)
            for dst, src in ((WkT[:], wkT), (WvT[:], wvT), (W8, w8.rearrange("o d e -> d o e")),
                             (b8, b8_src.partition_broadcast(RR))):
                sp.dma_start(dst, src).then_inc(ld_tab, 16)

            def load_tails(b, four):
                for j in range(4):
                    h = 4 * four + j
                    sp.dma_start(JBR[32 * j:32 * j + 32, four % 2],
                                 dj[b, h * NK:(h + 1) * NK].partition_broadcast(32)).then_inc(jbr_in[four % 2], 16)

            for piece in schedule:
                kind, b = piece[0], piece[1]
                if kind == "K":
                    sp.wait_ge(ks_ready, 1)
                    sp.dma_start(dk.rearrange("s e k -> e s k"), ks).then_inc(kparts_out, 16)
                elif kind == "A0a":
                    if b >= 1:
                        sp.wait_ge(mask_ready, b)
                    sp.dma_start(mraw[:], mask[b].rearrange("(t p) k -> p t k", p=128)).then_inc(ld_mask, 16)
                    sp.dma_start(mrawM[:], maskT[b, 0:KM]).then_inc(ld_mask, 16)
                    sp.dma_start(mrawR[:], maskT[b, KM:S2]).then_inc(ld_mask, 16)
                elif kind == "A0b":
                    sp.wait_ge(qs_ready, b + 1)
                    sp.dma_start(dq[b].rearrange("s e q -> e s q"), qs[:]).then_inc(qs_out, 16)
                    sp.wait_ge(qs_out, 16 * (b + 1))
                    if past[b]:
                        sp.wait_ge(st_ready, past[b])
                    else:
                        sp.wait_ge(kparts_out, 16)
                        sp.wait_ge(pre_pool, 3)
                    for i, s in enumerate(SLOT_K):
                        sp.dma_start(KAs[b][i * DK:(i + 1) * DK], dk[s].rearrange("(h d) k -> d h k", d=DK)
                                     [:, :, b * S2:(b + 1) * S2]).then_inc(kparts_in, 16)
                    for i, s in enumerate(SLOT_Q):
                        sp.dma_start(QAs[b][i * DK:(i + 1) * DK], dq[b, s].rearrange("(h d) q -> d h q", d=DK)).then_inc(qa_in, 16)
                elif kind == "A2":
                    sp.wait_ge(nms_ready, b + 1)
                    sp.dma_start(dm[b].rearrange("t h s q -> (t h) s q"), nms).then_inc(nms_out, 16)
                    sp.wait_ge(nms_out, 16 * (b + 1))
                    for t in range(NT):
                        sp.dma_start(QAs[b][QR:QM, :, t * 128:(t + 1) * 128], dm[b, t].rearrange("h s q -> s h q")).then_inc(qm_in, 16)
                elif kind == "G0d":
                    sp.wait_ge(jT_ready, b + 1)
                    sp.dma_start(dj[b], jT[:]).then_inc(j_out, 16)
                elif kind == "G0e":
                    sp.wait_ge(j_out, 16 * (b + 1))
                    if b == 0:
                        sp.wait_ge(st_ready, 2 * 2 * SU)
                    for h in range(2):
                        if b >= 1:
                            sp.wait_ge(oh_ready, b * H + h - 1)
                        sp.dma_start(JB[:, h % 2], dj[b, h * NK:(h + 1) * NK].partition_broadcast(128)).then_inc(jb_in[h % 2], 16)
                    load_tails(b, 0)
                elif kind == "G1":
                    h = piece[2] + 2
                    if h < H:
                        sp.wait_ge(oh_ready, b * H + h - 1)
                        sp.dma_start(JB[:, h % 2], dj[b, h * NK:(h + 1) * NK].partition_broadcast(128)).then_inc(jb_in[h % 2], 16)
                    four = piece[2] // 4 + 1
                    if piece[2] % 4 == 0 and four < H // 4:
                        if b * H // 4 + four >= 2:
                            sp.wait_ge(g_ready, 2 * (b * H + 4 * (four - 1)))
                        load_tails(b, four)
                elif kind == "G3d":
                    sp.wait_ge(x_done, b + 1)
                    sp.dma_start(out[b].rearrange("(t p) d -> p t d", p=128), X[:, b]).then_inc(stored, 16)
            sp.wait_ge(stored, 16 * B)

        @block.gpsimd
        def _(pool):
            done = [0]

            def step(ins):
                done[0] += 1
                ins.then_inc(pool_done, 1)
                pool.wait_ge(pool_done, done[0])

            pool.memset(GVf[:, 1024:1672], 0.0).then_inc(pre_pool, 1)
            step(pool.memset(vrow, 0.0))
            step(pool.memset(vrow[:, 1:1 + S2], 1.0))
            step(pool.memset(mhalf[:], -0.5))
            step(pool.memset(ones[:], 1.0))
            for w in range(2):
                last = pool.tensor_copy(vrowR[:, w], vrow[:, R0 + w:R0 + w + 32].unsqueeze(1).broadcast_to((1, 4, 32)))
            last.then_inc(pre_pool, 1)
            pool.wait_ge(pre_pool, 2)
            for t, v in ((one_col, 1.0), (VM, 0.0), (VT, 0.0), (KA0, 1.0), (r1[32:33, :], 1.0), (W9, 1.0)):
                step(pool.memset(t[:], v))
            step(pool.memset(pick[:], 0.0))
            for p in range(0, RR, 32):
                step(pool.memset(pick[p:p + 1, :], 1.0))
            pool.memset(KA1, 1.0).then_inc(pre_pool, 1)
            for n in range(4 * B):
                pool.wait_ge(var_ready, n + 1)
                pool.tensor_tensor(rstd[:], ve[:], mhalf[:], ALU.pow).then_inc(rstd_ready, 1)

        @block.scalar
        def _(act):
            for dst, src in ((X[:, 0], x[0].rearrange("(t p) d -> p t d", p=128)), (Wq[:], wq),
                             (bcol[:, 0:1], bq_col), (Wo[:], wo)):
                act.dma_start(dst, src).then_inc(ld_q, 16)
            act.wait_ge(ld_q, 16 * 4)
            act.wait_ge(ld_ctx, 16 * 5)
            for dst, src in ((Wr1[:], wr1), (br1[:], br1_col), (Wr2[0:32, :], wr2), (Wr2[32:33, :], br2),
                             (b1[:], b1_cols), (B2[:], b2)):
                act.dma_start(dst, src).then_inc(ld_moe, 16)
            for b in range(1, B):
                act.dma_start(X[:, b], x[b].rearrange("(t p) d -> p t d", p=128)).then_inc(ld_x, 16)
            for e in range(0, NE, 3):
                if e < 6:
                    act.dma_start(w1f[e // 3], w1[e:e + 3].rearrange("e d i -> d e i")).then_inc(ld_w1[e // 3], 16)
                act.dma_start(W2[:, e:e + 3], w2[e:e + 3].rearrange("e (c i) d -> i e c d", i=128)).then_inc(ld_moe, 16)
            for dst, src in ((WqT[:], wqT), (WoT[:], woT), (WoffT[:], woffT), (bcol[:, 2:3], bq1_col),
                             (boffr[:], boff.partition_broadcast(RR))):
                act.dma_start(dst, src).then_inc(ld_l1, 16)
            act.wait_ge(ld_const, 16 * 5)
            act.activation(tg[:], gin[:], ACT.Tanh).then_inc(gate_ready, 1)

            def evacuate(use, dst, src, bias=0.0):
                act.wait_ge(misc_ready, use + 1)
                act.activation(dst, src, ACT.Identity, bias=bias).then_inc(misc_free, 1)

            def lower_read(piece):
                if n := before(piece, "F0a"):
                    act.wait_ge(xl_ready, n)

            for piece in schedule:
                kind, b = piece[0], piece[1]
                m = misc_at[piece]
                if kind == "W":
                    act.wait_ge(lg_ready, 1)
                    act.activation(lg[:, 3, :], lg[:, 2, :], ACT.Exp, accum_out=lg1[:, 1:2]).then_inc(act_done, 1)
                    act.wait_ge(act_done, 1)
                    act.activation(lg1[:, 2:3], lg1[:, 1:2], ACT.Ln)
                    act.activation(lg[:, 4, :], lg[:, 1, :], ACT.Ln).then_inc(act_done, 1)
                    act.wait_ge(act_done, 2)
                    act.activation(lg[:, 5, :], lg[:, 4, :], ACT.Ln, scale=-1.0).then_inc(noise_ready, 1)
                elif kind == "S":
                    e = 3 * b
                    if b == 2:
                        act.wait_ge(w1_ready, 1)
                        act.dma_start(w1f[0], w1[e:e + 3].rearrange("e d i -> d e i")).then_inc(ld_w1[0], 16)
                    act.wait_ge(ld_w1[b % 2], 16 * (b // 2 + 1))
                    act.activation(W1[:, 0, e:e + 3], w1f[b % 2], ACT.Identity, scale=W1SCALE).then_inc(w1h_ready, 1)
                elif kind == "A0a":
                    lower_read(piece)
                    evacuate(m, xnT[:], MISC[:])
                elif kind in ("G0a", "G3a", "G3c"):
                    evacuate(m, QpTs[b], MISC[:])
                elif kind == "A3":
                    hb, u = piece[2:]
                    i = (b * 2 + hb) * SU + u
                    act.wait_ge(st_ready, i + 1)
                    if i >= 2:
                        act.wait_ge(pv_done, i - 1)
                    n = 1 if u % 3 == 2 else 2
                    act.activation(PT[:, i % 2, 0:n, :], RING[:, i % 2, 0:n * 256].rearrange("k (h q) -> k h q", h=n),
                                   ACT.Exp).then_inc(p_ready, 1)
                elif kind == "A4a":
                    act.wait_ge(pv_done, (b * 2 + piece[2] + 1) * SU)
                    if b * 2 + piece[2]:
                        act.wait_ge(ctx_ready, b * 2 + piece[2])
                    act.activation(OT[:], SUM[0:VW, :].rearrange("k (g q) -> k g q", g=2), ACT.Identity).then_inc(ot_ready, 1)
                elif kind == "A5a":
                    lower_read(piece)
                    evacuate(m, cxT[:], MISC[:])
                elif kind == "F0a":
                    evacuate(m, xnT[:], MISC[:])
                    act.wait_ge(misc_free, m + 1)
                    act.activation(xnTf[:, b % 2, 0], xnT[:], ACT.Identity).then_inc(xh_ready, 1)
                elif kind == "F0c":
                    act.wait_ge(misc_free, m + 1)
                    act.activation(gt[:, 1], gt[:, 0], ACT.Exp).then_inc(ex_out, 1)
                elif kind == "F0g":
                    act.wait_ge(d_ready, b + 1)
                    act.activation(gs[:, 6], gs[:, 5], ACT.Exp, scale=0.5).then_inc(ex_out, 1)
                elif kind == "F0d":
                    evacuate(m, w9T[:], MISC[0:NE, :])
                elif kind == "F1" and piece[2] < NE:
                    e, c = piece[2:]
                    if b == 0 and e == 0 and c == 0:
                        act.wait_ge(kparts_out, 16)
                        act.wait_ge(w1_ready, 3)
                        act.wait_ge(ld_moe, 16 * LD_MOE)
                    i = (b * NE + e) * NC + c
                    act.wait_ge(up_ready, i + 1)
                    if i >= HS:
                        act.wait_ge(down_ready, down_count(i - HS))
                    act.activation(hT[:, i % HS, :], UP[:, i % 2, :], ACT.Silu,
                                   bias=b1[:, e, c:c + 1], scale=1.0 / W1SCALE).then_inc(h_ready, 1)
                elif kind == "G0b":
                    act.wait_ge(ld_l1, 16 * 5)
                    evacuate(m, Qps[b].rearrange("p t e -> p (t e)"), MISC[:])
                    evacuate(m + 1, QpTs[b], MISC[:], bias=bcol[:, 2:3])
                elif kind == "G0d":
                    if b >= 1:
                        act.wait_ge(j_out, 16 * b)
                    act.wait_ge(misc_ready, m + 1)
                    act.activation(jT[:], MISC[0:HN, :], ACT.Identity).then_inc(jT_ready, 1)
                    act.wait_ge(jT_ready, b + 1)
                    act.nop().then_inc(misc_free, 1)
                elif kind == "G1":
                    h = piece[2]
                    if h == 0 and b >= 1:
                        act.wait_ge(cx1_ready, b)
                    if b * H + h >= 2:
                        act.wait_ge(gk_used, b * H + h - 1)
                    for tp in range(2):
                        i = (b * H + h) * 2 + tp
                        act.wait_ge(g_ready, i + 1)
                        both = GS[:, h % 2:h + 3:h + 2 - h % 2, 2 * tp:2 * tp + 2, :]
                        act.activation(both.rearrange("p k t c -> p t k c"),
                                       RING[:, i % 2, 0:320].rearrange("p (t k c) -> p t k c", t=2, k=2),
                                       ACT.Identity).then_inc(g_free, 1)
                elif kind == "G2b":
                    act.wait_ge(z_ready, b + 1)
                    act.activation(scs[b], scs[b], ACT.Exp, scale=1.0 / math.sqrt(DK)).then_inc(e_ready, 1)

        @block.tensor
        def _(pe):
            def take_misc(use):
                if use >= 1:
                    pe.wait_ge(misc_free, use)

            def transposes(use, src, width=128):
                take_misc(use)
                for t in range(NT):
                    last = pe.transpose(MISC[0:width, t * 128:(t + 1) * 128], src[:, t, :], ident)
                last.then_inc(misc_ready, 1)

            def rows_out(use, srcT, w, bias, width=128):
                take_misc(use)
                pe.matmul(MISC[:, 0:NT * width].rearrange("p (t e) -> p t e", t=NT), pick[:],
                          bias.unsqueeze(1).broadcast_to((RR, NT, width)), start=True, stop=False)
                for t in range(NT):
                    last = pe.matmul(MISC[:, t * width:(t + 1) * width], srcT[:, t * 128:(t + 1) * 128], w,
                                     start=False, stop=(t == NT - 1))
                last.then_inc(misc_ready, 1)

            def pv(b, hb, u):
                i = (b * 2 + hb) * SU + u
                pe.wait_ge(p_ready, i + 1)
                four, r = divmod(u, 3)
                o = SUM[0:VW, four // 2 * 256:(four // 2 + 1) * 256]
                if r < 2:
                    for k in range(2):
                        h = 4 * four + 2 * r + k
                        first = h * VW + VW - (DK + 1) - (DK + 1) * (h % 8)
                        last = pe.matmul(o, VM[:, first:first + VW], PT[:, i % 2, k, :],
                                         start=(h % 8 == 0), stop=False)
                else:
                    last = pe.matmul(o, VT[:, four // 2, four % 2 * VW:(four % 2 + 1) * VW], PT[:, i % 2, 0, :],
                                     start=False, stop=(four % 2 == 1))
                last.then_inc(pv_done, 1)

            def down(b, e, t):
                k = (b * NE + e) * NC
                n = outputs_at(b, e)
                if t == 0:
                    pe.wait_ge(h_ready, k + NC)
                    if n >= 2:
                        pe.wait_ge(down_free, n - 1)
                    else:
                        pe.wait_ge(ks_ready, 1)
                for c in range(NC):
                    last = pe.matmul(DOWN[:, n % 2, t * 128:(t + 1) * 128], hT[:, (k + c) % HS, t * 128:(t + 1) * 128],
                                     W2[:, e, c, :], start=(c == 0), stop=(c == NC - 1))
                if t == NT - 1:
                    last.then_inc(down_ready, 1)

            for piece in schedule:
                kind, b = piece[0], piece[1]
                m = misc_at[piece]
                if kind == "K":
                    pe.wait_ge(ld_ctx, 16 * 5)
                    for i in range(2):
                        last = pe.matmul(DOWN[:, i, 0:2 * S2].rearrange("p (b k) -> p b k", b=2), Wk[:],
                                         ctxP[:, 2 * i:2 * i + 2, 1:1 + S2], start=True, stop=True)
                    last.then_inc(k_ready, 1)
                elif kind == "V":
                    pe.wait_ge(pre_pool, 2)
                    pe.wait_ge(cr_ready, 1)
                    for n in range(B):
                        for c, (rws, valid) in enumerate((
                                (ctxP[:, n, 1:1 + KM], ones[:]),
                                (ctxR[:, n, 1].rearrange("p s k -> p (s k)"), vrowR[:, 1].rearrange("p s k -> p (s k)")))):
                            o = UP[:, n // 2, (n % 2 * 2 + c) * 128:(n % 2 * 2 + c + 1) * 128]
                            pe.matmul(o, valid, brow[0:1, 0, :], start=True, stop=False)
                            last = pe.matmul(o, rws, Wv[:], start=False, stop=True)
                    last.then_inc(v_ready, 1)
                elif kind == "T":
                    ch = piece[2]
                    i = 2 * b + ch
                    if i == 0:
                        pe.wait_ge(ld_tab, 16 * 4)
                    take_misc(m)
                    for kv, w in enumerate((WkT, WvT)):
                        for two in range(2):
                            o = MISC[:, (kv * 2 + two) * 128:(kv * 2 + two + 1) * 128]
                            if ch == 0:
                                valid, rws = vrow[:, two:two + R0], ctxP[:, b, two:two + R0]
                            else:
                                valid = vrowR[:, two].rearrange("p s k -> p (s k)")
                                rws = ctxR[:, b, two].rearrange("p s k -> p (s k)")
                            pe.matmul(o, valid, brow[0:1, 1 + kv, :], start=True, stop=False)
                            last = pe.matmul(o, rws, w[:], start=False, stop=True)
                    last.then_inc(misc_ready, 1)
                elif kind == "A0a":
                    if b == 0:
                        pe.wait_ge(ld_q, 16 * 4)
                    pe.wait_ge(xn_ready, norm_at["A0a", b] + 1)
                    transposes(m, xn)
                elif kind == "A0b":
                    take_misc(m)
                    pe.matmul(MISC[:], Wq[:], xnT[:], start=True, stop=True).then_inc(misc_ready, 1)
                elif kind == "A1":
                    t = piece[2]
                    QA, KA, mb = QAs[b], KAs[b], mbs[b]
                    if t == 0:
                        pe.wait_ge(qa_in, 16 * len(SLOT_Q) * (b + 1))
                        pe.wait_ge(mask_ready, b + 1)
                        pe.wait_ge(kparts_in, 16 * len(SLOT_K) * (b + 1))
                        if b:
                            pe.wait_ge(p_ready, b * 2 * SU)
                        if n := before(piece, "G1"):
                            pe.wait_ge(g_free, 2 * n)
                    h = 0
                    for g, n in enumerate(HG):
                        i = (b * NT + t) * len(HG) + g
                        if i >= 2:
                            pe.wait_ge(sa_free, i - 1)
                        o = RING[:, i % 2, 0:n * S2].rearrange("p (h k) -> p h k", h=n)
                        pe.matmul(o, identb[:], mb[:, t, :].unsqueeze(1).broadcast_to((128, n, S2)),
                                  start=True, stop=False)
                        for k in range(n):
                            last = pe.matmul(o[:, k, :], QA[0:QR, h, t * 128:(t + 1) * 128],
                                             KA[0:QR, h, :], start=False, stop=(k == n - 1))
                            h += 1
                        last.then_inc(sa_ready, 1)
                elif kind == "A2":
                    pe.wait_ge(sa_free, (b + 1) * NT * len(HG))
                    take_misc(m)
                    pe.transpose(MISC[0:NT * H, 0:128], nmax[:].rearrange("p t h -> p (t h)"), ident).then_inc(misc_ready, 1)
                elif kind == "A3":
                    hb, u = piece[2:]
                    i = (b * 2 + hb) * SU + u
                    QA, KA, mbM, mbR = QAs[b], KAs[b], mbMs[b], mbRs[b]
                    if u == 0:
                        if hb == 0:
                            pe.wait_ge(qm_in, 16 * NT * (b + 1))
                            pe.wait_ge(vm_ready, b + 1)
                        if b * 2 + hb:
                            pe.wait_ge(ot_ready, b * 2 + hb)
                    if i >= 2 and not (hb == 0 and u == 0):
                        pe.wait_ge(p_ready, i - 1)
                    q = slice(hb * 256, (hb + 1) * 256)
                    four, part = divmod(u, 3)
                    if part < 2:
                        o = RING[:, i % 2, :].rearrange("k (h q) -> k h q", h=2)
                        pe.matmul(o, identb[:], mbM[:, q].unsqueeze(1).broadcast_to((KM, 2, 256)), start=True, stop=False)
                        for k in range(2):
                            h = 4 * four + 2 * part + k
                            last = pe.matmul(o[:, k, :], KA[:, h, 0:KM], QA[:, h, q], start=False, stop=(k == 1))
                    else:
                        pe.matmul(RING[:, i % 2, 0:256], ident4[:].rearrange("k j c -> k (j c)"), mbR[:, q],
                                  start=True, stop=False)
                        for j in range(4):
                            last = pe.matmul(RING[32 * j:32 * j + KT, i % 2, 0:256], KA[:, 4 * four + j, KM:S2],
                                             QA[:, 4 * four + j, q], start=False, stop=True)
                    last.then_inc(st_ready, 1)
                    if u >= 1:
                        pv(b, hb, u - 1)
                elif kind == "A4a":
                    pv(b, piece[2], SU - 1)
                elif kind == "A4b":
                    pe.wait_ge(ot_ready, b * 2 + piece[2] + 1)
                    take_misc(m)
                    for t in range(2):
                        for g in range(2):
                            last = pe.transpose(MISC[:, (t * 2 + g) * VW:(t * 2 + g + 1) * VW],
                                                OT[:, g, t * 128:(t + 1) * 128], ident[0:VW, 0:VW])
                    last.then_inc(misc_ready, 1)
                elif kind == "A5a":
                    pe.wait_ge(ctx_ready, 2 * (b + 1))
                    transposes(m, cx)
                elif kind == "A5b":
                    if b == 0:
                        pe.wait_ge(bias_ready, 1)
                    rows_out(m, cxT, Wo[:], b_out)
                elif kind == "F0a":
                    if b == 0:
                        pe.wait_ge(ld_moe, 16 * LD_MOE)
                    pe.wait_ge(xn_ready, norm_at["F0a", b] + 1)
                    transposes(m, xn)
                elif kind == "F0b":
                    take_misc(m)
                    pe.matmul(MISC[0:32, :], Wr1[:], xnT[:], start=True, stop=True).then_inc(misc_ready, 1)
                elif kind == "F0c":
                    take_misc(m)
                    for t in range(NT):
                        last = pe.matmul(MISC[:, t * 8:(t + 1) * 8], r1[:, t * 128:(t + 1) * 128], Wr2[:],
                                         start=True, stop=True)
                    last.then_inc(misc_ready, 1)
                elif kind == "F0d":
                    pe.wait_ge(w9_ready, b + 1)
                    transposes(m, W9[:, b % 2], NE)
                elif kind == "F0e":
                    n = b * (NE + 1) + FB
                    pe.wait_ge(misc_free, misc_at["F0d", b] + 1)
                    pe.wait_ge(down_free, n - 1)
                    for t in range(NT):
                        last = pe.matmul(DOWN[:, n % 2, t * 128:(t + 1) * 128], w9T[:, t * 128:(t + 1) * 128], B2[:],
                                         start=True, stop=True)
                    last.then_inc(down_ready, 1)
                elif kind == "F1":
                    e, c = piece[2:]
                    if e < NE:
                        i = (b * NE + e) * NC + c
                        if i == 0:
                            pe.wait_ge(v_read, 1)
                            pe.wait_ge(w1_ready, 3)
                        if e == 0 and c == 0:
                            pe.wait_ge(xl_ready, b + 1)
                        if i >= 2:
                            pe.wait_ge(h_ready, i - 1)
                        for n, (pw, px) in enumerate(((0, 0), (1, 0), (0, 1))):
                            last = pe.matmul(UP[:, i % 2, :], W1[:, pw, e, c * 128:(c + 1) * 128],
                                             xnTf[:, b % 2, px], start=(n == 0), stop=(n == 2))
                        last.then_inc(up_ready, 1)
                    if e >= 1:
                        down(b, e - 1, c)
                elif kind == "G0a":
                    if b == 0:
                        pe.wait_ge(ld_l1, 16 * 5)
                    pe.wait_ge(xn_ready, norm_at["G0a", b] + 1)
                    transposes(m, xn)
                elif kind == "G0b":
                    rows_out(m, QpTs[b], WqT[:], b_q1)
                    take_misc(m + 1)
                    pe.matmul(MISC[:], WqT[:], QpTs[b], start=True, stop=True).then_inc(misc_ready, 1)
                elif kind == "G0c":
                    rows_out(m, QpTs[b], WoffT[:], b_off, HN)
                elif kind == "G0d":
                    pe.wait_ge(pos_ready, b + 1)
                    transposes(m, poss[b][:, 1], HN)
                elif kind == "G1":
                    h = piece[2]
                    idx = b * H + h

                    def table(a):
                        return a.rearrange("p (k c) -> p k c", k=2)

                    if h == 0:
                        pe.wait_ge(p_ready, before(piece, "A3"))
                    pe.wait_ge(oh_ready, idx + 1)
                    for tp in range(2):
                        i = idx * 2 + tp
                        if i >= 2:
                            pe.wait_ge(g_free, i - 1)
                        for t in range(2):
                            q = slice((2 * tp + t) * 128, (2 * tp + t + 1) * 128)
                            for n in range(NK):
                                o = RING[:, i % 2, t * 160:(t + 1) * 160].rearrange("p (k n c) -> p k n c", k=2, n=NK)[:, :, n, :]
                                rest = slice(32 * (h % 4), 32 * (h % 4) + 32)
                                for part in range(2):
                                    pe.matmul(o, OH[:, idx % 2, n, q], table(TAB[:, b, 0, part, h]),
                                              start=(part == 0), stop=False)
                                for part in range(2):
                                    last = pe.matmul(o, OHR[rest, h // 4 % 2, n, q], table(TAB[rest, b, 1, part, h]),
                                                     start=False, stop=(part == 1))
                        last.then_inc(g_ready, 1)
                elif kind == "G3a":
                    pe.wait_ge(cx1_ready, b + 1)
                    transposes(m, Qps[b])
                elif kind == "G3b":
                    rows_out(m, QpTs[b], WoT[:], b_out1)
                elif kind == "G3c":
                    pe.wait_ge(xn_ready, norm_at["G3c", b] + 1)
                    transposes(m, xn)
                elif kind == "G3d":
                    if b == 0:
                        pe.wait_ge(bias_ready, 2)
                    rows_out(m, QpTs[b], Wsel[:], b_sel)

        @block.vector
        def _(dve):
            done = [0]

            def step(ins):
                done[0] += 1
                ins.then_inc(dve_done, 1)
                dve.wait_ge(dve_done, done[0])

            def by_tile(a, n):
                return a.unsqueeze(2).broadcast_to((128, NT, n))

            def norm(b, key):
                n = norm_at[key]
                if n >= 1:
                    dve.wait_ge(misc_ready, misc_at[norms[n - 1]] + 1)
                for t in range(NT):
                    last = dve.bn_stats(st[:, t, :], X[:, b, t, :])
                step(last)
                for t in range(NT):
                    last = dve.bn_aggr(mv[:, t, :], st[:, t, :])
                step(last)
                dve.tensor_scalar(ve[:], mv[:, :, 1], EPS, None, ALU.add).then_inc(var_ready, 1)
                dve.wait_ge(rstd_ready, n + 1)
                for t in range(NT):
                    last = dve.tensor_scalar(xn[:, t, :], X[:, b, t, :], mv[:, t, 0:1], rstd[:, t:t + 1],
                                             ALU.subtract, ALU.mult)
                last.then_inc(xn_ready, 1)

            def add_misc(use, b, gate):
                dve.wait_ge(misc_ready, use + 1)
                dve.wait_ge(gate_ready, 1)
                xb = X[:, b].rearrange("p t d -> p (t d)")
                dve.scalar_tensor_tensor(out=xb, in0=MISC[:], scalar=tg[:, gate:gate + 1], in1=xb,
                                         op0=ALU.mult, op1=ALU.add).then_inc(misc_free, 1)
                dve.wait_ge(misc_free, use + 1)

            dve.wait_ge(ld_const, 16 * 5)
            dve.tensor_copy(identb[:], ident)
            dve.tensor_copy(ident4[:], ident[0:KT, 0:32].unsqueeze(1).broadcast_to((KT, 4, 32)))
            step(dve.tensor_reduce(lg1[:, 0:1], lg[:, 0, :], AX.X, ALU.max))
            dve.tensor_scalar(lg[:, 2, :], lg[:, 0, :], lg1[:, 0:1], None, ALU.subtract).then_inc(lg_ready, 1)
            step(dve.tensor_scalar(kmf.rearrange("p b k -> p (b k)"), km, -1.0, 1.0, ALU.mult, ALU.add))
            step(dve.tensor_reduce(lens[:, 0, :], kmf, AX.X, ALU.add))
            step(dve.tensor_scalar(lens[:, 0, :], lens[:, 0, :], -1.0, None, ALU.add))
            step(dve.tensor_scalar(sgn[:], lens[:, 0, :], 0.0, None, ALU.is_ge))
            step(dve.tensor_scalar(sgn[:], sgn[:], 2.0, -1.0, ALU.mult, ALU.add))
            step(dve.tensor_tensor(lens[:, 0, :], lens[:, 0, :], sgn[:], ALU.mult))
            dve.tensor_scalar(lens[:, 1, :], lens[:, 0, :], -1.0, None, ALU.mult)
            step(dve.reciprocal(lens[:, 2, :], lens[:, 0, :]))
            dve.tensor_scalar(lens[:, 3, :], sgn[:], S2 / (S2 - 1.0), None, ALU.mult)
            step(dve.tensor_tensor(lens[:, 2, :], lens[:, 2, :], sgn[:], ALU.mult))
            def onehot(b, h):
                idx = b * H + h
                dve.wait_ge(jb_in[h % 2], 16 * (idx // 2 + 1))
                if idx >= 2:
                    dve.wait_ge(g_ready, 2 * (idx - 1))
                elif idx == 0:
                    dve.wait_ge(st_ready, 2 * 2 * SU)
                if h % 4 == 0:
                    n = idx // 4
                    dve.wait_ge(jbr_in[n % 2], 64 * (n // 2 + 1))
                    dve.tensor_scalar(OHR[:, n % 2], JBR[:, n % 2], cst[:, C_KR:C_KR + 1], None, ALU.is_equal)
                dve.tensor_scalar(OH[:, idx % 2], JB[:, h % 2], cst[:, C_K0:C_K0 + 1], None,
                                  ALU.is_equal).then_inc(oh_ready, 1)

            def weigh(b, e):
                n = outputs_at(b, e)
                dve.wait_ge(down_ready, n + 1)
                if e == 0:
                    dve.wait_ge(w9_ready, b + 1)
                else:
                    dve.wait_ge(down_free, n)
                for t in range(NT):
                    o = DOWN[:, n % 2, t * 128:(t + 1) * 128]
                    if e == 0:
                        last = dve.tensor_scalar(acc[:, t, :], o, W9[:, b % 2, t, 0:1], None, ALU.mult)
                    else:
                        last = dve.scalar_tensor_tensor(out=acc[:, t, :], in0=o, scalar=W9[:, b % 2, t, e:e + 1],
                                                        in1=acc[:, t, :], op0=ALU.mult, op1=ALU.add)
                last.then_inc(down_free, 1)

            def biases(b):
                n = b * (NE + 1) + FB
                dve.wait_ge(down_ready, n + 1)
                dve.wait_ge(down_free, n)
                accf = acc[:].rearrange("p t d -> p (t d)")
                dve.tensor_tensor(accf, DOWN[:, n % 2, :], accf, ALU.add).then_inc(down_free, 1)

            def split_rows(dst, src):
                step(dve.tensor_copy(dst, src))
                step(dve.tensor_tensor(src, src, dst, ALU.subtract))
                dve.tensor_copy(dst[32:64], src[32:64])
                step(dve.tensor_copy(dst[64:96], src[64:96]))
                step(dve.tensor_tensor(src[64:96], src[64:96], dst[64:96], ALU.subtract))
                return dve.tensor_copy(dst[64:96], src[64:96])

            def scores_of(b):
                return scs[b], scs[b].rearrange("p t (h n) -> p (t h) n", n=NK)

            def taps(a):
                return a.unsqueeze(2).broadcast_to((128, NT * H, NK))

            for piece in schedule:
                kind, b = piece[0], piece[1]
                m = misc_at[piece]
                if kind == "K":
                    dve.wait_ge(k_ready, 1)
                    for i in range(2):
                        last = dve.tensor_scalar(ksf[:, 2 * i * S2:2 * (i + 1) * S2], DOWN[:, i, 0:2 * S2], bcol[:, 1:2],
                                                 None, ALU.add)
                    step(last)
                    for s in range(NS - 1):
                        step(dve.tensor_copy(ks[:, s, :], ksf))
                        step(dve.tensor_tensor(ksf, ksf, ks[:, s, :], ALU.subtract))
                    dve.tensor_copy(ks[:, NS - 1, :], ksf).then_inc(ks_ready, 1)
                elif kind == "V":
                    dve.wait_ge(ld_ctx, 16 * 5)
                    for n in range(B):
                        for two in range(2):
                            last = dve.tensor_copy(ctxR[:, n, two], ctxP[:, n, R0 + two:R0 + two + 32].unsqueeze(1)
                                                   .broadcast_to((128, 4, 32)))
                    last.then_inc(cr_ready, 1)
                    dve.wait_ge(v_ready, 1)
                    dve.wait_ge(pre_pool, 3)
                    for n in range(2):
                        dve.tensor_copy(VC[:, 2 * n:2 * n + 2].rearrange("p b c e -> p (b c e)"), UP[:, n, :])
                    dve.tensor_copy(VM[:, VW - DK - 1:].rearrange("p (h w) -> p h w", h=H)[:, :, DK], one_col[:])
                    for j in range(4):
                        for rp in range(2):
                            at = rp * (VW + 4 * (DK + 1)) + j * (DK + 1) + DK
                            last = dve.tensor_copy(VT[32 * j:32 * j + 32, :, at],
                                                   cst[32 * j:32 * j + 32, C_TAIL:C_TAIL + 1].broadcast_to((32, 2)))
                    last.then_inc(v_read, 1)
                elif kind == "T":
                    ch = piece[2]
                    dve.wait_ge(misc_ready, m + 1)

                    def entry(part):
                        return TAB[:, b, ch, part].rearrange("p h (w d) -> p h w d", w=4)

                    rws = MISC[:].rearrange("p (w h d) -> p h w d", w=4, h=H)
                    step(dve.tensor_copy(entry(0), rws))
                    dve.tensor_tensor(entry(1), rws, entry(0), ALU.subtract).then_inc(misc_free, 1)
                    dve.wait_ge(misc_free, m + 1)
                elif kind == "W":
                    dve.wait_ge(noise_ready, 1)
                    dve.wait_ge(ld_tab, 16 * 4)
                    step(dve.tensor_scalar(lg[:, 6, :], lg[:, 2, :], lg1[:, 2:3], None, ALU.subtract))
                    step(dve.tensor_tensor(lg[:, 6, :], lg[:, 6, :], lg[:, 5, :], ALU.subtract))
                    step(dve.tensor_reduce(lg1[:, 0:1], lg[:, 6, :], AX.X, ALU.max))
                    step(dve.tensor_scalar(lg[:, 7, :], lg[:, 6, :], lg1[:, 0:1], None, ALU.is_equal))
                    step(dve.tensor_tensor(lg[:, 6, :], lg[:, 7, :], cst[:, C_RANK:C_RANK + 8], ALU.mult))
                    step(dve.tensor_reduce(lg1[:, 0:1], lg[:, 6, :], AX.X, ALU.max))
                    step(dve.tensor_scalar(lg[:, 7, :], lg[:, 6, :], lg1[:, 0:1], None, ALU.is_equal))
                    dve.tensor_scalar(Wsel[:], W8[:, 0, :], lg[:, 7, 0:1], None, ALU.mult)
                    step(dve.tensor_scalar(bsel, b8[:, 0, :], lg[0:RR, 7, 0:1], None, ALU.mult))
                    for o in range(1, 8):
                        dve.scalar_tensor_tensor(out=Wsel[:], in0=W8[:, o, :], scalar=lg[:, 7, o:o + 1], in1=Wsel[:],
                                                 op0=ALU.mult, op1=ALU.add)
                        step(dve.scalar_tensor_tensor(out=bsel, in0=b8[:, o, :], scalar=lg[0:RR, 7, o:o + 1], in1=bsel,
                                                      op0=ALU.mult, op1=ALU.add))
                    split_rows(b_sel, bsel).then_inc(bias_ready, 1)
                elif kind == "S":
                    e = 3 * b
                    dve.wait_ge(w1h_ready, b + 1)
                    dve.scalar_tensor_tensor(out=W1[:, 1, e:e + 3], in0=w1f[b % 2], scalar=W1SCALE,
                                             in1=W1[:, 0, e:e + 3], op0=ALU.mult,
                                             op1=ALU.subtract).then_inc(w1_ready, 1)
                    if b == 0:
                        dve.wait_ge(ld_l1, 16 * 5)
                        split_rows(b_off, boffr[:])
                        split_rows(bparts[:, 0:3 * 128], brow[:, 3:6].rearrange("p a e -> p (a e)")).then_inc(bias_ready, 1)
                elif kind in ("A0a", "F0a", "G0a", "G3c"):
                    if kind == "A0a":
                        if b == 0:
                            dve.wait_ge(ld_q, 16 * 4)
                        else:
                            dve.wait_ge(ld_x, 16 * (B - 1))
                    norm(b, (kind, b))
                elif kind == "A0b":
                    mb, mbM, mbR = mbs[b], mbMs[b], mbRs[b]
                    if past[b]:
                        dve.wait_ge(st_ready, past[b])
                    dve.wait_ge(ld_mask, 48 * (b + 1))
                    dve.tensor_scalar(mb, mraw[:], MASKED, None, ALU.mult)
                    dve.tensor_scalar(mbM, mrawM[:], MASKED, None, ALU.mult)
                    dve.tensor_scalar(mbR, mrawR[:], MASKED, None, ALU.mult).then_inc(mask_ready, 1)
                    dve.wait_ge(misc_ready, m + 1)
                    dve.tensor_scalar(qf, MISC[:], bcol[:, 0:1], 1.0 / math.sqrt(DK), ALU.add,
                                      ALU.mult).then_inc(misc_free, 1)
                    dve.wait_ge(misc_free, m + 1)
                    if b:
                        dve.wait_ge(qs_out, 16 * b)
                    for s in range(NS - 1):
                        step(dve.tensor_copy(qs[:, s, :], qf))
                        step(dve.tensor_tensor(qf, qf, qs[:, s, :], ALU.subtract))
                    dve.tensor_copy(qs[:, NS - 1, :], qf).then_inc(qs_ready, 1)
                elif kind == "A1":
                    t, h = piece[2], 0
                    for g, n in enumerate(HG):
                        i = (b * NT + t) * len(HG) + g
                        dve.wait_ge(sa_ready, i + 1)
                        dve.tensor_reduce(nmax[:, t, h:h + n], RING[:, i % 2, 0:n * S2].rearrange("p (h k) -> p h k", h=n),
                                          AX.X, ALU.max, negate=True).then_inc(sa_free, 1)
                        h += n
                elif kind == "A2":
                    dve.wait_ge(misc_ready, m + 1)
                    dve.tensor_copy(nmr, MISC[0:NT * H, 0:128]).then_inc(misc_free, 1)
                    dve.wait_ge(misc_free, m + 1)
                    if b:
                        dve.wait_ge(nms_out, 16 * b)
                    for s in range(NS - 1):
                        step(dve.tensor_copy(nms[:, s, :], nmr))
                        step(dve.tensor_tensor(nmr, nmr, nms[:, s, :], ALU.subtract))
                    dve.tensor_copy(nms[:, NS - 1, :], nmr).then_inc(nms_ready, 1)
                    if b:
                        dve.wait_ge(pv_done, b * 2 * SU)
                    dve.wait_ge(v_read, 1)
                    dve.tensor_copy(VM[:, VW - DK - 1:].rearrange("p (h w) -> p h w", h=H)[:, :, 0:DK],
                                    VC[:, b, 0, :].rearrange("p (h d) -> p h d", d=DK))
                    for j in range(4):
                        for rp in range(2):
                            at = rp * (VW + 4 * (DK + 1)) + j * (DK + 1)
                            tail = VC[32 * j:32 * j + 32, b, 1, :].rearrange("p (r h d) -> p r h d", r=2, d=DK)
                            last = dve.tensor_copy(VT[32 * j:32 * j + 32, :, at:at + DK], tail[:, :, 4 * rp + j, :])
                    last.then_inc(vm_ready, 1)
                elif kind == "A4b":
                    hb = piece[2]
                    dve.wait_ge(misc_ready, m + 1)
                    sums = MISC[:, 0:2 * H * 9].rearrange("p (t h d) -> p t h d", t=2, h=H)
                    step(dve.reciprocal(rden[:], sums[:, :, :, DK]))
                    step(dve.tensor_tensor(cx[:, 2 * hb:2 * hb + 2, :].rearrange("p t (h d) -> p t h d", d=DK),
                                           sums[:, :, :, 0:DK], rden[:].unsqueeze(3).broadcast_to((128, 2, H, DK)),
                                           ALU.mult))
                    dve.nop().then_inc(misc_free, 1)
                    dve.nop().then_inc(ctx_ready, 1)
                elif kind == "A5b":
                    add_misc(m, b, 0)
                elif kind == "F0b":
                    if b == 0:
                        dve.wait_ge(ld_moe, 16 * LD_MOE)
                    dve.wait_ge(xh_ready, b + 1)
                    dve.tensor_tensor(xnTf[:, b % 2, 1], xnT[:], xnTf[:, b % 2, 0], ALU.subtract).then_inc(xl_ready, 1)
                    dve.wait_ge(misc_ready, m + 1)
                    dve.tensor_scalar(r1[0:32, :], MISC[0:32, :], br1[:, 0:1], 0.0, ALU.add, ALU.max).then_inc(misc_free, 1)
                elif kind == "F0c":
                    dve.wait_ge(misc_ready, m + 1)
                    lgt = MISC[:, 0:NT * 8].rearrange("p (t e) -> p t e", t=NT)
                    step(dve.tensor_reduce(gs[:, 0], lgt, AX.X, ALU.max))
                    dve.tensor_tensor(gt[:, 0], lgt, by_tile(gs[:, 0], 8), ALU.subtract).then_inc(misc_free, 1)
                elif kind == "F0g":
                    rank = cst[:, C_RANK:C_RANK + 8].unsqueeze(1).broadcast_to((128, NT, 8))
                    dve.wait_ge(ex_out, 2 * b + 1)
                    step(dve.tensor_reduce(gs[:, 1], gt[:, 1], AX.X, ALU.add))
                    step(dve.reciprocal(gs[:, 2], gs[:, 1]))
                    step(dve.tensor_tensor(gt[:, 2], gt[:, 1], by_tile(gs[:, 2], 8), ALU.mult))

                    def greatest(g, top, eq, rk, at, first):
                        step(dve.tensor_reduce(gs[:, top], gt[:, g], AX.X, ALU.max))
                        step(dve.tensor_tensor(gt[:, eq], gt[:, g], by_tile(gs[:, top], 8), ALU.is_equal))
                        step(dve.tensor_tensor(gt[:, rk], gt[:, eq], rank, ALU.mult))
                        step(dve.tensor_reduce(gs[:, at], gt[:, rk], AX.X, ALU.max))
                        step(dve.tensor_tensor(gt[:, first], gt[:, rk], by_tile(gs[:, at], 8), ALU.is_equal))

                    greatest(2, 3, 3, 3, 4, 5)
                    step(dve.scalar_tensor_tensor(out=gt[:, 6], in0=gt[:, 5], scalar=-4.0, in1=gt[:, 2],
                                                  op0=ALU.mult, op1=ALU.add))
                    greatest(6, 7, 7, 7, 8, 9)
                    dve.tensor_tensor(gs[:, 5], gs[:, 7], gs[:, 3], ALU.subtract).then_inc(d_ready, 1)
                elif kind == "F0h":
                    dve.wait_ge(ex_out, 2 * b + 2)
                    step(dve.tensor_scalar(gs[:, 9], gs[:, 6], 1.0, None, ALU.add))
                    step(dve.reciprocal(gs[:, 1], gs[:, 9]))
                    step(dve.tensor_tensor(gs[:, 2], gs[:, 6], gs[:, 1], ALU.mult))
                    dve.tensor_tensor(gt[:, 8], gt[:, 5], by_tile(gs[:, 1], 8), ALU.mult)
                    step(dve.tensor_tensor(gt[:, 4], gt[:, 9], by_tile(gs[:, 2], 8), ALU.mult))
                    dve.tensor_tensor(W9[:, b % 2, :, 0:8], gt[:, 8], gt[:, 4], ALU.add).then_inc(w9_ready, 1)
                elif kind == "F1" and piece[2] >= 2 and piece[3] == 0:
                    weigh(b, piece[2] - 2)
                    if piece[2] == FB + 1:
                        biases(b)
                elif kind == "F2":
                    weigh(b, NE - 1)
                    dve.wait_ge(down_free, (b + 1) * (NE + 1))
                    step(dve.scalar_tensor_tensor(out=X[:, b], in0=acc[:], scalar=tg[:, 2:3], in1=X[:, b],
                                                  op0=ALU.mult, op1=ALU.add))
                elif kind == "G0c":
                    p, wts = [poss[b][:, i] for i in range(5)], wtss[b]
                    dve.wait_ge(misc_ready, m + 1)
                    dve.tensor_tensor(p[0], MISC[:, 0:NT * HN].rearrange("p (t n) -> p t n", t=NT),
                                      cst[:, C_REF:C_REF + HN].unsqueeze(1).broadcast_to((128, NT, HN)),
                                      ALU.add).then_inc(misc_free, 1)
                    dve.wait_ge(misc_free, m + 1)
                    step(dve.tensor_tensor(p[1], p[0], by_tile(cst[:, C_LOC:C_LOC + NT], HN), ALU.add))
                    size, less, per, back = (lens[:, i, b:b + 1] for i in range(4))
                    dve.tensor_scalar(p[0], p[1], sgn[:, b:b + 1], None, ALU.mult)
                    step(dve.tensor_scalar(p[2], p[1], per, -0.5, ALU.mult, ALU.add))
                    step(dve.tensor_scalar(p[2], p[2], MAGIC, None, ALU.add))
                    step(dve.tensor_scalar(p[2], p[2], -MAGIC, less, ALU.add, ALU.mult))
                    step(dve.tensor_tensor(p[0], p[0], p[2], ALU.add))
                    step(dve.tensor_scalar(p[1], p[0], size, less, ALU.is_ge, ALU.mult))
                    step(dve.tensor_tensor(p[0], p[0], p[1], ALU.add))
                    step(dve.tensor_scalar(p[1], p[0], 0.0, size, ALU.is_lt, ALU.mult))
                    step(dve.tensor_tensor(p[0], p[0], p[1], ALU.add))
                    step(dve.tensor_scalar(p[2], p[0], back, -0.5, ALU.mult, ALU.add))
                    step(dve.tensor_scalar(p[3], p[2], -0.5, MAGIC, ALU.add, ALU.add))
                    step(dve.tensor_scalar(p[3], p[3], -MAGIC, None, ALU.add))
                    dve.tensor_scalar(p[1], p[3], 1.0, None, ALU.add).then_inc(pos_ready, 1)
                    step(dve.tensor_tensor(p[4], p[2], p[3], ALU.subtract))
                    dve.tensor_scalar(wts[:, :, :, 1], p[4], 0.5, None, ALU.mult)
                    step(dve.tensor_scalar(wts[:, :, :, 0], p[4], -0.5, 0.5, ALU.mult, ALU.add))
                elif kind == "G0e":
                    onehot(b, 0)
                elif kind == "G1":
                    h = piece[2]
                    if h + 1 < H:
                        onehot(b, h + 1)
                    if h == 0:
                        dve.wait_ge(misc_free, misc_at["G0b", b] + 1)
                    idx = b * H + h
                    dve.wait_ge(g_free, 2 * (idx + 1))
                    dve.tensor_tensor(prod[:], GS[:, h % 2].rearrange("p t (n d) -> p t n d", d=DK),
                                      Qps[b][:, :, h * DK:(h + 1) * DK].unsqueeze(2).broadcast_to((128, NT, 10, DK)),
                                      ALU.mult).then_inc(gk_used, 1)
                    dve.wait_ge(gk_used, idx + 1)
                    step(dve.tensor_reduce(dots[:, :, h, :], prod[:], AX.X, ALU.add))
                elif kind == "G2a":
                    wf = wtss[b].rearrange("p t n w -> p (t n w)")
                    sc, scf = scores_of(b)
                    df = dots[:].rearrange("p t h w -> p (t h w)")
                    step(dve.tensor_tensor(df, df, wf, ALU.mult))
                    step(dve.tensor_reduce(sc.rearrange("p t n -> p (t n)"), df.rearrange("p (n w) -> p n w", w=2),
                                           AX.X, ALU.add))
                    step(dve.tensor_reduce(sm[:, 0], scf, AX.X, ALU.max))
                    dve.tensor_tensor(scf, scf, taps(sm[:, 0]), ALU.subtract).then_inc(z_ready, 1)
                elif kind == "G2b":
                    dve.wait_ge(e_ready, b + 1)
                    (sc, scf), aw, wts = scores_of(b), aws[b], wtss[b]
                    step(dve.tensor_reduce(sm[:, 1], scf, AX.X, ALU.add))
                    step(dve.reciprocal(sm[:, 2], sm[:, 1]))
                    step(dve.tensor_tensor(scf, scf, taps(sm[:, 2]), ALU.mult))
                    step(dve.tensor_tensor(aw, wts, sc.unsqueeze(3).broadcast_to((128, NT, HN, 2)), ALU.mult))
                elif kind == "G2c":
                    t = piece[2]
                    gv = GV[:, :, t, :].rearrange("p h (m d) -> p h m d", d=DK)
                    step(dve.tensor_tensor(gv, gv, aws[b][:, t].rearrange("p (h n) w -> p h (n w)", h=H).unsqueeze(3)
                                           .broadcast_to((128, H, 10, DK)), ALU.mult))
                    last = dve.tensor_reduce(Qps[b][:, t].rearrange("p (h d) -> p h d", d=DK),
                                             GV[:, :, t, :].rearrange("p h (m d) -> p h d m", d=DK), AX.X, ALU.add)
                    if t == NT - 1:
                        last.then_inc(cx1_ready, 1)
                elif kind == "G3b":
                    add_misc(m, b, 1)
                elif kind == "G3d":
                    add_misc(m, b, 3)
                    dve.nop().then_inc(x_done, 1)


def order():
    pieces = []
    for text in ORDER.split():
        kind, *numbers = text.split(".")
        first, _, last = numbers.pop().partition("-")
        for n in range(int(first), int(last or first) + 1):
            pieces.append((kind, *map(int, numbers), n))
    return pieces


def kernel(**inputs):
    import numpy as np
    import concourse.bacc as bacc
    from concourse.bass_utils import run_bass_kernel_spmd

    a = {k: np.ascontiguousarray(v) for k, v in inputs.items()}
    row = np.arange(128)
    consts = np.zeros((128, C_N), np.float32)
    consts[:, C_ID:C_ID + 128] = np.eye(128)
    consts[:, C_K0] = row
    consts[:, C_KR] = R0 + row % 32
    consts[:, C_LOC:C_LOC + NT] = row[:, None] + 128 * np.arange(NT)
    consts[:, C_REF:C_REF + HN] = np.tile(np.arange(NK) + (-NK // 2), H)
    consts[:, C_TAIL] = row % 32 < KT
    consts[:, C_RANK:C_RANK + 8] = 8 - np.arange(8)
    mask = a["mask_BxSxS2_bf0"]
    b1 = np.concatenate([a["L0_ffn_be1"], a["L0_ffn_bs1"][None]])
    laid_out = {
        "x": a["x"],
        "ctxT": a["ctx_1024"].transpose(2, 0, 1),
        "mask": mask,
        "maskT": mask.transpose(0, 2, 1),
        "kmask": a["mask_BxS2_if0"],
        "gates": np.concatenate([a["g_xattn"], a["g_ffn"]]),
        "consts": consts,
        "wq": a["L0_xattn_Wq"], "wk": a["L0_xattn_Wk"], "wv": a["L0_xattn_Wv"], "wo": a["L0_xattn_Wo"],
        "bq_col": a["L0_xattn_bq"][:, None], "bk_col": a["L0_xattn_bk"][:, None],
        "rows": np.stack([a["L0_xattn_bv"], a["L1_xattn_bk"], a["L1_xattn_bv"], a["L0_xattn_bo"],
                          a["L1_xattn_bq"], a["L1_xattn_bo"]]),
        "wr1": a["L0_ffn_Wr1"], "br1_col": a["L0_ffn_br1"][:, None],
        "wr2": a["L0_ffn_Wr2"], "br2": a["L0_ffn_br2"][None],
        "w1": np.concatenate([a["L0_ffn_We1"], a["L0_ffn_Ws1"][None]]),
        "b1_cols": b1.reshape(NE, NC, 128).transpose(2, 0, 1),
        "w2": np.concatenate([a["L0_ffn_We2"], a["L0_ffn_Ws2"][None]]),
        "b2": np.concatenate([a["L0_ffn_be2"], a["L0_ffn_bs2"][None]]),
        "wkT": a["L1_xattn_Wk"].T, "wvT": a["L1_xattn_Wv"].T, "wqT": a["L1_xattn_Wq"].T,
        "woffT": a["L1_xattn_Woff"].T, "woT": a["L1_xattn_Wo"].T,
        "bq1_col": a["L1_xattn_bq"][:, None], "boff": a["L1_xattn_boff"][None],
        "w8": a["L1_ffn_W"], "b8": a["L1_ffn_b"][None], "logits": a["L1_ffn_logits"], "u": a["L1_ffn_u"],
    }
    nc = bacc.Bacc("TRN2", target_bir_lowering=False, num_devices=1, dynamic_dma_scratch_size=1024)
    arrays, args = {}, []
    for name, v in laid_out.items():
        v = np.ascontiguousarray(v)
        arrays[f"in_{name}"] = v
        args.append(nc.dram_tensor(f"in_{name}", v.shape, mybir.dt.from_np(v.dtype), kind="ExternalInput").ap())
    args.append(nc.dram_tensor("out_x", (B, S, D), F32, kind="ExternalOutput").ap())
    build(nc, *args)
    r = run_bass_kernel_spmd(nc, [arrays], core_ids=[0])
    return r.results[0]["out_x"]
```
